# Optimizing a Trainium2 kernel written in Bass

```python
import numpy as np
import jax
import jax.numpy as jnp

def _softmax(x, axis=-1):
    return jax.nn.softmax(x, axis=axis)

def _gelu(x):
    return jax.nn.gelu(x, approximate=True)

def _silu(x):
    return jax.nn.silu(x)

def _sigmoid(x):
    return jax.nn.sigmoid(x)

def _layernorm(x, axis=-1, eps=1e-05):
    m = jnp.mean(x, axis=axis, keepdims=True)
    v = jnp.var(x, axis=axis, keepdims=True)
    return (x - m) / jnp.sqrt(v + eps)

def _scatter_add(tgt, idx, src, axis=0):
    return tgt.at[idx].add(src)

def _segment_sum(src, seg, n):
    return jax.ops.segment_sum(src, seg, n)
kernel_name = 'mk_seq_preln_d1_jaxref_r4_bbcf32'

def setup_inputs(seed: int=0):
    np.random.seed(seed)
    _w = jnp.asarray

    def _L0_attn_setup():
        import jax, jax.numpy as jnp
        import numpy as np
        B, S, D_IN = (2, 512, 512)
        D_OUT, DL, H = (512, 128, 16)
        DH = D_OUT // H
        key = jax.random.key(seed)
        ks = jax.random.split(key, 20)
        g = lambda k, shp: jax.random.normal(k, shp, dtype=jnp.float32) * 0.02
        return {'x': jax.random.normal(ks[0], (B, S, D_IN), dtype=jnp.float32), 'wq_w': g(ks[1], (D_IN, D_OUT)), 'wq_b': g(ks[2], (D_OUT,)), 'wk_w': g(ks[3], (D_IN, D_OUT)), 'wk_b': g(ks[4], (D_OUT,)), 'wkl_w': g(ks[5], (D_OUT, DL)), 'wkl_b': g(ks[6], (DL,)), 'wv_w': g(ks[7], (D_IN, D_OUT)), 'wv_b': g(ks[8], (D_OUT,)), 'wvl_w': g(ks[9], (D_OUT, DL)), 'wvl_b': g(ks[10], (DL,)), 'upk_w': g(ks[11], (H, DL, DH)), 'upk_b': g(ks[12], (H, DH)), 'upv_w': g(ks[13], (H, DL, DH)), 'upv_b': g(ks[14], (H, DH)), 'wo_w': g(ks[15], (D_OUT, D_OUT)), 'wo_b': g(ks[16], (D_OUT,))}
    _L0_attn_in = _L0_attn_setup()

    def _L0_ffn_setup():
        import jax, jax.numpy as jnp
        import numpy as np
        NUM_EXPERTS = 8
        TOP_K = 2
        ROUTED_SCALE = 1.0
        D_MODEL = 512
        D_FFN = 352
        key = jax.random.key(seed)
        ks = jax.random.split(key, 8)
        s = 0.02
        return {'hidden_states': jax.random.normal(ks[0], (2, 256, D_MODEL), jnp.float32), 'gate_w': jax.random.normal(ks[1], (NUM_EXPERTS, D_MODEL), jnp.float32) * s, 'w_gate': jax.random.normal(ks[2], (NUM_EXPERTS, D_MODEL, D_FFN), jnp.float32) * s, 'w_up': jax.random.normal(ks[3], (NUM_EXPERTS, D_MODEL, D_FFN), jnp.float32) * s, 'w_down': jax.random.normal(ks[4], (NUM_EXPERTS, D_FFN, D_MODEL), jnp.float32) * s, 'sw_gate': jax.random.normal(ks[5], (D_MODEL, D_FFN), jnp.float32) * s, 'sw_up': jax.random.normal(ks[6], (D_MODEL, D_FFN), jnp.float32) * s, 'sw_down': jax.random.normal(ks[7], (D_FFN, D_MODEL), jnp.float32) * s}
    _L0_ffn_in = _L0_ffn_setup()
    _d = {'L0_attn_x': _L0_attn_in['x'], 'L0_attn_wq_w': _L0_attn_in['wq_w'], 'L0_attn_wq_b': _L0_attn_in['wq_b'], 'L0_attn_wk_w': _L0_attn_in['wk_w'], 'L0_attn_wk_b': _L0_attn_in['wk_b'], 'L0_attn_wkl_w': _L0_attn_in['wkl_w'], 'L0_attn_wkl_b': _L0_attn_in['wkl_b'], 'L0_attn_wv_w': _L0_attn_in['wv_w'], 'L0_attn_wv_b': _L0_attn_in['wv_b'], 'L0_attn_wvl_w': _L0_attn_in['wvl_w'], 'L0_attn_wvl_b': _L0_attn_in['wvl_b'], 'L0_attn_upk_w': _L0_attn_in['upk_w'], 'L0_attn_upk_b': _L0_attn_in['upk_b'], 'L0_attn_upv_w': _L0_attn_in['upv_w'], 'L0_attn_upv_b': _L0_attn_in['upv_b'], 'L0_attn_wo_w': _L0_attn_in['wo_w'], 'L0_attn_wo_b': _L0_attn_in['wo_b'], 'L0_ffn_gate_w': _L0_ffn_in['gate_w'], 'L0_ffn_w_gate': _L0_ffn_in['w_gate'], 'L0_ffn_w_up': _L0_ffn_in['w_up'], 'L0_ffn_w_down': _L0_ffn_in['w_down'], 'L0_ffn_sw_gate': _L0_ffn_in['sw_gate'], 'L0_ffn_sw_up': _L0_ffn_in['sw_up'], 'L0_ffn_sw_down': _L0_ffn_in['sw_down']}
    _x0 = _d['L0_attn_x']
    _d['L0_attn_x'] = jax.random.normal(jax.random.fold_in(jax.random.key(seed), 1), (2, 2048, 512), dtype=_x0.dtype)
    del _x0
    return _d

def reference(L0_attn_x, L0_attn_wq_w, L0_attn_wq_b, L0_attn_wk_w, L0_attn_wk_b, L0_attn_wkl_w, L0_attn_wkl_b, L0_attn_wv_w, L0_attn_wv_b, L0_attn_wvl_w, L0_attn_wvl_b, L0_attn_upk_w, L0_attn_upk_b, L0_attn_upv_w, L0_attn_upv_b, L0_attn_wo_w, L0_attn_wo_b, L0_ffn_gate_w, L0_ffn_w_gate, L0_ffn_w_up, L0_ffn_w_down, L0_ffn_sw_gate, L0_ffn_sw_up, L0_ffn_sw_down):

    def _L0_attn_ref(x, wq_w, wq_b, wk_w, wk_b, wkl_w, wkl_b, wv_w, wv_b, wvl_w, wvl_b, upk_w, upk_b, upv_w, upv_b, wo_w, wo_b):
        import jax, jax.numpy as jnp
        import numpy as np
        B, S, D_IN = (2, 512, 512)
        D_OUT, DL, H = (512, 128, 16)
        DH = D_OUT // H
        b, s, _ = x.shape
        k_lat = (x @ wk_w + wk_b) @ wkl_w + wkl_b
        v_lat = (x @ wv_w + wv_b) @ wvl_w + wvl_b
        q = (x @ wq_w + wq_b).reshape(b, s, H, DH).transpose(0, 2, 1, 3)
        k = jnp.einsum('bsl,hld->bhsd', k_lat, upk_w) + upk_b[None, :, None, :]
        v = jnp.einsum('bsl,hld->bhsd', v_lat, upv_w) + upv_b[None, :, None, :]
        scores = jnp.einsum('bhqd,bhkd->bhqk', q, k) / jnp.sqrt(jnp.float32(DH))
        causal = jnp.tril(jnp.ones((s, s), dtype=bool))
        scores = jnp.where(causal[None, None], scores, -jnp.inf)
        attn = jax.nn.softmax(scores, axis=-1)
        out = jnp.einsum('bhqk,bhkd->bhqd', attn, v)
        out = out.transpose(0, 2, 1, 3).reshape(b, s, D_OUT)
        return out @ wo_w + wo_b

    def _L0_ffn_ref(hidden_states, gate_w, w_gate, w_up, w_down, sw_gate, sw_up, sw_down):
        import jax, jax.numpy as jnp
        import numpy as np
        NUM_EXPERTS = 8
        TOP_K = 2
        ROUTED_SCALE = 1.0
        D_MODEL = 512
        D_FFN = 352
        B, S, D = hidden_states.shape
        x = hidden_states.reshape(-1, D)
        T = x.shape[0]
        logits = jnp.einsum('td,ed->te', x.astype(jnp.float32), gate_w)
        probs = jax.nn.softmax(logits, axis=-1)
        topk_w, topk_ids = jax.lax.top_k(probs, TOP_K)
        topk_w = topk_w / jnp.sum(topk_w, axis=-1, keepdims=True)
        gates = jnp.zeros((T, NUM_EXPERTS), jnp.float32).at[jnp.arange(T)[:, None], topk_ids].add(topk_w)
        gates = gates.astype(x.dtype)
        g = jnp.einsum('td,edf->etf', x, w_gate)
        u = jnp.einsum('td,edf->etf', x, w_up)
        h = jax.nn.silu(g) * u
        down = jnp.einsum('etf,efd->etd', h, w_down)
        routed = jnp.einsum('te,etd->td', gates, down)
        routed = routed * ROUTED_SCALE
        shared = jax.nn.silu(x @ sw_gate) * (x @ sw_up) @ sw_down
        out = routed + shared
        return out.reshape(B, S, D)
    x = L0_attn_x
    x = x + _L0_attn_ref(_layernorm(x, axis=-1), L0_attn_wq_w, L0_attn_wq_b, L0_attn_wk_w, L0_attn_wk_b, L0_attn_wkl_w, L0_attn_wkl_b, L0_attn_wv_w, L0_attn_wv_b, L0_attn_wvl_w, L0_attn_wvl_b, L0_attn_upk_w, L0_attn_upk_b, L0_attn_upv_w, L0_attn_upv_b, L0_attn_wo_w, L0_attn_wo_b)
    x = x + _L0_ffn_ref(_layernorm(x, axis=-1), L0_ffn_gate_w, L0_ffn_w_gate, L0_ffn_w_up, L0_ffn_w_down, L0_ffn_sw_gate, L0_ffn_sw_up, L0_ffn_sw_down)
    return x

_drawn_inputs = setup_inputs


def setup_inputs(seed=0):
    import zlib

    import numpy as np

    out = dict(_drawn_inputs(seed))
    spreads = {}
    factors = {'L0_attn_wq_w': 8.0,
     'L0_attn_wq_b': 8.0,
     'L0_attn_wk_w': 8.0,
     'L0_attn_wk_b': 200.0,
     'L0_attn_wkl_w': 8.0,
     'L0_attn_wkl_b': 200.0,
     'L0_attn_wv_w': 8.0,
     'L0_attn_wv_b': 8.0,
     'L0_attn_wvl_w': 8.0,
     'L0_attn_wvl_b': 30.317,
     'L0_attn_upk_w': 8.0,
     'L0_attn_upk_b': 200.0,
     'L0_attn_upv_w': 8.0,
     'L0_attn_upv_b': 48.72,
     'L0_attn_wo_w': 5.837,
     'L0_attn_wo_b': 81.669,
     'L0_ffn_gate_w': 8.0,
     'L0_ffn_w_gate': 8.0,
     'L0_ffn_w_up': 8.0,
     'L0_ffn_w_down': 8.0,
     'L0_ffn_sw_gate': 8.0,
     'L0_ffn_sw_up': 8.0,
     'L0_ffn_sw_down': 8.0}
    for name, (base, spread) in spreads.items():
        noise = np.random.default_rng([zlib.crc32(name.encode()), seed]).standard_normal(out[name].shape)
        drawn = base * np.exp(spread * noise) if base else spread * noise
        out[name] = jnp.asarray(drawn.astype(out[name].dtype))
    for name, factor in factors.items():
        out[name] = (out[name] * factor).astype(out[name].dtype)
    return out
```

```python
from contextlib import ExitStack

import concourse.bass as bass
from concourse import mybir

F32 = mybir.dt.float32
F32R = mybir.dt.float32r
I32 = mybir.dt.int32
U32 = mybir.dt.uint32
ALU = mybir.AluOpType
ACT = mybir.ActivationFunctionType
AX = mybir.AxisListType

P = 128
BATCH, SEQ, D = 2, 2048, 512
T = BATCH * SEQ
H, DH, DL = 16, 32, 128
KD = D // P
CH = 512
NCH = T // CH
CPB = SEQ // CH
TPC = CH // P
EPS = 1e-5


class Alloc:

    def __init__(self, nc, ctx):
        self.nc, self.ctx = nc, ctx

    def sb(self, name, shape, dt=F32):
        return self.ctx.enter_context(self.nc.sbuf_tensor(name, shape, dt))

    def bank(self, name, cols=512, dt=F32):
        return self.ctx.enter_context(self.nc.psum_tensor(name, [P, cols], dt))

    def sem(self, name):
        return self.ctx.enter_context(self.nc.semaphore(name))


def f32(ap):
    return ap.bitcast(F32)


def wait_apart(eng, sem, value, passed):
    eng.wait_ge(sem, value)
    eng.sem_inc(passed, 1)


def mm3(nc, out, wh, wl, xh, xl, first, last):
    nc.tensor.matmul(out, wh, xh, start=first, stop=False)
    nc.tensor.matmul(out, wl, xh, start=False, stop=False)
    return nc.tensor.matmul(out, wh, xl, start=False, stop=last)


def broadcast_rows(ap1d, n):
    return bass.AP(ap1d.tensor, ap1d.offset, [[0, P], [1, n]])


def make_identity(g, ident, s_made, count):
    g.memset(ident[:], 0.0).then_inc(s_made, 1)
    g.wait_ge(s_made, count + 1)
    g.affine_select(out=ident[:], in_=ident[:], compare_op=ALU.not_equal, fill=1.0, base=0,
                    pattern=[[-1, P]], channel_multiplier=1).then_inc(s_made, 1)


def phase_project(nc, x, w, scratch):
    with ExitStack() as ctx:
        al = Alloc(nc, ctx)
        ident = al.sb("a_ident", [P, P])
        wstage = al.sb("a_wstage", [P, 3, KD, D])
        lat = al.sb("a_lat", [P, 2, KD, DL])
        up = al.sb("a_up", [P, 2, D])
        wT = al.sb("a_wT", [P, 2, KD, D])
        bcol = al.sb("a_bcol", [P, 5, KD])
        vb = al.sb("a_vb", [P, D])
        wqh, wql = al.sb("a_wqh", [P, KD, D], F32R), al.sb("a_wql", [P, KD, D], F32R)
        fh, fl = al.sb("a_fh", [P, 2, KD, DL], F32R), al.sb("a_fl", [P, 2, KD, DL], F32R)
        uh, ul = al.sb("a_uh", [P, 2, D], F32R), al.sb("a_ul", [P, 2, D], F32R)
        xin = al.sb("a_xin", [P, TPC, D])
        xn = al.sb("a_xn", [P, TPC, D])
        xh, xl = al.sb("a_xh", [P, KD, CH], F32R), al.sb("a_xl", [P, KD, CH], F32R)
        st = al.sb("a_stats", [P, TPC, 6])
        mv = al.sb("a_mv", [P, TPC, 2])
        vare = al.sb("a_vare", [P, TPC])
        mhalf = al.sb("a_mhalf", [P, TPC])
        rstd = al.sb("a_rstd", [P, TPC])
        lh, ll = al.sb("a_lh", [P, 2, CH], F32R), al.sb("a_ll", [P, 2, CH], F32R)
        qh, ql = al.sb("a_qh", [P, KD, CH], F32R), al.sb("a_ql", [P, KD, CH], F32R)
        kh, kl = al.sb("a_kh", [P, KD, CH], F32R), al.sb("a_kl", [P, KD, CH], F32R)
        vo = al.sb("a_vo", [P, TPC, D])
        tb = [al.bank(f"a_tb{n}") for n in range(KD)]
        ob = [al.bank(f"a_ob{n}") for n in range(4)]

        s_w = al.sem("a_weights_in")
        s_vpass, s_gpass = al.sem("a_vector_passed"), al.sem("a_pool_passed")
        s_id = al.sem("a_ident_made")
        s_wt = al.sem("a_weight_transposed")
        s_wc = al.sem("a_weight_copied")
        s_fold = al.sem("a_folded")
        s_split = al.sem("a_weights_split")
        s_x = al.sem("a_x_in")
        s_xfree = al.sem("a_x_read")
        s_stat = al.sem("a_stats_made")
        s_var = al.sem("a_var_made")
        s_vare = al.sem("a_vare_made")
        s_rstd = al.sem("a_rstd_made")
        s_xn = al.sem("a_xn_made")
        s_t = al.sem("a_x_transposed")
        s_xh = al.sem("a_xh_made")
        s_xl = al.sem("a_xl_made")
        s_mm = al.sem("a_product_made")
        s_hi = al.sem("a_hi_made")
        s_out = al.sem("a_bank_read")
        s_st = al.sem("a_stored")
        s_free = al.sem("a_stage_free")

        NP = 2 + KD + KD + TPC
        Q0, K0, V0 = 2, 2 + KD, 2 + 2 * KD

        with nc.Block() as block:
            @block.sync
            def _(sp):
                with nc.allow_non_contiguous_dma(reason="bias columns"):
                    for n, name in enumerate(("wq_w", "wk_w", "wv_w")):
                        sp.dma_start(wstage[:, n], w[name].rearrange("(k p) n -> p k n", p=P)).then_inc(s_w, 16)
                    for n, name in enumerate(("wkl_w", "wvl_w")):
                        sp.dma_start(lat[:, n], w[name].rearrange("(k p) n -> p k n", p=P)).then_inc(s_w, 16)
                    for n, name in enumerate(("upk_w", "upv_w")):
                        sp.dma_start(up[:, n].rearrange("p (h d) -> p h d", h=H),
                                     w[name].rearrange("h l d -> l h d")).then_inc(s_w, 16)
                    for n, name in enumerate(("wq_b", "wk_b", "wv_b")):
                        sp.dma_start(bcol[:, n], w[name].rearrange("(k p) -> p k", p=P)).then_inc(s_w, 16)
                    sp.dma_start(bcol[:, 3], w["upk_b"].rearrange("h d -> (h d)").rearrange("(k p) -> p k", p=P)).then_inc(s_w, 16)
                    for n, name in enumerate(("wkl_b", "wvl_b")):
                        sp.dma_start(bcol[:, 4, n:n + 1], w[name].rearrange("(p a) -> p a", a=1)).then_inc(s_w, 16)
                    sp.dma_start(vb[:], broadcast_rows(w["upv_b"], D)).then_inc(s_w, 16)

                def store(c):
                    rows = "(k p) t -> p k t"
                    sp.wait_ge(s_out, c * NP + K0)
                    sp.dma_start(scratch["qh"][c].rearrange(rows, p=P), f32(qh[:])).then_inc(s_st, 16)
                    sp.dma_start(scratch["ql"][c].rearrange(rows, p=P), f32(ql[:])).then_inc(s_st, 16)
                    sp.wait_ge(s_out, c * NP + V0)
                    sp.dma_start(scratch["kh"][c].rearrange(rows, p=P), f32(kh[:])).then_inc(s_st, 16)
                    sp.dma_start(scratch["kl"][c].rearrange(rows, p=P), f32(kl[:])).then_inc(s_st, 16)
                    sp.wait_ge(s_out, c * NP + NP)
                    sp.dma_start(scratch["v"][c].rearrange("(t p) n -> p t n", p=P), vo[:]).then_inc(s_st, 16)
                    sp.wait_ge(s_st, c * 80 + 80)
                    sp.nop().then_inc(s_free, 1)

                with sp.Fori(0, NCH) as c:
                    store(c)

            @block.gpsimd
            def _(g):
                make_identity(g, ident, s_id, 0)
                g.memset(mhalf[:], -0.5).then_inc(s_vare, 1)

                def chunk(c, first=False):
                    if not first:
                        g.wait_ge(s_xfree, c)
                    g.dma_start(xin[:], x[bass.ds(c * CH, CH), :].rearrange("(t p) n -> p t n", p=P)).then_inc(s_x, 16)
                    wait_apart(g, s_var, c * TPC + TPC, s_gpass)
                    g.tensor_scalar(vare[:], mv[:, :, 1], EPS, None, ALU.add).then_inc(s_vare, 1)
                    g.wait_ge(s_vare, c + 2)
                    g.tensor_tensor(rstd[:], vare[:], mhalf[:], ALU.pow).then_inc(s_rstd, 1)

                chunk(0, first=True)
                with g.Fori(1, NCH) as c:
                    chunk(c)

            @block.scalar
            def _(act):
                act.wait_ge(s_w, 16 * 14)
                act.activation(wqh[:], wstage[:, 0], ACT.Copy).then_inc(s_split, 1)
                act.activation(uh[:], up[:], ACT.Copy).then_inc(s_split, 1)
                for n in range(2):
                    for k in range(KD):
                        act.wait_ge(s_wt, n * KD + k + 1)
                        act.activation(wT[:, n, k], tb[k][:], ACT.Copy).then_inc(s_wc, 1)
                for n in range(2):
                    act.wait_ge(s_fold, n + 1)
                    act.activation(fh[:, n], ob[n][:].rearrange("p (k l) -> p k l", k=KD), ACT.Copy).then_inc(s_split, 1)

                def chunk(c, first=False):
                    if not first:
                        act.wait_ge(s_mm, (c - 1) * NP + K0)
                    for k in range(KD):
                        act.wait_ge(s_t, c * KD + k + 1)
                        act.activation(xh[:, k], tb[k][:], ACT.Copy).then_inc(s_xh, 1)
                    if not first:
                        act.wait_ge(s_free, c)
                    for j in range(V0):
                        act.wait_ge(s_mm, c * NP + j + 1)
                        dst, bias = (
                            (lh[:, j], bcol[:, 4, 2 + j:3 + j]) if j < Q0 else
                            (qh[:, j - Q0], bcol[:, 0, j - Q0:j - Q0 + 1]) if j < K0 else
                            (kh[:, j - K0], bcol[:, 3, j - K0:j - K0 + 1]))
                        act.activation(dst, ob[j % 4][:], ACT.Identity, bias=bias).then_inc(s_hi, 1)

                act.wait_ge(s_split, 9)
                chunk(0, first=True)
                with act.Fori(1, NCH) as c:
                    chunk(c)

            @block.vector
            def _(v):
                v.wait_ge(s_split, 2)
                v.tensor_tensor(wql[:], wstage[:, 0], f32(wqh[:]), ALU.subtract).then_inc(s_split, 1)
                v.tensor_tensor(ul[:], up[:], f32(uh[:]), ALU.subtract).then_inc(s_split, 1)

                def norm(c, first=False):
                    v.wait_ge(s_x, c * 16 + 16)
                    for t in range(TPC):
                        v.bn_stats(st[:, t], xin[:, t]).then_inc(s_stat, 1)
                    for t in range(TPC):
                        wait_apart(v, s_stat, c * TPC + t + 1, s_vpass)
                        v.bn_aggr(mv[:, t], st[:, t]).then_inc(s_var, 1)
                    v.wait_ge(s_rstd, c + 1)
                    if not first:
                        v.wait_ge(s_t, c * KD)
                    for t in range(TPC):
                        ins = v.tensor_scalar(xn[:, t], xin[:, t], mv[:, t, 0:1], rstd[:, t:t + 1], ALU.subtract, ALU.mult)
                        ins.then_inc(s_xn, 1)
                    v.wait_ge(s_xn, c * TPC + TPC)
                    v.nop().then_inc(s_xfree, 1)

                def low_x(c):
                    for k in range(KD):
                        v.wait_ge(s_xh, c * KD + k + 1)
                        v.tensor_tensor(xl[:, k], tb[k][:], f32(xh[:, k]), ALU.subtract).then_inc(s_xl, 1)

                def low(c, js):
                    for j in js:
                        if j < V0:
                            v.wait_ge(s_hi, c * V0 + j + 1)
                            dst, hi, bias = (
                                (ll[:, j], lh[:, j], bcol[:, 4, 2 + j:3 + j]) if j < Q0 else
                                (ql[:, j - Q0], qh[:, j - Q0], bcol[:, 0, j - Q0:j - Q0 + 1]) if j < K0 else
                                (kl[:, j - K0], kh[:, j - K0], bcol[:, 3, j - K0:j - K0 + 1]))
                            ins = v.scalar_tensor_tensor(out=dst, in0=ob[j % 4][:], scalar=bias, in1=f32(hi), op0=ALU.add, op1=ALU.subtract)
                        else:
                            v.wait_ge(s_mm, c * NP + j + 1)
                            ins = v.tensor_tensor(vo[:, j - V0], ob[j % 4][:], vb[:], ALU.add)
                        ins.then_inc(s_out, 1)

                for n in range(2):
                    v.wait_ge(s_split, 6)
                    v.tensor_tensor(fl[:, n], ob[n][:].rearrange("p (k l) -> p k l", k=KD), f32(fh[:, n]), ALU.subtract).then_inc(s_split, 1)
                v.wait_ge(s_fold, 3)
                v.tensor_tensor(bcol[:, 4, 2:4], ob[2][:, 0:2], bcol[:, 4, 0:2], ALU.add).then_inc(s_split, 1)
                v.wait_ge(s_split, 9)
                norm(0, first=True)
                with v.Fori(0, NCH - 1) as c:
                    low_x(c)
                    low(c, range(0, K0))
                    norm(c + 1)
                    low(c, range(K0, NP))
                low_x(NCH - 1)
                low(NCH - 1, range(NP))

            @block.tensor
            def _(pe):
                pe.wait_ge(s_id, 2)
                pe.wait_ge(s_w, 16 * 14)
                for n in range(2):
                    for k in range(KD):
                        if n:
                            pe.wait_ge(s_wc, k + 1)
                        for m in range(KD):
                            ins = pe.transpose(tb[k][:, m * P:(m + 1) * P], wstage[:, 1 + n, m, k * P:(k + 1) * P], ident[:])
                        ins.then_inc(s_wt, 1)
                pe.wait_ge(s_wc, 2 * KD)
                for n in range(2):
                    for m in range(KD):
                        for k in range(KD):
                            ins = pe.matmul(ob[n][:, m * DL:(m + 1) * DL], wT[:, n, k, m * P:(m + 1) * P], lat[:, n, k],
                                            start=(k == 0), stop=(k == KD - 1))
                    ins.then_inc(s_fold, 1)
                for n in range(2):
                    for k in range(KD):
                        ins = pe.matmul(ob[2][:, n:n + 1], lat[:, n, k], bcol[:, 1 + n, k:k + 1],
                                        start=(k == 0), stop=(k == KD - 1))
                ins.then_inc(s_fold, 1)

                def transposes(c, first=False):
                    pe.wait_ge(s_xn, c * TPC + TPC)
                    for k in range(KD):
                        if not first:
                            pe.wait_ge(s_xl, (c - 1) * KD + k + 1)
                        for t in range(TPC):
                            ins = pe.transpose(tb[k][:, t * P:(t + 1) * P], xn[:, t, k * P:(k + 1) * P], ident[:])
                        ins.then_inc(s_t, 1)

                def products(c, js, first=False):
                    for j in js:
                        if not (first and j < 4):
                            pe.wait_ge(s_out, c * NP + j - 3)
                        bank = ob[j % 4][:]
                        if j < K0:
                            if j == 0:
                                pe.wait_ge(s_xl, c * KD + KD)
                            for k in range(KD):
                                wh, wl = ((fh[:, j, k], fl[:, j, k]) if j < Q0 else
                                          (wqh[:, k, (j - Q0) * P:(j - Q0 + 1) * P], wql[:, k, (j - Q0) * P:(j - Q0 + 1) * P]))
                                ins = mm3(nc, bank, wh, wl, xh[:, k], xl[:, k], k == 0, k == KD - 1)
                        elif j < V0:
                            m = j - K0
                            ins = mm3(nc, bank, uh[:, 0, m * P:(m + 1) * P], ul[:, 0, m * P:(m + 1) * P], lh[:, 0], ll[:, 0], True, True)
                        else:
                            t = j - V0
                            ins = mm3(nc, bank, lh[:, 1, t * P:(t + 1) * P], ll[:, 1, t * P:(t + 1) * P], uh[:, 1], ul[:, 1], True, True)
                        ins.then_inc(s_mm, 1)

                pe.wait_ge(s_split, 9)
                transposes(0, first=True)
                products(0, range(K0), first=True)
                transposes(1)
                products(0, range(K0, NP))
                with pe.Fori(1, NCH - 1) as c:
                    products(c, range(K0))
                    transposes(c + 1)
                    products(c, range(K0, NP))
                products(NCH - 1, range(NP))


GPB = H // 4
NG = BATCH * GPB
PAIRS = 2
NQ = SEQ // CH
SCALE = 1.0 / DH ** 0.5


def attention_plan():
    units = [(p, q) for p in range(PAIRS) for q in range(NQ)]
    steps, first_step = [], []
    for u, (p, q) in enumerate(units):
        first_step.append(len(steps))
        steps += [(u, p, q, kt) for kt in range(TPC * (q + 1))]
    stream, pending, end = [], None, []
    for u, (p, q) in enumerate(units):
        items = [("max", u, t, h, c) for t in range(TPC) for h in range(2) for c in range(q + 1)]
        lag = min(4, len(items))
        stream += items[:lag]
        if pending is not None:
            stream.append(("turn", pending))
            end.append(len(stream))
        stream += items[lag:]
        pending = u
    stream.append(("turn", pending))
    end.append(len(stream))
    ahead = 2
    upto, pos = [], end[0] + 4
    start = pos
    for n in range(len(steps)):
        rate = 0
        for u in range(len(units)):
            left = first_step[u] - ahead - n
            if end[u] > pos and first_step[u] > n:
                rate = max(rate, -(-(end[u] - pos) // max(left, 1)))
        pos = min(pos + rate, len(stream))
        upto.append(pos)
    return units, steps, first_step, stream, start, upto, end


def phase_attention(nc, scratch):
    units, steps, first_step, stream, start, upto, end = attention_plan()
    NS, NI, NU = len(steps), len(stream), len(units)
    NPB, NST, NMX, NOB = 4, 2, 2, 2
    assert NS % NPB == 0 and NI % NMX == 0 and NU % NOB == 0 and NS % NST == 0
    NRED = sum(i[0] == "max" for i in stream)
    KR = 3 * DH
    MROW = KR
    MCOL = (MROW, 64)

    with ExitStack() as ctx:
        al = Alloc(nc, ctx)
        ident = al.sb("b_ident", [P, P])
        ones = al.sb("b_ones", [P, DH])
        qb = [al.sb(f"b_q{p}", [MROW + 1, 2, SEQ], F32R) for p in range(PAIRS)]
        kb = [al.sb(f"b_k{p}", [MROW + 1, 2, SEQ], F32R) for p in range(PAIRS)]
        vbuf = [al.sb(f"b_v{p}", [P, SEQ // P, 2 * DH]) for p in range(PAIRS)]
        pt = [al.sb(f"b_pt{n}", [P, 2, CH]) for n in range(NPB)]
        mpart = [al.sb(f"b_mpart{n}", [P, 2, TPC, NQ]) for n in range(2)]
        mt = [al.sb(f"b_mt{n}", [P, TPC, MROW + 1]) for n in range(2)]
        ost = [al.sb(f"b_ost{n}", [P, CH]) for n in range(NOB)]
        causal = al.sb("b_causal", [P, P], mybir.dt.bfloat16)
        identb = al.sb("b_identb", [P, P], mybir.dt.bfloat16)
        stb = [al.bank(f"b_st{n}", 2 * CH) for n in range(NST)]
        mxb = [al.bank(f"b_mx{n}") for n in range(NMX)]
        ob = [al.bank(f"b_ob{n}") for n in range(NOB)]

        s_cst = al.sem("b_constants_made")
        s_rows = al.sem("b_rows_made")
        s_ld = [al.sem(f"b_pair{p}_in") for p in range(PAIRS)]
        s_item = al.sem("b_item_made")
        s_iread = al.sem("b_item_read")
        s_mcol = al.sem("b_max_columns")
        s_red = al.sem("b_partial_max")
        s_st = al.sem("b_scores_made")
        s_exp = al.sem("b_exp_made")
        s_pv = al.sem("b_step_used")
        s_oev = al.sem("b_out_read")
        s_ost = [al.sem(f"b_out_stored{n}") for n in range(NOB)]

        with nc.Block() as block:
            @block.gpsimd
            def _(g):
                make_identity(g, ident, s_cst, 0)
                g.memset(causal[:], 0.0).then_inc(s_cst, 1)
                g.wait_ge(s_cst, 3)
                g.affine_select(out=causal[:], in_=causal[:], compare_op=ALU.is_ge, fill=-1e30, base=0,
                                pattern=[[-1, P]], channel_multiplier=1).then_inc(s_cst, 1)
                g.memset(identb[:], 0.0).then_inc(s_cst, 1)
                g.wait_ge(s_cst, 5)
                g.affine_select(out=identb[:], in_=identb[:], compare_op=ALU.not_equal, fill=1.0, base=0,
                                pattern=[[-1, P]], channel_multiplier=1).then_inc(s_cst, 1)
                g.memset(ones[:], 1.0).then_inc(s_cst, 1)

            NCST = 7
            LD = 13 * 16
            STO = NU // NOB * 48

            @block.sync
            def _(sp):
                def load(it, p, first=False):
                    if not first:
                        sp.wait_ge(s_pv, (it - 1) * NS + (p + 1) * NS // PAIRS)
                    b, g = (it // GPB, it % GPB) if not first else (0, 0)
                    if not first:
                        b, g = sp.snap(b), sp.snap(g)
                    for h in range(2):
                        row = g * P + p * 2 * DH + h * DH
                        for buf, parts in ((qb[p], ("qh", "ql", "qh")), (kb[p], ("kh", "kh", "kl"))):
                            for n, name in enumerate(parts):
                                dst = f32(buf[n * DH:(n + 1) * DH, h]).rearrange("d (c t) -> d c t", c=CPB)
                                src = scratch[name][bass.ds(b * CPB, CPB), bass.ds(row, DH), :].rearrange("c d t -> d c t")
                                sp.dma_start(dst, src).then_inc(s_ld[p], 16)
                    src = scratch["v"][bass.ds(b * CPB, CPB), :, bass.ds(g * P + p * 2 * DH, 2 * DH)]
                    sp.dma_start(vbuf[p][:], src.rearrange("c (t k) d -> k (c t) d", k=P)).then_inc(s_ld[p], 16)

                for p in range(PAIRS):
                    load(0, p, first=True)
                with sp.Fori(1, NG) as it:
                    for p in range(PAIRS):
                        load(it, p)
                for sem in s_ost:
                    sp.wait_ge(sem, NG * STO)


            @block.vector
            def _(v):
                def item(it, i, what):
                    bank = mxb[i % NMX]
                    v.wait_ge(s_item, it * NI + i + 1)
                    if what[0] == "max":
                        _, u, t, h, c = what
                        n = (TPC * units[u][1] + t + 1) * P
                        w = min(CH, n - c * CH)
                        w = 2 * P if w == P and n > P else w
                        v.tensor_reduce(mpart[u % 2][:, h, t, c:c + 1], bank[:, 0:w], AX.X, ALU.max).then_inc(s_iread, 1)
                        if (t, h, c) == (TPC - 1, 1, units[u][1]):
                            done = sum(x[0] == "max" for x in stream[:i + 1]) + sum(x[0] == "turn" for x in stream[:i + 1])
                            v.wait_ge(s_iread, it * NI + done)
                            for hh in range(2):
                                v.tensor_reduce(mt[u % 2][:, :, MCOL[hh]], mpart[u % 2][:, hh, :, 0:units[u][1] + 1],
                                                AX.X, ALU.max, negate=True).then_inc(s_mcol, 1)
                    else:
                        u = what[1]
                        p, q = units[u]
                        for h in range(2):
                            ins = v.tensor_copy(qb[p][MROW:MROW + 1, h, q * CH:(q + 1) * CH], bank[MCOL[h]:MCOL[h] + 1, :])
                        ins.then_inc(s_iread, 1)

                for p in range(PAIRS):
                    v.memset(f32(kb[p][MROW:MROW + 1]), 1.0).then_inc(s_rows, 1)
                for n in range(2):
                    v.memset(mt[n][:], 0.0).then_inc(s_rows, 1)
                v.wait_ge(s_rows, 4)
                with v.Fori(0, NG) as it:
                    for i, what in enumerate(stream):
                        item(it, i, what)

            @block.scalar
            def _(act):
                def exps(it, n):
                    u, p, q, kt = steps[n]
                    lo = max(kt - TPC * q, 0) * P
                    act.wait_ge(s_st, it * NS + n + 1)
                    if n >= NPB:
                        act.wait_ge(s_pv, it * NS + n - NPB + 1)
                    act.activation(pt[n % NPB][:, :, lo:], stb[n % NST][:].rearrange("k (h q) -> k h q", h=2)[:, :, lo:],
                                   ACT.Exp, scale=SCALE).then_inc(s_exp, 1)

                def evacuate(it, u):
                    last = (first_step + [NS])[u + 1]
                    act.wait_ge(s_pv, it * NS + last)
                    if u >= NOB:
                        act.wait_ge(s_ost[u % NOB], it * STO + u // NOB * 48)
                    act.activation(ost[u % NOB][:], ob[u % NOB][:], ACT.Copy).then_inc(s_oev, 1)

                def store(it, b, g, u):
                    p, q = units[u]
                    act.wait_ge(s_oev, it * NU + u + 1)
                    st, chunk = ost[u % NOB], b * CPB + q
                    act.dma_start(scratch["oT"][bass.ds(chunk, 1), bass.ds(g * P + p * 2 * DH, 2 * DH), :].rearrange("c d t -> (c d) t"),
                                  st[0:2 * DH, :]).then_inc(s_ost[u % NOB], 16)
                    for h in range(2):
                        act.dma_start(scratch["sums"][bass.ds(chunk, 1), bass.ds(g * 4 + p * 2 + h, 1), :].rearrange("c d t -> (c d) t"),
                                      st[2 * DH + h * DH:2 * DH + h * DH + 1, :]).then_inc(s_ost[u % NOB], 16)

                with act.Fori(0, NG) as it:
                    b, g = act.snap(it // GPB), act.snap(it % GPB)
                    for n, (u, p, q, kt) in enumerate(steps):
                        exps(it, n)
                        if u and kt == 1:
                            evacuate(it, u - 1)
                        if u and kt == 2:
                            store(it, b, g, u - 1)
                    evacuate(it, NU - 1)
                    store(it, b, g, NU - 1)
                    for sem in s_ost:
                        act.wait_ge(sem, (it + 1) * STO)

            @block.tensor
            def _(pe):
                def item(it, i):
                    what = stream[i]
                    bank = mxb[i % NMX]
                    if i >= NMX:
                        pe.wait_ge(s_iread, it * NI + i - NMX + 1)
                    if what[0] == "max":
                        _, u, t, h, c = what
                        p, q = units[u]
                        tile = TPC * q + t
                        n = (tile + 1) * P
                        w = min(CH, n - c * CH)
                        lo = c * CH
                        if w == P and n > P:
                            lo, w = lo - P, 2 * P
                        if (t, h, c) == (0, 0, 0):
                            pe.wait_ge(s_ld[p], it * LD + LD)
                        diag = lo + w == n
                        ins = pe.matmul(bank[:, 0:w], qb[p][0:KR, h, tile * P:(tile + 1) * P], kb[p][0:KR, h, lo:lo + w],
                                        start=True, stop=not diag)
                        if diag:
                            ins = pe.matmul(bank[:, w - P:w], identb[:], causal[:], start=False, stop=True)
                        ins.then_inc(s_item, 1)
                    else:
                        u = what[1]
                        pe.wait_ge(s_mcol, it * 2 * NU + 2 * u + 2)
                        for t in range(TPC):
                            ins = pe.transpose(bank[0:MROW + 1, t * P:(t + 1) * P], mt[u % 2][:, t, :], ident[:])
                        ins.then_inc(s_item, 1)

                def scores(it, n):
                    u, p, q, kt = steps[n]
                    d = kt - TPC * q
                    lo = min(max(d, 0) * P, 2 * P)
                    if n >= NST:
                        pe.wait_ge(s_exp, it * NS + n - NST + 1)
                    if kt == 0:
                        pe.wait_ge(s_iread, it * NI + end[u])
                    for h in range(2):
                        ins = pe.matmul(stb[n % NST][:, h * CH + lo:(h + 1) * CH], kb[p][:, h, kt * P:(kt + 1) * P],
                                        qb[p][:, h, q * CH + lo:(q + 1) * CH], start=True, stop=d < 0)
                        if d >= 0:
                            ins = pe.matmul(stb[n % NST][:, h * CH + d * P:h * CH + (d + 1) * P], causal[:], identb[:],
                                            start=False, stop=True)
                    ins.then_inc(s_st, 1)

                def values(it, n):
                    u, p, q, kt = steps[n]
                    d = kt - TPC * q
                    lo = max(d, 0) * P
                    pe.wait_ge(s_exp, it * NS + n + 1)
                    if kt == 0 and u >= NOB:
                        pe.wait_ge(s_oev, it * NU + u - NOB + 1)
                    for j, w in enumerate((vbuf[p][:, kt, 0:DH], vbuf[p][:, kt, DH:2 * DH], ones[:], ones[:])):
                        ins = pe.matmul(ob[u % NOB][j * DH:(j + 1) * DH, lo:], w, pt[n % NPB][:, j % 2, lo:],
                                        start=(kt == 0), stop=(d == TPC - 1))
                    ins.then_inc(s_pv, 1)

                pe.wait_ge(s_cst, NCST)
                pe.wait_ge(s_rows, 4)
                with pe.Fori(0, NG) as it:
                    done = 0
                    for i in range(start):
                        item(it, i)
                    done = start
                    for n in range(NS):
                        scores(it, n)
                        for i in range(done, upto[n]):
                            item(it, i)
                        done = upto[n]
                        if n:
                            values(it, n - 1)
                    values(it, NS - 1)


E = 8
F = 352
FS = [(0, P), (P, P), (2 * P, F - 2 * P)]
NF = len(FS)
NT = T // P


class FfnWeights:

    def __init__(self, al, name, raw=None):
        if raw is None:
            raw = (al.sb(f"{name}_gu", [P, 2, KD, F]), al.sb(f"{name}_d", [P, NF, D]))
        self.gu, self.d = raw
        self.guh, self.gul = al.sb(f"{name}_guh", [P, 2, KD, F], F32R), al.sb(f"{name}_gul", [P, 2, KD, F], F32R)
        self.dh, self.dl = al.sb(f"{name}_dh", [P, NF, D], F32R), al.sb(f"{name}_dl", [P, NF, D], F32R)

    def down_parts(self):
        w = FS[-1][1]
        return [(self.d[:, 0:NF - 1], self.dh[:, 0:NF - 1], self.dl[:, 0:NF - 1]),
                (self.d[0:w, NF - 1], self.dh[0:w, NF - 1], self.dl[0:w, NF - 1])]


def load_ffn(dma, wt, gate, up, down, sem):
    dma(wt.gu[:, 0], gate.rearrange("(k p) f -> p k f", p=P)).then_inc(sem, 16)
    dma(wt.gu[:, 1], up.rearrange("(k p) f -> p k f", p=P)).then_inc(sem, 16)
    dma(wt.d[:, 0:NF - 1], down[0:(NF - 1) * P].rearrange("(k p) n -> p k n", p=P)).then_inc(sem, 16)
    dma(wt.d[0:FS[-1][1], NF - 1], down[(NF - 1) * P:F]).then_inc(sem, 16)


def gate_up(nc, bank, wt, which, f, xh, xl):
    lo, w = FS[f]
    for k in range(KD):
        ins = mm3(nc, bank[0:w, :], wt.guh[:, which, k, lo:lo + w], wt.gul[:, which, k, lo:lo + w],
                  xh[:, k], xl[:, k], k == 0, k == KD - 1)
    return ins


def down(nc, bank, wt, hh, hl, t):
    for f, (_, w) in enumerate(FS):
        ins = mm3(nc, bank, hh[0:w, f, t * P:(t + 1) * P], hl[0:w, f, t * P:(t + 1) * P],
                  wt.dh[0:w, f], wt.dl[0:w, f], f == 0, f == NF - 1)
    return ins


def phase_shared(nc, x, w, scratch):
    with ExitStack() as ctx:
        al = Alloc(nc, ctx)
        ident = al.sb("c_ident", [P, P])
        mhalf = al.sb("c_mhalf", [P, TPC])
        wob = al.sb("c_wob", [P, D])
        wos = al.sb("c_wo", [P, KD, D])
        woh, wol = al.sb("c_woh", [P, KD, D], F32R), al.sb("c_wol", [P, KD, D], F32R)
        gw = al.sb("c_gw", [P, KD, E])
        gwh, gwl = al.sb("c_gwh", [P, KD, E], F32R), al.sb("c_gwl", [P, KD, E], F32R)
        wt = FfnWeights(al, "c_sw")
        sums = al.sb("c_sums", [P, CH])
        rsum = al.sb("c_rsum", [P, CH])
        oin = al.sb("c_oin", [P, KD, CH])
        rin = al.sb("c_rin", [P, KD, CH])
        xin = al.sb("c_xin", [P, TPC, D])
        on = oin
        oh, ol = al.sb("c_oh", [P, KD, CH], F32R), al.sb("c_ol", [P, KD, CH], F32R)
        xw = rin[:].rearrange("p k n -> p (k n)").rearrange("p (t n) -> p t n", t=TPC)
        x1 = al.sb("c_x1", [P, TPC, D])
        x1k = al.sb("c_x1k", [P, TPC, D])
        xn = al.sb("c_xn", [P, TPC, D])
        st, mv = al.sb("c_stats", [P, TPC, 6]), al.sb("c_mv", [P, TPC, 2])
        vare, rstd = al.sb("c_vare", [P, TPC]), al.sb("c_rstd", [P, TPC])
        xh, xl = al.sb("c_xh", [P, KD, CH], F32R), al.sb("c_xl", [P, KD, CH], F32R)
        sg = al.sb("c_sg", [P, NF, CH])
        hf = al.sb("c_hf", [P, NF, CH])
        hh, hl = al.sb("c_hh", [P, NF, CH], F32R), al.sb("c_hl", [P, NF, CH], F32R)
        acc = al.sb("c_acc", [P, TPC, D])
        lgT = al.sb("c_lgT", [E, CH])
        lg = al.sb("c_lg", [P, TPC, E])
        ab = [al.bank(f"c_ab{n}") for n in range(2)]
        lb = al.bank("c_lb")
        fb = [al.bank(f"c_fb{n}") for n in range(5)]

        s_w = al.sem("c_weights_in")
        s_vpass, s_gpass, s_ppass = al.sem("c_vector_passed"), al.sem("c_pool_passed"), al.sem("c_tensor_passed")
        s_cst = al.sem("c_constants_made")
        s_wh = al.sem("c_weights_high")
        s_wl = al.sem("c_weights_low")
        s_sum = al.sem("c_sums_in")
        s_rs = al.sem("c_reciprocals_made")
        s_rst = al.sem("c_reciprocals_stored")
        s_o = al.sem("c_attention_in")
        s_x = al.sem("c_x_in")
        s_on = al.sem("c_o_normalized")
        s_xw = al.sem("c_xw_made")
        s_oh = al.sem("c_oh_made")
        s_ol = al.sem("c_ol_made")
        s_at = al.sem("c_att_made")
        s_x1 = al.sem("c_x1_made")
        s_x1k = al.sem("c_x1_kept")
        s_stat = al.sem("c_stats_made")
        s_var = al.sem("c_var_made")
        s_vare = al.sem("c_vare_made")
        s_rstd = al.sem("c_rstd_made")
        s_xn = al.sem("c_xn_made")
        s_t = al.sem("c_transposed")
        s_xh = al.sem("c_xh_made")
        s_xl = al.sem("c_xl_made")
        s_lt = al.sem("c_logits_made")
        s_ltc = al.sem("c_logits_copied")
        s_gu = al.sem("c_gate_up_made")
        s_sg = al.sem("c_silu_made")
        s_h = al.sem("c_h_made")
        s_hh = al.sem("c_hh_made")
        s_hl = al.sem("c_hl_made")
        s_dn = al.sem("c_down_made")
        s_acc = al.sem("c_acc_made")
        s_xst = al.sem("c_xn_stored")
        s_ast = al.sem("c_acc_stored")
        s_lst = al.sem("c_logits_stored")

        with nc.Block() as block:
            @block.sync
            def _(sp):
                sp.dma_start(sums[:], scratch["sums"].rearrange("c h t -> (c h) t")).then_inc(s_sum, 16)
                sp.dma_start(wos[:], w["wo_w"].rearrange("(k p) n -> p k n", p=P)).then_inc(s_w, 16)
                sp.dma_start(wob[:], broadcast_rows(w["wo_b"], D)).then_inc(s_w, 16)
                with nc.allow_non_contiguous_dma(reason="router weights as columns"):
                    for k in range(KD):
                        sp.dma_start(gw[:, k], w["gate_w"][:, k * P:(k + 1) * P].rearrange("e p -> p e")).then_inc(s_w, 16)
                load_ffn(sp.dma_start, wt, w["sw_gate"], w["sw_up"], w["sw_down"], s_w)
                sp.wait_ge(s_rs, 1)
                sp.dma_start(scratch["rsum"].rearrange("c h t -> (c h) t"), rsum[:]).then_inc(s_rst, 16)
                sp.wait_ge(s_rst, 16)

                def load(c, first=False):
                    if not first:
                        sp.wait_ge(s_ol, c)
                    sp.dma_start(oin[:], scratch["oT"][bass.ds(c, 1)].rearrange("c (k p) t -> p (c k) t", p=P)).then_inc(s_o, 16)
                    if not first:
                        sp.wait_ge(s_x1, c * TPC)
                    for j in range(H // KD):
                        src = scratch["rsum"][bass.ds(c, 1), bass.ds(j, 1), :]
                        src = bass.AP(src.tensor, src.offset, [[0, DH], [H // KD * CH, KD], [1, CH]])
                        sp.dma_start(rin[j * DH:(j + 1) * DH], src).then_inc(s_o, 16)
                    sp.dma_start(xin[:], x[bass.ds(c * CH, CH), :].rearrange("(t p) n -> p t n", p=P)).then_inc(s_x, 16)

                def store_rows(c):
                    sp.wait_ge(s_xn, c * TPC + TPC)
                    sp.dma_start(scratch["xn"][bass.ds(c * CH, CH), :].rearrange("(t p) n -> p t n", p=P), xn[:]).then_inc(s_xst, 16)

                def store_acc(c):
                    sp.wait_ge(s_acc, c * TPC + TPC)
                    sp.dma_start(scratch["acc"][bass.ds(c * CH, CH), :].rearrange("(t p) n -> p t n", p=P), acc[:]).then_inc(s_ast, 16)

                def store_logits(c):
                    sp.wait_ge(s_ltc, c * 2 + 2)
                    sp.dma_start(scratch["logits"][:, bass.ds(c * TPC, TPC), :], lg[:]).then_inc(s_lst, 16)

                load(0, first=True)
                store_rows(0)
                store_logits(0)
                with sp.Fori(0, NCH - 1) as c:
                    load(c + 1)
                    store_rows(c + 1)
                    store_acc(c)
                    store_logits(c + 1)
                store_acc(NCH - 1)
                for sem in (s_xst, s_ast, s_lst):
                    sp.wait_ge(sem, NCH * 16)

            @block.gpsimd
            def _(g):
                make_identity(g, ident, s_cst, 0)
                g.memset(mhalf[:], -0.5).then_inc(s_cst, 1)

                def ahead(c, first=False):
                    g.wait_ge(s_o, c * 80 + 80)
                    g.tensor_tensor(on[:], oin[:], rin[:], ALU.mult).then_inc(s_on, 1)
                    g.wait_ge(s_x, c * 16 + 16)
                    g.wait_ge(s_on, c + 1)
                    for t in range(TPC):
                        ins = g.tensor_tensor(xw[:, t], xin[:, t], wob[:], ALU.add)
                    ins.then_inc(s_xw, 1)
                    wait_apart(g, s_var, c * TPC + TPC, s_gpass)
                    g.tensor_scalar(vare[:], mv[:, :, 1], EPS, None, ALU.add).then_inc(s_vare, 1)
                    g.wait_ge(s_vare, c + 1)
                    g.tensor_tensor(rstd[:], vare[:], mhalf[:], ALU.pow).then_inc(s_rstd, 1)

                g.wait_ge(s_cst, 3)
                g.wait_ge(s_w, 16 * 10)
                with g.Fori(0, NCH) as c:
                    ahead(c)

            @block.scalar
            def _(act):
                act.wait_ge(s_w, 16 * 10)
                act.activation(woh[:], wos[:], ACT.Copy).then_inc(s_wh, 1)
                act.activation(gwh[:], gw[:], ACT.Copy).then_inc(s_wh, 1)
                act.activation(wt.guh[:], wt.gu[:], ACT.Copy).then_inc(s_wh, 1)
                for raw, hi, lo in wt.down_parts():
                    act.activation(hi, raw, ACT.Copy).then_inc(s_wh, 1)

                def o_high(c, first=False):
                    act.wait_ge(s_on, c + 1)
                    if not first:
                        act.wait_ge(s_at, c * TPC)
                    act.activation(oh[:], on[:], ACT.Copy).then_inc(s_oh, 1)

                def hidden(c, f, first=False):
                    w = FS[f][1]
                    act.wait_ge(s_gu, (c * NF + f) * 2 + 2)
                    if not first:
                        act.wait_ge(s_h, (c - 1) * NF + f + 1)
                    act.activation(sg[0:w, f], fb[2 * f % 5][0:w, :], ACT.Silu).then_inc(s_sg, 1)
                    act.wait_ge(s_h, c * NF + f + 1)
                    if not first:
                        act.wait_ge(s_dn, c * TPC)
                    act.activation(hh[0:w, f], hf[0:w, f], ACT.Copy).then_inc(s_hh, 1)

                def x_high(c, first=False):
                    for k in range(KD):
                        act.wait_ge(s_t, c * KD + k + 1)
                        act.activation(xh[:, k], ab[k % 2][:], ACT.Copy).then_inc(s_xh, 1)

                def keep(c, first=False):
                    if not first:
                        act.wait_ge(s_acc, c * TPC)
                    act.wait_ge(s_x1, c * TPC + TPC)
                    act.activation(x1k[:], x1[:], ACT.Copy).then_inc(s_x1k, 1)

                o_high(0, first=True)
                x_high(0, first=True)
                keep(0, first=True)

                def step(c, first=False, last=False):
                    if not last:
                        o_high(c + 1)
                    for f in range(NF):
                        hidden(c, f, first)
                    if not last:
                        x_high(c + 1)
                        keep(c + 1)

                step(0, first=True)
                with act.Fori(1, NCH - 1) as c:
                    step(c)
                step(NCH - 1, last=True)

            @block.vector
            def _(v):
                v.wait_ge(s_sum, 16)
                v.reciprocal(rsum[:], sums[:]).then_inc(s_rs, 1)
                v.wait_ge(s_wh, 5)
                v.tensor_tensor(wol[:], wos[:], f32(woh[:]), ALU.subtract).then_inc(s_wl, 1)
                v.tensor_tensor(gwl[:], gw[:], f32(gwh[:]), ALU.subtract).then_inc(s_wl, 1)
                v.tensor_tensor(wt.gul[:], wt.gu[:], f32(wt.guh[:]), ALU.subtract).then_inc(s_wl, 1)
                for raw, hi, lo in wt.down_parts():
                    v.tensor_tensor(lo, raw, f32(hi), ALU.subtract).then_inc(s_wl, 1)

                def o_low(c, first=False):
                    v.wait_ge(s_oh, c + 1)
                    v.tensor_tensor(ol[:], on[:], f32(oh[:]), ALU.subtract).then_inc(s_ol, 1)

                def residual(c, first=False):
                    v.wait_ge(s_xw, c + 1)
                    if not first:
                        v.wait_ge(s_x1k, c)
                    for t in range(TPC):
                        v.wait_ge(s_at, c * TPC + t + 1)
                        v.tensor_tensor(x1[:, t], ab[t % 2][:], xw[:, t], ALU.add).then_inc(s_x1, 1)
                    for t in range(TPC):
                        v.wait_ge(s_x1, c * TPC + t + 1)
                        v.bn_stats(st[:, t], x1[:, t]).then_inc(s_stat, 1)
                    for t in range(TPC):
                        wait_apart(v, s_stat, c * TPC + t + 1, s_vpass)
                        v.bn_aggr(mv[:, t], st[:, t]).then_inc(s_var, 1)

                def norm(c, first=False):
                    v.wait_ge(s_rstd, c + 1)
                    v.wait_ge(s_var, c * TPC + TPC)
                    if not first:
                        v.wait_ge(s_xst, c * 16)
                        v.wait_ge(s_t, c * KD)
                    for t in range(TPC):
                        v.tensor_scalar(xn[:, t], x1[:, t], mv[:, t, 0:1], rstd[:, t:t + 1], ALU.subtract, ALU.mult).then_inc(s_xn, 1)

                def x_low(c, first=False):
                    for k in range(KD):
                        v.wait_ge(s_xh, c * KD + k + 1)
                        v.tensor_tensor(xl[:, k], ab[k % 2][:], f32(xh[:, k]), ALU.subtract).then_inc(s_xl, 1)

                def logits(c, first=False):
                    v.wait_ge(s_lt, c * 2 + 1)
                    v.tensor_copy(lgT[:], lb[0:E, :]).then_inc(s_ltc, 1)
                    v.wait_ge(s_lt, c * 2 + 2)
                    if not first:
                        v.wait_ge(s_lst, c * 16)
                    v.tensor_copy(lg[:], lb[:, 0:TPC * E].rearrange("p (t e) -> p t e", t=TPC)).then_inc(s_ltc, 1)

                def hidden(c, f, first=False):
                    w = FS[f][1]
                    v.wait_ge(s_sg, c * NF + f + 1)
                    if not first:
                        v.wait_ge(s_hl, (c - 1) * NF + f + 1)
                    v.tensor_tensor(hf[0:w, f], sg[0:w, f], fb[(2 * f + 1) % 5][0:w, :], ALU.mult).then_inc(s_h, 1)
                    v.wait_ge(s_hh, c * NF + f + 1)
                    v.tensor_tensor(hl[0:w, f], hf[0:w, f], f32(hh[0:w, f]), ALU.subtract).then_inc(s_hl, 1)

                def add_shared(c, first=False):
                    v.wait_ge(s_x1k, c + 1)
                    if not first:
                        v.wait_ge(s_ast, c * 16)
                    for t in range(TPC):
                        v.wait_ge(s_dn, c * TPC + t + 1)
                        v.tensor_tensor(acc[:, t], fb[(2 * NF + t) % 5][:], x1k[:, t], ALU.add).then_inc(s_acc, 1)

                o_low(0, first=True)
                residual(0, first=True)
                norm(0, first=True)
                x_low(0, first=True)
                logits(0, first=True)

                def step(c, first=False, last=False):
                    if not last:
                        o_low(c + 1)
                    for f in range(NF - 1):
                        hidden(c, f, first)
                    if not last:
                        residual(c + 1)
                    hidden(c, NF - 1, first)
                    if not last:
                        norm(c + 1)
                    add_shared(c, first)
                    if not last:
                        x_low(c + 1)
                        logits(c + 1)

                step(0, first=True)
                with v.Fori(1, NCH - 1) as c:
                    step(c)
                step(NCH - 1, last=True)

            @block.tensor
            def _(pe):
                NFB = 2 * NF + TPC

                def att(c, first=False):
                    pe.wait_ge(s_ol, c + 1)
                    for t in range(TPC):
                        if t >= 2:
                            pe.wait_ge(s_x1, c * TPC + t - 1)
                        elif not first:
                            pe.wait_ge(s_xl, c * KD - 1 + t)
                        for k in range(KD):
                            ins = mm3(nc, ab[t % 2][:], oh[:, k, t * P:(t + 1) * P], ol[:, k, t * P:(t + 1) * P],
                                      woh[:, k], wol[:, k], k == 0, k == KD - 1)
                        ins.then_inc(s_at, 1)

                def transposes(c, first=False):
                    pe.wait_ge(s_xn, c * TPC + TPC)
                    for k in range(KD):
                        if k >= 2:
                            pe.wait_ge(s_xl, c * KD + k - 1)
                        for t in range(TPC):
                            ins = pe.transpose(ab[k % 2][:, t * P:(t + 1) * P], xn[:, t, k * P:(k + 1) * P], ident[:])
                        ins.then_inc(s_t, 1)

                def logits(c, first=False):
                    pe.wait_ge(s_xl, c * KD + KD)
                    if not first:
                        pe.wait_ge(s_ltc, c * 2)
                    for k in range(KD):
                        ins = mm3(nc, lb[0:E, :], gwh[:, k], gwl[:, k], xh[:, k], xl[:, k], k == 0, k == KD - 1)
                    ins.then_inc(s_lt, 1)
                    wait_apart(pe, s_ltc, c * 2 + 1, s_ppass)
                    for t in range(TPC):
                        ins = pe.transpose(lb[:, t * E:(t + 1) * E], lgT[:, t * P:(t + 1) * P], ident[0:E, 0:E])
                    ins.then_inc(s_lt, 1)

                def hidden(c, f, first=False):
                    for which in range(2):
                        n = 2 * f + which
                        if n >= 5:
                            pe.wait_ge(s_sg, c * NF + (n - 5) // 2 + 1)
                        elif not first:
                            pe.wait_ge(s_acc, c * TPC)
                        gate_up(nc, fb[n % 5][:], wt, which, f, xh, xl).then_inc(s_gu, 1)

                def down_rows(c, first=False):
                    pe.wait_ge(s_hl, c * NF + NF)
                    for t in range(TPC):
                        pe.wait_ge(s_h, c * NF + NF)
                        down(nc, fb[(2 * NF + t) % 5][:], wt, hh, hl, t).then_inc(s_dn, 1)

                pe.wait_ge(s_cst, 3)
                pe.wait_ge(s_wl, 5)
                att(0, first=True)
                transposes(0, first=True)
                logits(0, first=True)

                def step(c, first=False, last=False):
                    for f in range(NF - 1):
                        hidden(c, f, first)
                    if not last:
                        att(c + 1)
                    hidden(c, NF - 1, first)
                    down_rows(c, first)
                    if not last:
                        transposes(c + 1)
                        logits(c + 1)

                step(0, first=True)
                with pe.Fori(1, NCH - 1) as c:
                    step(c)
                step(NCH - 1, last=True)


SLOTS = 512
NB = (2 * T + E * (SLOTS - 1)) // SLOTS
TPB = SLOTS // P


def phase_route(nc, keep, scratch):
    with ExitStack() as ctx:
        al = Alloc(nc, ctx)
        ident = al.sb("d_ident", [P, P])
        ones = al.sb("d_ones", [P, P])
        before = al.sb("d_before", [P, P])
        rank = al.sb("d_rank", [P, NT, E])
        steps = al.sb("d_steps", [P, E, T // SLOTS])
        blk = al.sb("d_blk", [P, NB, E])
        tok = al.sb("d_tok", [P, NT])
        zero = al.sb("d_zero", [NB * TPB, P])
        lg = al.sb("d_lg", [P, NT, E])
        a, b2 = al.sb("d_a", [P, NT, E]), al.sb("d_b", [P, NT, E])
        oh = [al.sb(f"d_oh{n}", [P, NT, E]) for n in range(2)]
        m = [al.sb(f"d_m{n}", [P, NT]) for n in range(2)]
        r = al.sb("d_r", [P, NT])
        both = al.sb("d_both", [P, NT, E])
        tot, cum = al.sb("d_tot", [P, NT, E]), al.sb("d_cum", [P, NT, E])
        cmp1 = al.sb("d_cmp1", [P, E, T // SLOTS])
        cmp2 = al.sb("d_cmp2", [P, NB, E])
        nb, endb, startb = al.sb("d_nb", [P, E]), al.sb("d_endb", [P, E]), al.sb("d_startb", [P, E])
        ebf = al.sb("d_ebf", [P, NB])
        slotf = [al.sb(f"d_slotf{n}", [P, NT]) for n in range(2)]
        ex = al.sb("d_ex", [P, NT])
        den = al.sb("d_den", [P, NT])
        ids = al.sb("d_ids", [NB * TPB, P])
        pre, tob = al.bank("d_pre"), al.bank("d_totals")
        idb = al.bank("d_idb")

        s_in = al.sem("d_logits_in")
        s_cst = al.sem("d_constants_made")
        s_v = al.sem("d_vector_step")
        s_mm = al.sem("d_counts_made")
        s_ex = al.sem("d_exp_made")
        s_z = al.sem("d_ids_cleared")
        s_sc = al.sem("d_ids_scattered")
        s_id = al.sem("d_ids_in")
        s_it = al.sem("d_ids_turned")
        marks = {}

        with nc.Block() as block:
            @block.vector
            def _(v):
                done = [0]

                def step(ins, mark=None):
                    done[0] += 1
                    ins.then_inc(s_v, 1)
                    v.wait_ge(s_v, done[0])
                    if mark:
                        marks[mark] = done[0]

                def over(ap, n, axis):
                    return ap.unsqueeze(axis).to_broadcast([P, n, E] if axis == 1 else [P, ap.shape[1], n])

                v.wait_ge(s_cst, 10)
                v.wait_ge(s_in, 16)
                src = lg
                for n in range(2):
                    step(v.tensor_reduce(m[n][:], src[:], AX.X, ALU.max), "max2" if n else None)
                    step(v.tensor_tensor(a[:], src[:], over(m[n][:], E, 2), ALU.is_equal))
                    step(v.tensor_tensor(b2[:], a[:], rank[:], ALU.mult))
                    step(v.tensor_reduce(r[:], b2[:], AX.X, ALU.max))
                    step(v.tensor_tensor(oh[n][:], b2[:], over(r[:], E, 2), ALU.is_equal))
                    if n == 0:
                        step(v.scalar_tensor_tensor(out=both[:], in0=oh[0][:], scalar=-3e38, in1=lg[:], op0=ALU.mult, op1=ALU.add))
                        src = both
                step(v.tensor_tensor(both[:], oh[0][:], oh[1][:], ALU.add), "both")
                step(v.tensor_tensor(ex[:], m[1][:], m[0][:], ALU.subtract), "gap")
                v.wait_ge(s_mm, 1)
                step(v.tensor_copy(tot[:], tob[:, 0:NT * E].rearrange("p (t e) -> p t e", t=NT)))
                for e in range(E):
                    step(v.tensor_tensor_scan(cum[:, :, e], ones[:, 0:NT], tot[:, :, e], 0.0, ALU.mult, ALU.add))
                step(v.tensor_tensor(cmp1[:], steps[:], over(cum[:, NT - 1, :], T // SLOTS, 2), ALU.is_lt))
                step(v.tensor_reduce(nb[:], cmp1[:], AX.X, ALU.add))
                step(v.tensor_tensor_scan(endb[:], ones[:, 0:E], nb[:], 0.0, ALU.mult, ALU.add))
                step(v.tensor_tensor(startb[:], endb[:], nb[:], ALU.subtract))
                step(v.tensor_scalar(startb[:], startb[:], float(SLOTS), None, ALU.mult))
                step(v.tensor_tensor(cum[:], cum[:], tot[:], ALU.subtract))
                step(v.tensor_tensor(cum[:], cum[:], over(startb[:], NT, 1), ALU.add))
                step(v.tensor_tensor(cum[:], pre[:, 0:NT * E].rearrange("p (t e) -> p t e", t=NT), cum[:], ALU.add))
                for n in range(2):
                    step(v.tensor_tensor(a[:], cum[:], oh[n][:], ALU.mult))
                    step(v.tensor_reduce(slotf[n][:], a[:], AX.X, ALU.add))
                    step(v.tensor_copy(keep["slot"][n][:], slotf[n][:]), f"slot{n}")
                step(v.tensor_tensor(cmp2[:], blk[:], over(endb[:], NB, 1), ALU.is_ge))
                step(v.tensor_reduce(ebf[:], cmp2[:], AX.X, ALU.add))
                step(v.tensor_scalar(ebf[:], ebf[:], float(E - 1), None, ALU.min))
                step(v.tensor_copy(keep["expert"][:], ebf[:]))
                v.wait_ge(s_ex, 1)
                step(v.tensor_scalar(den[:], ex[:], 1.0, None, ALU.add))
                step(v.reciprocal(keep["weight"][0][:], den[:]))
                step(v.tensor_tensor(keep["weight"][1][:], ex[:], keep["weight"][0][:], ALU.mult))
                v.wait_ge(s_it, 1)
                v.tensor_copy(keep["token"][:], idb[:, 0:NB * TPB])

            @block.sync
            def _(sp):
                sp.dma_start(lg[:], scratch["logits"]).then_inc(s_in, 16)
                sp.wait_ge(s_cst, 10)
                sp.dma_start(scratch["tokens"].rearrange("(s p) a -> s (p a)", p=P), zero[:]).then_inc(s_z, 16)
                sp.wait_ge(s_sc, 16 * 2 * NT)
                sp.dma_start(ids[:], scratch["tokens"].rearrange("(s p) a -> s (p a)", p=P)).then_inc(s_id, 16)

            @block.gpsimd
            def _(g):
                with nc.allow_low_precision(reason="integers below 2^24"):
                    make_identity(g, ident, s_cst, 0)
                    g.memset(ones[:], 1.0).then_inc(s_cst, 1)
                    g.memset(before[:], 1.0).then_inc(s_cst, 1)
                    g.memset(zero[:], 0.0).then_inc(s_cst, 1)
                    g.wait_ge(s_cst, 5)
                    g.affine_select(out=before[:], in_=before[:], compare_op=ALU.is_gt, fill=0.0, base=0,
                                    pattern=[[1, P]], channel_multiplier=-1).then_inc(s_cst, 1)
                    kw = dict(allow_small_or_imprecise_dtypes=True)
                    g.iota(rank[:], [[0, NT], [-1, E]], base=E, channel_multiplier=0, **kw).then_inc(s_cst, 1)
                    g.iota(steps[:], [[0, E], [SLOTS, T // SLOTS]], base=0, channel_multiplier=0, **kw).then_inc(s_cst, 1)
                    g.iota(blk[:], [[1, NB], [0, E]], base=0, channel_multiplier=0, **kw).then_inc(s_cst, 1)
                    g.iota(tok[:], [[P, NT]], base=0, channel_multiplier=1, **kw).then_inc(s_cst, 1)
                g.wait_ge(s_cst, 10)
                g.wait_ge(s_z, 16)
                for n in range(2):
                    g.wait_ge(s_v, marks[f"slot{n}"])
                    for t in range(NT):
                        g.indirect_dma_start(out=scratch["tokens"], in_=tok[:, t:t + 1], in_offset=None,
                                             out_offset=bass.IndirectOffsetOnAxis(ap=keep["slot"][n][:, t:t + 1], axis=0)).then_inc(s_sc, 16)

            @block.scalar
            def _(act):
                act.wait_ge(s_v, marks["gap"])
                act.activation(ex[:], ex[:], ACT.Exp).then_inc(s_ex, 1)

            @block.tensor
            def _(pe):
                pe.wait_ge(s_cst, 10)
                pe.wait_ge(s_v, marks["both"])
                rows = both[:].rearrange("p t e -> p (t e)")
                pe.matmul(pre[:, 0:NT * E], before[:], rows, start=True, stop=True)
                pe.matmul(tob[:, 0:NT * E], ones[:], rows, start=True, stop=True).then_inc(s_mm, 1)
                pe.wait_ge(s_id, 16)
                pe.transpose(idb[:, 0:NB * TPB], ids[:], ident[0:NB * TPB, 0:NB * TPB]).then_inc(s_it, 1)


def phase_experts(nc, keep, w, scratch):
    with ExitStack() as ctx:
        al = Alloc(nc, ctx)
        ident = al.sb("e_ident", [P, P])
        wt = [FfnWeights(al, f"e_w{n}") for n in range(2)]
        xg = [al.sb(f"e_xg{n}", [P, TPB, D]) for n in range(2)]
        idx = [al.sb(f"e_idx{n}", [P, TPB], U32) for n in range(2)]
        xh, xl = al.sb("e_xh", [P, KD, SLOTS], F32R), al.sb("e_xl", [P, KD, SLOTS], F32R)
        sg, hf = al.sb("e_sg", [P, NF, SLOTS]), al.sb("e_hf", [P, NF, SLOTS])
        hh, hl = al.sb("e_hh", [P, NF, SLOTS], F32R), al.sb("e_hl", [P, NF, SLOTS], F32R)
        y = al.sb("e_y", [P, TPB, D])
        tbk = [al.bank(f"e_tb{n}") for n in range(2)]
        fb = [al.bank(f"e_fb{n}") for n in range(5)]

        s_cst = al.sem("e_constants_made")
        s_gpass = al.sem("e_pool_passed")
        s_w = [al.sem(f"e_weights_in{n}") for n in range(2)]
        s_x = [al.sem(f"e_rows_in{n}") for n in range(2)]
        s_wh, s_wl = al.sem("e_weights_high"), al.sem("e_weights_low")
        s_idx = al.sem("e_tokens_copied")
        s_t = al.sem("e_transposed")
        s_xh, s_xl = al.sem("e_xh_made"), al.sem("e_xl_made")
        s_gu, s_sg, s_h = al.sem("e_gate_up_made"), al.sem("e_silu_made"), al.sem("e_h_made")
        s_hh, s_hl = al.sem("e_hh_made"), al.sem("e_hl_made")
        s_dn, s_y, s_yst = al.sem("e_down_made"), al.sem("e_y_made"), al.sem("e_y_stored")

        def in_pairs(eng, step):
            step(0, 0, True, False)
            step(1, 1, False, False)
            with eng.Fori(1, (NB - 1) // 2) as i:
                step(i * 2, 0, False, False)
                step(i * 2 + 1, 1, False, False)
            step(NB - 1, 0, False, True)

        assert NB % 2 == 1

        def turns(b, n):
            return b // 2 + 1 if isinstance(b, int) else (b - n) // 2 + 1

        with nc.Block() as block:
            @block.sync
            def _(sp):
                def fetch(b, n, first=False):
                    if not first:
                        sp.wait_ge(s_wl, (b - 1) * 3)
                    e = sp.value_load(keep["expert"][0:1, bass.ds(b, 1)], min_val=0, max_val=E - 1)
                    load_ffn(sp.dma_start, wt[n], w["w_gate"][bass.ds(e, 1)].rearrange("e d f -> (e d) f"),
                             w["w_up"][bass.ds(e, 1)].rearrange("e d f -> (e d) f"),
                             w["w_down"][bass.ds(e, 1)].rearrange("e f d -> (e f) d"), s_w[n])

                def store(b):
                    sp.wait_ge(s_y, b * TPB + TPB)
                    sp.dma_start(scratch["y"][bass.ds(b * SLOTS, SLOTS), :].rearrange("(t p) n -> p t n", p=P), y[:]).then_inc(s_yst, 16)

                fetch(0, 0, True)
                fetch(1, 1, True)
                fetch(2, 0)
                store(0)
                with sp.Fori(1, (NB - 1) // 2) as i:
                    fetch(i * 2 + 1, 1)
                    store(i * 2 - 1)
                    fetch(i * 2 + 2, 0)
                    store(i * 2)
                store(NB - 2)
                store(NB - 1)
                sp.wait_ge(s_yst, NB * 16)

            @block.gpsimd
            def _(g):
                make_identity(g, ident, s_cst, 0)

                def gather(b, n, first=False, last=False):
                    if not (isinstance(b, int) and b < 2):
                        g.wait_ge(s_t, (b - 1) * KD)
                    g.tensor_copy(idx[n][:], keep["token"][:, bass.ds(b * TPB, TPB)]).then_inc(s_idx, 1)
                    wait_apart(g, s_idx, b + 1, s_gpass)
                    for t in range(TPB):
                        g.indirect_dma_start(out=xg[n][:, t, :], in_=scratch["xn"], out_offset=None,
                                             in_offset=bass.IndirectOffsetOnAxis(ap=idx[n][:, t:t + 1], axis=0)).then_inc(s_x[n], 16)

                in_pairs(g, gather)

            @block.scalar
            def _(act):
                def split(b, n, first=False):
                    act.wait_ge(s_w[n], turns(b, n) * 64)
                    if not first:
                        act.wait_ge(s_dn, (b - 1) * TPB)
                    act.activation(wt[n].guh[:], wt[n].gu[:], ACT.Copy).then_inc(s_wh, 1)
                    for raw, hi, lo in wt[n].down_parts():
                        act.activation(hi, raw, ACT.Copy).then_inc(s_wh, 1)

                def x_high(b, first=False):
                    for k in range(KD):
                        act.wait_ge(s_t, b * KD + k + 1)
                        act.activation(xh[:, k], tbk[k % 2][:], ACT.Copy).then_inc(s_xh, 1)

                def step(b, n, first, last):
                    for f, (_, width) in enumerate(FS):
                        act.wait_ge(s_gu, (b * NF + f) * 2 + 2)
                        if not first:
                            act.wait_ge(s_h, (b - 1) * NF + f + 1)
                        act.activation(sg[0:width, f], fb[2 * f % 5][0:width, :], ACT.Silu).then_inc(s_sg, 1)
                        act.wait_ge(s_h, b * NF + f + 1)
                        if not first:
                            act.wait_ge(s_dn, b * TPB)
                        act.activation(hh[0:width, f], hf[0:width, f], ACT.Copy).then_inc(s_hh, 1)
                        if f == 0 and not last:
                            split(b + 1, 1 - n, first)
                    if not last:
                        x_high(b + 1)

                split(0, 0, True)
                x_high(0, True)
                in_pairs(act, step)

            @block.vector
            def _(v):
                def split(b, n):
                    v.wait_ge(s_wh, b * 3 + 3)
                    v.tensor_tensor(wt[n].gul[:], wt[n].gu[:], f32(wt[n].guh[:]), ALU.subtract).then_inc(s_wl, 1)
                    for raw, hi, lo in wt[n].down_parts():
                        v.tensor_tensor(lo, raw, f32(hi), ALU.subtract).then_inc(s_wl, 1)

                def x_low(b):
                    for k in range(KD):
                        v.wait_ge(s_xh, b * KD + k + 1)
                        v.tensor_tensor(xl[:, k], tbk[k % 2][:], f32(xh[:, k]), ALU.subtract).then_inc(s_xl, 1)

                def step(b, n, first, last):
                    for f, (_, width) in enumerate(FS):
                        v.wait_ge(s_sg, b * NF + f + 1)
                        v.tensor_tensor(hf[0:width, f], sg[0:width, f], fb[(2 * f + 1) % 5][0:width, :], ALU.mult).then_inc(s_h, 1)
                        v.wait_ge(s_hh, b * NF + f + 1)
                        v.tensor_tensor(hl[0:width, f], hf[0:width, f], f32(hh[0:width, f]), ALU.subtract).then_inc(s_hl, 1)
                        if f == 0 and not last:
                            split(b + 1, 1 - n)
                    if not last:
                        x_low(b + 1)
                    if not first:
                        v.wait_ge(s_yst, b * 16)
                    for t in range(TPB):
                        v.wait_ge(s_dn, b * TPB + t + 1)
                        v.tensor_copy(y[:, t], fb[(2 * NF + t) % 5][:]).then_inc(s_y, 1)

                split(0, 0)
                x_low(0)
                in_pairs(v, step)

            @block.tensor
            def _(pe):
                def transposes(b, n, first=False):
                    pe.wait_ge(s_x[n], turns(b, n) * TPB * 16)
                    for k in range(KD):
                        if k >= 2:
                            pe.wait_ge(s_xl, b * KD + k - 1)
                        elif not first:
                            pe.wait_ge(s_xl, b * KD - 1 + k)
                        for t in range(TPB):
                            ins = pe.transpose(tbk[k % 2][:, t * P:(t + 1) * P], xg[n][:, t, k * P:(k + 1) * P], ident[:])
                        ins.then_inc(s_t, 1)

                def step(b, n, first, last):
                    pe.wait_ge(s_wl, b * 3 + 3)
                    pe.wait_ge(s_xl, b * KD + KD)
                    for f in range(NF):
                        for which in range(2):
                            j = 2 * f + which
                            if j >= 5:
                                pe.wait_ge(s_sg, b * NF + (j - 5) // 2 + 1)
                            elif not first:
                                pe.wait_ge(s_y, b * TPB)
                            gate_up(nc, fb[j % 5][:], wt[n], which, f, xh, xl).then_inc(s_gu, 1)
                    if not last:
                        transposes(b + 1, 1 - n)
                    pe.wait_ge(s_hl, b * NF + NF)
                    for t in range(TPB):
                        down(nc, fb[(2 * NF + t) % 5][:], wt[n], hh, hl, t).then_inc(s_dn, 1)

                pe.wait_ge(s_cst, 2)
                transposes(0, 0, True)
                in_pairs(pe, step)


def phase_combine(nc, keep, scratch, out):
    RING = 4
    with ExitStack() as ctx:
        al = Alloc(nc, ctx)
        y = [[al.sb(f"f_y{k}_{n}", [P, D]) for n in range(RING)] for k in range(2)]
        acc = [al.sb(f"f_acc{n}", [P, D]) for n in range(RING)]
        mid = al.sb("f_mid", [P, D])
        res = [al.sb(f"f_res{n}", [P, D]) for n in range(RING)]
        s_y = [al.sem(f"f_rows_in{n}") for n in range(RING)]
        s_a = [al.sem(f"f_acc_in{n}") for n in range(RING)]
        s_o = [al.sem(f"f_out_stored{n}") for n in range(RING)]
        s_m, s_r = al.sem("f_first_added"), al.sem("f_second_added")

        with nc.Block() as block:
            @block.gpsimd
            def _(g):
                for t in range(NT):
                    n = t % RING
                    if t >= RING:
                        g.wait_ge(s_r, t - RING + 1)
                    for k in range(2):
                        g.indirect_dma_start(out=y[k][n][:], in_=scratch["y"], out_offset=None,
                                             in_offset=bass.IndirectOffsetOnAxis(ap=keep["slot"][k][:, t:t + 1], axis=0)).then_inc(s_y[n], 16)

            @block.sync
            def _(sp):
                for t in range(NT):
                    n = t % RING
                    if t >= RING:
                        sp.wait_ge(s_r, t - RING + 1)
                    sp.dma_start(acc[n][:], scratch["acc"][t * P:(t + 1) * P, :]).then_inc(s_a[n], 16)

            @block.scalar
            def _(act):
                for t in range(NT):
                    act.wait_ge(s_r, t + 1)
                    act.dma_start(out[t * P:(t + 1) * P, :], res[t % RING][:]).then_inc(s_o[t % RING], 16)
                for n in range(RING):
                    act.wait_ge(s_o[n], 16 * NT // RING)

            @block.vector
            def _(v):
                for t in range(NT):
                    n = t % RING
                    v.wait_ge(s_y[n], (t // RING + 1) * 32)
                    v.wait_ge(s_a[n], (t // RING + 1) * 16)
                    if t:
                        v.wait_ge(s_r, t)
                    v.scalar_tensor_tensor(out=mid[:], in0=y[0][n][:], scalar=keep["weight"][0][:, t:t + 1], in1=acc[n][:],
                                           op0=ALU.mult, op1=ALU.add).then_inc(s_m, 1)
                    v.wait_ge(s_m, t + 1)
                    if t >= RING:
                        v.wait_ge(s_o[n], t // RING * 16)
                    v.scalar_tensor_tensor(out=res[n][:], in0=y[1][n][:], scalar=keep["weight"][1][:, t:t + 1], in1=mid[:],
                                           op0=ALU.mult, op1=ALU.add).then_inc(s_r, 1)


INS = ['L0_attn_x', 'L0_attn_wq_w', 'L0_attn_wq_b', 'L0_attn_wk_w', 'L0_attn_wk_b', 'L0_attn_wkl_w', 'L0_attn_wkl_b',
       'L0_attn_wv_w', 'L0_attn_wv_b', 'L0_attn_wvl_w', 'L0_attn_wvl_b', 'L0_attn_upk_w', 'L0_attn_upk_b',
       'L0_attn_upv_w', 'L0_attn_upv_b', 'L0_attn_wo_w', 'L0_attn_wo_b', 'L0_ffn_gate_w', 'L0_ffn_w_gate',
       'L0_ffn_w_up', 'L0_ffn_w_down', 'L0_ffn_sw_gate', 'L0_ffn_sw_up', 'L0_ffn_sw_down']


def program(nc, ins, out):
    w = {n.split("_", 2)[2]: ap for n, ap in ins.items()}
    x = ins['L0_attn_x'].rearrange("b s d -> (b s) d")

    def dram(name, shape, dt=F32):
        return nc.dram_tensor(name, shape, dt, kind="Internal").ap()

    scratch = {
        "qh": dram("scr_qh", (NCH, D, CH)), "ql": dram("scr_ql", (NCH, D, CH)),
        "kh": dram("scr_kh", (NCH, D, CH)), "kl": dram("scr_kl", (NCH, D, CH)),
        "v": dram("scr_v", (NCH, CH, D)),
        "oT": dram("scr_oT", (NCH, D, CH)), "sums": dram("scr_sums", (NCH, H, CH)),
        "rsum": dram("scr_rsum", (NCH, H, CH)), "xn": dram("scr_xn", (T, D)), "acc": dram("scr_acc", (T, D)),
        "logits": dram("scr_logits", (P, NT, E)), "tokens": dram("scr_tokens", (NB * SLOTS, 1)),
        "y": dram("scr_y", (NB * SLOTS, D)),
    }
    phase_project(nc, x, w, scratch)
    phase_attention(nc, scratch)
    phase_shared(nc, x, w, scratch)
    with ExitStack() as ctx:
        al = Alloc(nc, ctx)
        keep = {
            "slot": [al.sb(f"slot{n}", [P, NT], U32) for n in range(2)],
            "weight": [al.sb(f"weight{n}", [P, NT]) for n in range(2)],
            "expert": al.sb("expert", [P, NB], I32),
            "token": al.sb("token", [P, NB * TPB], U32),
        }
        phase_route(nc, keep, scratch)
        phase_experts(nc, keep, w, scratch)
        phase_combine(nc, keep, scratch, out.rearrange("b s d -> (b s) d"))


_OUTS = [((BATCH, SEQ, D), 'float32')]


def kernel(**inputs):
    import numpy as _np
    import concourse.bacc as _bacc
    from concourse import mybir as _mybir
    from concourse.bass_utils import run_bass_kernel_spmd as _run

    nc = _bacc.Bacc("TRN2", target_bir_lowering=False, num_devices=1)
    arrays, ins = {}, {}
    for name in INS:
        a = _np.ascontiguousarray(inputs[name])
        arrays[f"in_{name}_dram"] = a
        ins[name] = nc.dram_tensor(f"in_{name}_dram", a.shape, _mybir.dt.from_np(a.dtype), kind="ExternalInput").ap()
    shape, dtype = _OUTS[0]
    out = nc.dram_tensor("out_0_dram", shape, _mybir.dt.from_np(_np.dtype(dtype)), kind="ExternalOutput").ap()
    program(nc, ins, out)
    r = _run(nc, [arrays], core_ids=[0])
    return r.results[0]["out_0_dram"]
```

```python
from contextlib import ExitStack

import concourse.bass as bass
from concourse import mybir

F32 = mybir.dt.float32
F32R = mybir.dt.float32r
I32 = mybir.dt.int32
U32 = mybir.dt.uint32
ALU = mybir.AluOpType
ACT = mybir.ActivationFunctionType
AX = mybir.AxisListType

P = 128
BATCH, SEQ, D = 2, 2048, 512
T = BATCH * SEQ
H, DH, DL = 16, 32, 128
KD = D // P
CH = 512
NCH = T // CH
CPB = SEQ // CH
TPC = CH // P
EPS = 1e-5


class Alloc:

    def __init__(self, nc, ctx):
        self.nc, self.ctx = nc, ctx

    def sb(self, name, shape, dt=F32):
        return self.ctx.enter_context(self.nc.sbuf_tensor(name, shape, dt))

    def bank(self, name, cols=512, dt=F32):
        return self.ctx.enter_context(self.nc.psum_tensor(name, [P, cols], dt))

    def sem(self, name):
        return self.ctx.enter_context(self.nc.semaphore(name))


def f32(ap):
    return ap.bitcast(F32)


def wait_apart(eng, sem, value, passed):
    eng.wait_ge(sem, value)
    eng.sem_inc(passed, 1)


def mm3(nc, out, wh, wl, xh, xl, first, last):
    nc.tensor.matmul(out, wh, xh, start=first, stop=False)
    nc.tensor.matmul(out, wl, xh, start=False, stop=False)
    return nc.tensor.matmul(out, wh, xl, start=False, stop=last)


def broadcast_rows(ap1d, n):
    return bass.AP(ap1d.tensor, ap1d.offset, [[0, P], [1, n]])


def make_identity(g, ident, s_made, count):
    g.memset(ident[:], 0.0).then_inc(s_made, 1)
    g.wait_ge(s_made, count + 1)
    g.affine_select(out=ident[:], in_=ident[:], compare_op=ALU.not_equal, fill=1.0, base=0,
                    pattern=[[-1, P]], channel_multiplier=1).then_inc(s_made, 1)


def phase_project(nc, x, w, scratch):
    with ExitStack() as ctx:
        al = Alloc(nc, ctx)
        ident = al.sb("a_ident", [P, P])
        wstage = al.sb("a_wstage", [P, 3, KD, D])
        lat = al.sb("a_lat", [P, 2, KD, DL])
        up = al.sb("a_up", [P, 2, D])
        wT = al.sb("a_wT", [P, 2, KD, D])
        bcol = al.sb("a_bcol", [P, 5, KD])
        vb = al.sb("a_vb", [P, D])
        wqh, wql = al.sb("a_wqh", [P, KD, D], F32R), al.sb("a_wql", [P, KD, D], F32R)
        fh, fl = al.sb("a_fh", [P, 2, KD, DL], F32R), al.sb("a_fl", [P, 2, KD, DL], F32R)
        uh, ul = al.sb("a_uh", [P, 2, D], F32R), al.sb("a_ul", [P, 2, D], F32R)
        xin = al.sb("a_xin", [P, TPC, D])
        xn = al.sb("a_xn", [P, TPC, D])
        xh, xl = al.sb("a_xh", [P, KD, CH], F32R), al.sb("a_xl", [P, KD, CH], F32R)
        st = al.sb("a_stats", [P, TPC, 6])
        mv = al.sb("a_mv", [P, TPC, 2])
        vare = al.sb("a_vare", [P, TPC])
        mhalf = al.sb("a_mhalf", [P, TPC])
        rstd = al.sb("a_rstd", [P, TPC])
        lh, ll = al.sb("a_lh", [P, 2, CH], F32R), al.sb("a_ll", [P, 2, CH], F32R)
        qh, ql = al.sb("a_qh", [P, KD, CH], F32R), al.sb("a_ql", [P, KD, CH], F32R)
        kh, kl = al.sb("a_kh", [P, KD, CH], F32R), al.sb("a_kl", [P, KD, CH], F32R)
        vo = al.sb("a_vo", [P, TPC, D])
        tb = [al.bank(f"a_tb{n}") for n in range(KD)]
        ob = [al.bank(f"a_ob{n}") for n in range(4)]

        s_w = al.sem("a_weights_in")
        s_vpass, s_gpass = al.sem("a_vector_passed"), al.sem("a_pool_passed")
        s_id = al.sem("a_ident_made")
        s_wt = al.sem("a_weight_transposed")
        s_wc = al.sem("a_weight_copied")
        s_fold = al.sem("a_folded")
        s_split = al.sem("a_weights_split")
        s_x = al.sem("a_x_in")
        s_xfree = al.sem("a_x_read")
        s_stat = al.sem("a_stats_made")
        s_var = al.sem("a_var_made")
        s_vare = al.sem("a_vare_made")
        s_rstd = al.sem("a_rstd_made")
        s_xn = al.sem("a_xn_made")
        s_t = al.sem("a_x_transposed")
        s_xh = al.sem("a_xh_made")
        s_xl = al.sem("a_xl_made")
        s_mm = al.sem("a_product_made")
        s_hi = al.sem("a_hi_made")
        s_out = al.sem("a_bank_read")
        s_st = al.sem("a_stored")
        s_free = al.sem("a_stage_free")

        NP = 2 + KD + KD + TPC
        Q0, K0, V0 = 2, 2 + KD, 2 + 2 * KD

        with nc.Block() as block:
            @block.sync
            def _(sp):
                with nc.allow_non_contiguous_dma(reason="bias columns"):
                    for n, name in enumerate(("wq_w", "wk_w", "wv_w")):
                        sp.dma_start(wstage[:, n], w[name].rearrange("(k p) n -> p k n", p=P)).then_inc(s_w, 16)
                    for n, name in enumerate(("wkl_w", "wvl_w")):
                        sp.dma_start(lat[:, n], w[name].rearrange("(k p) n -> p k n", p=P)).then_inc(s_w, 16)
                    for n, name in enumerate(("upk_w", "upv_w")):
                        sp.dma_start(up[:, n].rearrange("p (h d) -> p h d", h=H),
                                     w[name].rearrange("h l d -> l h d")).then_inc(s_w, 16)
                    for n, name in enumerate(("wq_b", "wk_b", "wv_b")):
                        sp.dma_start(bcol[:, n], w[name].rearrange("(k p) -> p k", p=P)).then_inc(s_w, 16)
                    sp.dma_start(bcol[:, 3], w["upk_b"].rearrange("h d -> (h d)").rearrange("(k p) -> p k", p=P)).then_inc(s_w, 16)
                    for n, name in enumerate(("wkl_b", "wvl_b")):
                        sp.dma_start(bcol[:, 4, n:n + 1], w[name].rearrange("(p a) -> p a", a=1)).then_inc(s_w, 16)
                    sp.dma_start(vb[:], broadcast_rows(w["upv_b"], D)).then_inc(s_w, 16)

                def store(c):
                    rows = "(k p) t -> p k t"
                    sp.wait_ge(s_out, c * NP + K0)
                    sp.dma_start(scratch["qh"][c].rearrange(rows, p=P), f32(qh[:])).then_inc(s_st, 16)
                    sp.dma_start(scratch["ql"][c].rearrange(rows, p=P), f32(ql[:])).then_inc(s_st, 16)
                    sp.wait_ge(s_out, c * NP + V0)
                    sp.dma_start(scratch["kh"][c].rearrange(rows, p=P), f32(kh[:])).then_inc(s_st, 16)
                    sp.dma_start(scratch["kl"][c].rearrange(rows, p=P), f32(kl[:])).then_inc(s_st, 16)
                    sp.wait_ge(s_out, c * NP + NP)
                    sp.dma_start(scratch["v"][c].rearrange("(t p) n -> p t n", p=P), vo[:]).then_inc(s_st, 16)
                    sp.wait_ge(s_st, c * 80 + 80)
                    sp.nop().then_inc(s_free, 1)

                with sp.Fori(0, NCH) as c:
                    store(c)

            @block.gpsimd
            def _(g):
                make_identity(g, ident, s_id, 0)
                g.memset(mhalf[:], -0.5).then_inc(s_vare, 1)

                def chunk(c, first=False):
                    if not first:
                        g.wait_ge(s_xfree, c)
                    g.dma_start(xin[:], x[bass.ds(c * CH, CH), :].rearrange("(t p) n -> p t n", p=P)).then_inc(s_x, 16)
                    wait_apart(g, s_var, c * TPC + TPC, s_gpass)
                    g.tensor_scalar(vare[:], mv[:, :, 1], EPS, None, ALU.add).then_inc(s_vare, 1)
                    g.wait_ge(s_vare, c + 2)
                    g.tensor_tensor(rstd[:], vare[:], mhalf[:], ALU.pow).then_inc(s_rstd, 1)

                chunk(0, first=True)
                with g.Fori(1, NCH) as c:
                    chunk(c)

            @block.scalar
            def _(act):
                act.wait_ge(s_w, 16 * 14)
                act.activation(wqh[:], wstage[:, 0], ACT.Copy).then_inc(s_split, 1)
                act.activation(uh[:], up[:], ACT.Copy).then_inc(s_split, 1)
                for n in range(2):
                    for k in range(KD):
                        act.wait_ge(s_wt, n * KD + k + 1)
                        act.activation(wT[:, n, k], tb[k][:], ACT.Copy).then_inc(s_wc, 1)
                for n in range(2):
                    act.wait_ge(s_fold, n + 1)
                    act.activation(fh[:, n], ob[n][:].rearrange("p (k l) -> p k l", k=KD), ACT.Copy).then_inc(s_split, 1)

                def chunk(c, first=False):
                    if not first:
                        act.wait_ge(s_mm, (c - 1) * NP + K0)
                    for k in range(KD):
                        act.wait_ge(s_t, c * KD + k + 1)
                        act.activation(xh[:, k], tb[k][:], ACT.Copy).then_inc(s_xh, 1)
                    if not first:
                        act.wait_ge(s_free, c)
                    for j in range(V0):
                        act.wait_ge(s_mm, c * NP + j + 1)
                        dst, bias = (
                            (lh[:, j], bcol[:, 4, 2 + j:3 + j]) if j < Q0 else
                            (qh[:, j - Q0], bcol[:, 0, j - Q0:j - Q0 + 1]) if j < K0 else
                            (kh[:, j - K0], bcol[:, 3, j - K0:j - K0 + 1]))
                        act.activation(dst, ob[j % 4][:], ACT.Identity, bias=bias).then_inc(s_hi, 1)

                act.wait_ge(s_split, 9)
                chunk(0, first=True)
                with act.Fori(1, NCH) as c:
                    chunk(c)

            @block.vector
            def _(v):
                v.wait_ge(s_split, 2)
                v.tensor_tensor(wql[:], wstage[:, 0], f32(wqh[:]), ALU.subtract).then_inc(s_split, 1)
                v.tensor_tensor(ul[:], up[:], f32(uh[:]), ALU.subtract).then_inc(s_split, 1)

                def norm(c, first=False):
                    v.wait_ge(s_x, c * 16 + 16)
                    for t in range(TPC):
                        v.bn_stats(st[:, t], xin[:, t]).then_inc(s_stat, 1)
                    for t in range(TPC):
                        wait_apart(v, s_stat, c * TPC + t + 1, s_vpass)
                        v.bn_aggr(mv[:, t], st[:, t]).then_inc(s_var, 1)
                    v.wait_ge(s_rstd, c + 1)
                    if not first:
                        v.wait_ge(s_t, c * KD)
                    for t in range(TPC):
                        ins = v.tensor_scalar(xn[:, t], xin[:, t], mv[:, t, 0:1], rstd[:, t:t + 1], ALU.subtract, ALU.mult)
                        ins.then_inc(s_xn, 1)
                    v.wait_ge(s_xn, c * TPC + TPC)
                    v.nop().then_inc(s_xfree, 1)

                def low_x(c):
                    for k in range(KD):
                        v.wait_ge(s_xh, c * KD + k + 1)
                        v.tensor_tensor(xl[:, k], tb[k][:], f32(xh[:, k]), ALU.subtract).then_inc(s_xl, 1)

                def low(c, js):
                    for j in js:
                        if j < V0:
                            v.wait_ge(s_hi, c * V0 + j + 1)
                            dst, hi, bias = (
                                (ll[:, j], lh[:, j], bcol[:, 4, 2 + j:3 + j]) if j < Q0 else
                                (ql[:, j - Q0], qh[:, j - Q0], bcol[:, 0, j - Q0:j - Q0 + 1]) if j < K0 else
                                (kl[:, j - K0], kh[:, j - K0], bcol[:, 3, j - K0:j - K0 + 1]))
                            ins = v.scalar_tensor_tensor(out=dst, in0=ob[j % 4][:], scalar=bias, in1=f32(hi), op0=ALU.add, op1=ALU.subtract)
                        else:
                            v.wait_ge(s_mm, c * NP + j + 1)
                            ins = v.tensor_tensor(vo[:, j - V0], ob[j % 4][:], vb[:], ALU.add)
                        ins.then_inc(s_out, 1)

                for n in range(2):
                    v.wait_ge(s_split, 6)
                    v.tensor_tensor(fl[:, n], ob[n][:].rearrange("p (k l) -> p k l", k=KD), f32(fh[:, n]), ALU.subtract).then_inc(s_split, 1)
                v.wait_ge(s_fold, 3)
                v.tensor_tensor(bcol[:, 4, 2:4], ob[2][:, 0:2], bcol[:, 4, 0:2], ALU.add).then_inc(s_split, 1)
                v.wait_ge(s_split, 9)
                norm(0, first=True)
                with v.Fori(0, NCH - 1) as c:
                    low_x(c)
                    low(c, range(0, K0))
                    norm(c + 1)
                    low(c, range(K0, NP))
                low_x(NCH - 1)
                low(NCH - 1, range(NP))

            @block.tensor
            def _(pe):
                pe.wait_ge(s_id, 2)
                pe.wait_ge(s_w, 16 * 14)
                for n in range(2):
                    for k in range(KD):
                        if n:
                            pe.wait_ge(s_wc, k + 1)
                        for m in range(KD):
                            ins = pe.transpose(tb[k][:, m * P:(m + 1) * P], wstage[:, 1 + n, m, k * P:(k + 1) * P], ident[:])
                        ins.then_inc(s_wt, 1)
                pe.wait_ge(s_wc, 2 * KD)
                for n in range(2):
                    for m in range(KD):
                        for k in range(KD):
                            ins = pe.matmul(ob[n][:, m * DL:(m + 1) * DL], wT[:, n, k, m * P:(m + 1) * P], lat[:, n, k],
                                            start=(k == 0), stop=(k == KD - 1))
                    ins.then_inc(s_fold, 1)
                for n in range(2):
                    for k in range(KD):
                        ins = pe.matmul(ob[2][:, n:n + 1], lat[:, n, k], bcol[:, 1 + n, k:k + 1],
                                        start=(k == 0), stop=(k == KD - 1))
                ins.then_inc(s_fold, 1)

                def transposes(c, first=False):
                    pe.wait_ge(s_xn, c * TPC + TPC)
                    for k in range(KD):
                        if not first:
                            pe.wait_ge(s_xl, (c - 1) * KD + k + 1)
                        for t in range(TPC):
                            ins = pe.transpose(tb[k][:, t * P:(t + 1) * P], xn[:, t, k * P:(k + 1) * P], ident[:])
                        ins.then_inc(s_t, 1)

                def products(c, js, first=False):
                    for j in js:
                        if not (first and j < 4):
                            pe.wait_ge(s_out, c * NP + j - 3)
                        bank = ob[j % 4][:]
                        if j < K0:
                            if j == 0:
                                pe.wait_ge(s_xl, c * KD + KD)
                            for k in range(KD):
                                wh, wl = ((fh[:, j, k], fl[:, j, k]) if j < Q0 else
                                          (wqh[:, k, (j - Q0) * P:(j - Q0 + 1) * P], wql[:, k, (j - Q0) * P:(j - Q0 + 1) * P]))
                                ins = mm3(nc, bank, wh, wl, xh[:, k], xl[:, k], k == 0, k == KD - 1)
                        elif j < V0:
                            m = j - K0
                            ins = mm3(nc, bank, uh[:, 0, m * P:(m + 1) * P], ul[:, 0, m * P:(m + 1) * P], lh[:, 0], ll[:, 0], True, True)
                        else:
                            t = j - V0
                            ins = mm3(nc, bank, lh[:, 1, t * P:(t + 1) * P], ll[:, 1, t * P:(t + 1) * P], uh[:, 1], ul[:, 1], True, True)
                        ins.then_inc(s_mm, 1)

                pe.wait_ge(s_split, 9)
                transposes(0, first=True)
                products(0, range(K0), first=True)
                transposes(1)
                products(0, range(K0, NP))
                with pe.Fori(1, NCH - 1) as c:
                    products(c, range(K0))
                    transposes(c + 1)
                    products(c, range(K0, NP))
                products(NCH - 1, range(NP))


GPB = H // 4
NG = BATCH * GPB
PAIRS = 2
NQ = SEQ // CH
SCALE = 1.0 / DH ** 0.5


def attention_plan():
    units = [(p, q) for p in range(PAIRS) for q in range(NQ)]
    steps, first_step = [], []
    for u, (p, q) in enumerate(units):
        first_step.append(len(steps))
        steps += [(u, p, q, kt) for kt in range(TPC * (q + 1))]
    stream, pending, end = [], None, []
    for u, (p, q) in enumerate(units):
        items = [("max", u, t, h, c) for t in range(TPC) for h in range(2) for c in range(q + 1)]
        lag = min(4, len(items))
        stream += items[:lag]
        if pending is not None:
            stream.append(("turn", pending))
            end.append(len(stream))
        stream += items[lag:]
        pending = u
    stream.append(("turn", pending))
    end.append(len(stream))
    ns, ni = len(steps), len(stream)
    ahead = 3
    start = max([end[0] + 1] + [end[u] + 1 - ni * (first_step[u] - ahead) // ns for u in range(1, len(units))])
    upto = [start + ni * (n + 1) // ns for n in range(ns)]
    return units, steps, first_step, stream, start, upto, end


def over_groups(eng, group):
    group(0, True, False)
    with eng.Fori(1, NG - 1) as it:
        group(it, False, False)
    group(NG - 1, False, True)


def phase_attention(nc, scratch):
    units, steps, first_step, stream, start, upto, end = attention_plan()
    NS, NI, NU = len(steps), len(stream), len(units)
    NPB, NST, NMX, NOB, NSB = 8, 2, 2, 2, 2
    assert NS % NPB == 0 and NI % NMX == 0 and NU % NOB == 0 and NS % NST == 0
    pooled = [kt < TPC * q for _, p, q, kt in steps]
    adds = [m and kt > 0 for m, (_, p, q, kt) in zip(pooled, steps)]
    NA = sum(adds)
    added = [sum(adds[:n + 1]) + (pooled[n] and not adds[n]) for n in range(NS)]
    fin = [u for u, (p, q) in enumerate(units) if q > 0]
    NFIN = len(fin)
    assert NFIN % NSB == 0
    KR = 3 * DH
    MROW = KR
    MCOL = (MROW, 64)

    with ExitStack() as ctx:
        al = Alloc(nc, ctx)
        ident = al.sb("b_ident", [P, P])
        ones = al.sb("b_ones", [P, DH])
        qb = [al.sb(f"b_q{p}", [MROW + 1, 2, SEQ], F32R) for p in range(PAIRS)]
        kb = [al.sb(f"b_k{p}", [MROW + 1, 2, SEQ], F32R) for p in range(PAIRS)]
        vbuf = [al.sb(f"b_v{p}", [P, SEQ // P, 2 * DH]) for p in range(PAIRS)]
        pt = [al.sb(f"b_pt{n}", [P, 2, CH]) for n in range(NPB)]
        psum = [al.sb(f"b_psum{n}", [P, 2, CH]) for n in range(NSB)]
        mpart = [al.sb(f"b_mpart{n}", [P, 2, TPC, NQ]) for n in range(2)]
        mt = [al.sb(f"b_mt{n}", [P, TPC, MROW + 1]) for n in range(2)]
        ost = [al.sb(f"b_ost{n}", [P, CH]) for n in range(NOB)]
        causal = al.sb("b_causal", [P, P], mybir.dt.bfloat16)
        identb = al.sb("b_identb", [P, P], mybir.dt.bfloat16)
        stb = [al.bank(f"b_st{n}", 2 * CH) for n in range(NST)]
        mxb = [al.bank(f"b_mx{n}") for n in range(NMX)]
        ob = [al.bank(f"b_ob{n}") for n in range(NOB)]

        s_cst = al.sem("b_constants_made")
        s_rows = al.sem("b_rows_made")
        s_ld = [al.sem(f"b_pair{p}_in") for p in range(PAIRS)]
        s_item = al.sem("b_item_made")
        s_iread = al.sem("b_item_read")
        s_mcol = al.sem("b_max_columns")
        s_red = al.sem("b_partial_max")
        s_st = al.sem("b_scores_made")
        s_exp = al.sem("b_exp_made")
        s_pv = al.sem("b_step_used")
        s_add = al.sem("b_exp_added")
        s_fin = al.sem("b_added_used")
        s_oev = al.sem("b_out_read")
        s_ost = [al.sem(f"b_out_stored{n}") for n in range(NOB)]

        with nc.Block() as block:
            @block.gpsimd
            def _(g):
                make_identity(g, ident, s_cst, 0)
                g.memset(causal[:], 0.0).then_inc(s_cst, 1)
                g.wait_ge(s_cst, 3)
                g.affine_select(out=causal[:], in_=causal[:], compare_op=ALU.is_ge, fill=-1e30, base=0,
                                pattern=[[-1, P]], channel_multiplier=1).then_inc(s_cst, 1)
                g.memset(identb[:], 0.0).then_inc(s_cst, 1)
                g.wait_ge(s_cst, 5)
                g.affine_select(out=identb[:], in_=identb[:], compare_op=ALU.not_equal, fill=1.0, base=0,
                                pattern=[[-1, P]], channel_multiplier=1).then_inc(s_cst, 1)
                g.memset(ones[:], 1.0).then_inc(s_cst, 1)

                def add(it, n, first):
                    u, kt = steps[n][0], steps[n][3]
                    f = fin.index(u)
                    so_far = psum[f % NSB][:] if kt > 1 else pt[(n - 1) % NPB][:]
                    if kt == 1 and (not first or f >= NSB):
                        g.wait_ge(s_fin, it * NFIN + f - NSB + 1)
                    if kt > 1:
                        g.wait_ge(s_add, it * NA + added[n] - 1)
                    g.wait_ge(s_exp, it * NS + n + 1)
                    g.tensor_tensor(psum[f % NSB][:], so_far, pt[n % NPB][:], ALU.add).then_inc(s_add, 1)

                def group(it, first, last):
                    for n in range(NS):
                        if adds[n]:
                            add(it, n, first)

                over_groups(g, group)

            NCST = 7
            LD = 13 * 16
            STO = NU // NOB * 48

            @block.sync
            def _(sp):
                def load(it, p, first=False):
                    if not first:
                        sp.wait_ge(s_pv, (it - 1) * NS + (p + 1) * NS // PAIRS)
                    b, g = (it // GPB, it % GPB) if not first else (0, 0)
                    if not first:
                        b, g = sp.snap(b), sp.snap(g)
                    for h in range(2):
                        row = g * P + p * 2 * DH + h * DH
                        for buf, parts in ((qb[p], ("qh", "ql", "qh")), (kb[p], ("kh", "kh", "kl"))):
                            for n, name in enumerate(parts):
                                dst = f32(buf[n * DH:(n + 1) * DH, h]).rearrange("d (c t) -> d c t", c=CPB)
                                src = scratch[name][bass.ds(b * CPB, CPB), bass.ds(row, DH), :].rearrange("c d t -> d c t")
                                sp.dma_start(dst, src).then_inc(s_ld[p], 16)
                    src = scratch["v"][bass.ds(b * CPB, CPB), :, bass.ds(g * P + p * 2 * DH, 2 * DH)]
                    sp.dma_start(vbuf[p][:], src.rearrange("c (t k) d -> k (c t) d", k=P)).then_inc(s_ld[p], 16)

                for p in range(PAIRS):
                    load(0, p, first=True)
                with sp.Fori(1, NG) as it:
                    for p in range(PAIRS):
                        load(it, p)
                for sem in s_ost:
                    sp.wait_ge(sem, NG * STO)


            @block.vector
            def _(v):
                def item(it, i, what):
                    bank = mxb[i % NMX]
                    v.wait_ge(s_item, it * NI + i + 1)
                    if what[0] == "max":
                        _, u, t, h, c = what
                        n = (TPC * units[u][1] + t + 1) * P
                        w = min(CH, n - c * CH)
                        w = 2 * P if w == P and n > P else w
                        v.tensor_reduce(mpart[u % 2][:, h, t, c:c + 1], bank[:, 0:w], AX.X, ALU.max).then_inc(s_iread, 1)
                        if (t, h, c) == (TPC - 1, 1, units[u][1]):
                            done = sum(x[0] == "max" for x in stream[:i + 1]) + sum(x[0] == "turn" for x in stream[:i + 1])
                            v.wait_ge(s_iread, it * NI + done)
                            for hh in range(2):
                                v.tensor_reduce(mt[u % 2][:, :, MCOL[hh]], mpart[u % 2][:, hh, :, 0:units[u][1] + 1],
                                                AX.X, ALU.max, negate=True).then_inc(s_mcol, 1)
                    else:
                        u = what[1]
                        p, q = units[u]
                        for h in range(2):
                            ins = v.tensor_copy(qb[p][MROW:MROW + 1, h, q * CH:(q + 1) * CH], bank[MCOL[h]:MCOL[h] + 1, :])
                        ins.then_inc(s_iread, 1)

                for p in range(PAIRS):
                    v.memset(f32(kb[p][MROW:MROW + 1]), 1.0).then_inc(s_rows, 1)
                for n in range(2):
                    v.memset(mt[n][:], 0.0).then_inc(s_rows, 1)
                v.wait_ge(s_rows, 4)
                for i in range(start):
                    item(0, i, stream[i])
                with v.Fori(0, NG - 1) as it:
                    for i in range(start, NI):
                        item(it, i, stream[i])
                    for i in range(start):
                        item(it + 1, i, stream[i])
                for i in range(start, NI):
                    item(NG - 1, i, stream[i])

            @block.scalar
            def _(act):
                def exps(it, n, first):
                    u, p, q, kt = steps[n]
                    lo = max(kt - TPC * q, 0) * P
                    act.wait_ge(s_st, it * NS + n + 1)
                    before = n - NPB
                    if before >= 0 or not first:
                        act.wait_ge(s_pv, it * NS + before + 1)
                        if pooled[before]:
                            act.wait_ge(s_add, it * NA + added[before] - (NA if before < 0 else 0))
                    act.activation(pt[n % NPB][:, :, lo:], stb[n % NST][:].rearrange("k (h q) -> k h q", h=2)[:, :, lo:],
                                   ACT.Exp, scale=SCALE).then_inc(s_exp, 1)

                def evacuate(it, u, first):
                    if u in fin:
                        act.wait_ge(s_fin, it * NFIN + fin.index(u) + 1)
                    else:
                        act.wait_ge(s_pv, it * NS + (first_step + [NS])[u + 1])
                    if u >= NOB or not first:
                        act.wait_ge(s_ost[u % NOB], it * STO + u // NOB * 48)
                    act.activation(ost[u % NOB][:], ob[u % NOB][:], ACT.Copy).then_inc(s_oev, 1)

                def store(it, b, g, u):
                    p, q = units[u]
                    act.wait_ge(s_oev, it * NU + u + 1)
                    st, chunk = ost[u % NOB], b * CPB + q
                    act.dma_start(scratch["oT"][bass.ds(chunk, 1), bass.ds(g * P + p * 2 * DH, 2 * DH), :].rearrange("c d t -> (c d) t"),
                                  st[0:2 * DH, :]).then_inc(s_ost[u % NOB], 16)
                    for h in range(2):
                        act.dma_start(scratch["sums"][bass.ds(chunk, 1), bass.ds(g * 4 + p * 2 + h, 1), :].rearrange("c d t -> (c d) t"),
                                      st[2 * DH + h * DH:2 * DH + h * DH + 1, :]).then_inc(s_ost[u % NOB], 16)

                def place(it):
                    return (it // GPB, it % GPB) if isinstance(it, int) else (act.snap(it // GPB), act.snap(it % GPB))

                def group(it, first, last):
                    b, g = place(it)
                    if not first:
                        before = it - 1
                        bb, gg = place(before)
                    for n, (u, p, q, kt) in enumerate(steps):
                        exps(it, n, first)
                        if kt == 3 and u:
                            evacuate(it, u - 1, first)
                        if kt == 3 and not u and not first:
                            evacuate(before, NU - 1, False)
                        if n and steps[n - 1][3] == 3:
                            made = steps[n - 1][0] - 1
                            if made >= 0:
                                store(it, b, g, made)
                            elif not first:
                                store(before, bb, gg, NU - 1)
                    if last:
                        evacuate(it, NU - 1, False)
                        store(it, b, g, NU - 1)

                over_groups(act, group)
                for sem in s_ost:
                    act.wait_ge(sem, NG * STO)

            @block.tensor
            def _(pe):
                def item(it, i, first):
                    what = stream[i]
                    bank = mxb[i % NMX]
                    if i >= NMX or not first:
                        pe.wait_ge(s_iread, it * NI + i - NMX + 1)
                    if what[0] == "max":
                        _, u, t, h, c = what
                        p, q = units[u]
                        tile = TPC * q + t
                        n = (tile + 1) * P
                        w = min(CH, n - c * CH)
                        lo = c * CH
                        if w == P and n > P:
                            lo, w = lo - P, 2 * P
                        if (t, h, c) == (0, 0, 0):
                            pe.wait_ge(s_ld[p], it * LD + LD)
                        diag = lo + w == n
                        ins = pe.matmul(bank[:, 0:w], qb[p][0:KR, h, tile * P:(tile + 1) * P], kb[p][0:KR, h, lo:lo + w],
                                        start=True, stop=not diag)
                        if diag:
                            ins = pe.matmul(bank[:, w - P:w], identb[:], causal[:], start=False, stop=True)
                        ins.then_inc(s_item, 1)
                    else:
                        u = what[1]
                        pe.wait_ge(s_mcol, it * 2 * NU + 2 * u + 2)
                        for t in range(TPC):
                            ins = pe.transpose(bank[0:MROW + 1, t * P:(t + 1) * P], mt[u % 2][:, t, :], ident[:])
                        ins.then_inc(s_item, 1)

                def scores(it, n, first):
                    u, p, q, kt = steps[n]
                    d = kt - TPC * q
                    lo = min(max(d, 0) * P, 2 * P)
                    if n >= NST or not first:
                        pe.wait_ge(s_exp, it * NS + n - NST + 1)
                    if kt == 0:
                        pe.wait_ge(s_iread, it * NI + end[u])
                    for h in range(2):
                        ins = pe.matmul(stb[n % NST][:, h * CH + lo:(h + 1) * CH], kb[p][:, h, kt * P:(kt + 1) * P],
                                        qb[p][:, h, q * CH + lo:(q + 1) * CH], start=True, stop=d < 0)
                        if d >= 0:
                            ins = pe.matmul(stb[n % NST][:, h * CH + d * P:h * CH + (d + 1) * P], causal[:], identb[:],
                                            start=False, stop=True)
                    ins.then_inc(s_st, 1)

                def values(it, n, first):
                    u, p, q, kt = steps[n]
                    d = kt - TPC * q
                    lo = max(d, 0) * P
                    pe.wait_ge(s_exp, it * NS + n + 1)
                    if kt == 0 and (u >= NOB or not first):
                        pe.wait_ge(s_oev, it * NU + u - NOB + 1)
                    for j in range(2):
                        ins = pe.matmul(ob[u % NOB][j * DH:(j + 1) * DH, lo:], vbuf[p][:, kt, j * DH:(j + 1) * DH],
                                        pt[n % NPB][:, j, lo:], start=(kt == 0), stop=(d == TPC - 1))
                    if d >= 0:
                        for j in range(2):
                            ins = pe.matmul(ob[u % NOB][(2 + j) * DH:(3 + j) * DH, lo:], ones[:], pt[n % NPB][:, j, lo:],
                                            start=(d == 0), stop=(d == TPC - 1 and u not in fin))
                    ins.then_inc(s_pv, 1)

                def finish(it, u):
                    f = fin.index(u)
                    pe.wait_ge(s_add, it * NA + added[first_step[u] + TPC * units[u][1] - 1])
                    for j in range(2):
                        ins = pe.matmul(ob[u % NOB][(2 + j) * DH:(3 + j) * DH, :], ones[:], psum[f % NSB][:, j],
                                        start=False, stop=True)
                    ins.then_inc(s_fin, 1)

                pe.wait_ge(s_cst, NCST)
                pe.wait_ge(s_rows, 4)
                for i in range(start):
                    item(0, i, True)

                def group(it, first, last):
                    done = start

                    def items(upto):
                        nonlocal done
                        for i in range(done, upto):
                            if i < NI:
                                item(it, i, first)
                            elif not last:
                                item(it + 1, i - NI, False)
                        done = max(done, upto)

                    for n in range(NS):
                        scores(it, n, first)
                        items((done + upto[n] + 1) // 2)
                        if n:
                            values(it, n - 1, first)
                            u, kt = steps[n - 1][0], steps[n - 1][3]
                            if kt == 2 and u - 1 in fin:
                                finish(it, u - 1)
                            if kt == 2 and u == 0 and not first:
                                finish(it - 1, NU - 1)
                        elif not first:
                            values(it - 1, NS - 1, False)
                        items(upto[n])
                    if last:
                        values(it, NS - 1, False)
                        finish(it, NU - 1)

                over_groups(pe, group)


E = 8
F = 352
FS = [(0, P), (P, P), (2 * P, F - 2 * P)]
NF = len(FS)
NT = T // P


class FfnWeights:

    def __init__(self, al, name, raw=None):
        if raw is None:
            raw = (al.sb(f"{name}_gu", [P, 2, KD, F]), al.sb(f"{name}_d", [P, NF, D]))
        self.gu, self.d = raw
        self.guh, self.gul = al.sb(f"{name}_guh", [P, 2, KD, F], F32R), al.sb(f"{name}_gul", [P, 2, KD, F], F32R)
        self.dh, self.dl = al.sb(f"{name}_dh", [P, NF, D], F32R), al.sb(f"{name}_dl", [P, NF, D], F32R)

    def down_parts(self):
        w = FS[-1][1]
        return [(self.d[:, 0:NF - 1], self.dh[:, 0:NF - 1], self.dl[:, 0:NF - 1]),
                (self.d[0:w, NF - 1], self.dh[0:w, NF - 1], self.dl[0:w, NF - 1])]


def load_ffn(dma, wt, gate, up, down, sem):
    dma(wt.gu[:, 0], gate.rearrange("(k p) f -> p k f", p=P)).then_inc(sem, 16)
    dma(wt.gu[:, 1], up.rearrange("(k p) f -> p k f", p=P)).then_inc(sem, 16)
    dma(wt.d[:, 0:NF - 1], down[0:(NF - 1) * P].rearrange("(k p) n -> p k n", p=P)).then_inc(sem, 16)
    dma(wt.d[0:FS[-1][1], NF - 1], down[(NF - 1) * P:F]).then_inc(sem, 16)


def gate_up(nc, bank, wt, which, f, xh, xl):
    lo, w = FS[f]
    for k in range(KD):
        ins = mm3(nc, bank[0:w, :], wt.guh[:, which, k, lo:lo + w], wt.gul[:, which, k, lo:lo + w],
                  xh[:, k], xl[:, k], k == 0, k == KD - 1)
    return ins


def down(nc, bank, wt, hh, hl, t, slices=range(NF)):
    for f in slices:
        w = FS[f][1]
        ins = mm3(nc, bank, hh[0:w, f, t * P:(t + 1) * P], hl[0:w, f, t * P:(t + 1) * P],
                  wt.dh[0:w, f], wt.dl[0:w, f], f == 0, f == NF - 1)
    return ins


def phase_shared(nc, x, w, scratch):
    with ExitStack() as ctx:
        al = Alloc(nc, ctx)
        ident = al.sb("c_ident", [P, P])
        mhalf = al.sb("c_mhalf", [P, TPC])
        wob = al.sb("c_wob", [P, D])
        wos = al.sb("c_wo", [P, KD, D])
        woh, wol = al.sb("c_woh", [P, KD, D], F32R), al.sb("c_wol", [P, KD, D], F32R)
        gw = al.sb("c_gw", [P, KD, E])
        gwh, gwl = al.sb("c_gwh", [P, KD, E], F32R), al.sb("c_gwl", [P, KD, E], F32R)
        wt = FfnWeights(al, "c_sw")
        sums = al.sb("c_sums", [P, CH])
        rsum = al.sb("c_rsum", [P, CH])
        oin = al.sb("c_oin", [P, KD, CH])
        rin = al.sb("c_rin", [P, KD, CH])
        xin = al.sb("c_xin", [P, TPC, D])
        on = oin
        oh, ol = al.sb("c_oh", [P, KD, CH], F32R), al.sb("c_ol", [P, KD, CH], F32R)
        xw = rin[:].rearrange("p k n -> p (k n)").rearrange("p (t n) -> p t n", t=TPC)
        x1 = al.sb("c_x1", [P, TPC, D])
        x1k = al.sb("c_x1k", [P, TPC, D])
        xn = al.sb("c_xn", [P, TPC, D])
        st, mv = al.sb("c_stats", [P, TPC, 6]), al.sb("c_mv", [P, TPC, 2])
        vare, rstd = al.sb("c_vare", [P, TPC]), al.sb("c_rstd", [P, TPC])
        xh, xl = al.sb("c_xh", [P, KD, CH], F32R), al.sb("c_xl", [P, KD, CH], F32R)
        sg = al.sb("c_sg", [P, NF, CH])
        hf = al.sb("c_hf", [P, NF, CH])
        hh, hl = al.sb("c_hh", [P, NF, CH], F32R), al.sb("c_hl", [P, NF, CH], F32R)
        acc = al.sb("c_acc", [P, TPC, D])
        lgT = al.sb("c_lgT", [E, CH])
        lg = al.sb("c_lg", [P, TPC, E])
        ab = [al.bank(f"c_ab{n}") for n in range(2)]
        lb = al.bank("c_lb")
        fb = [al.bank(f"c_fb{n}") for n in range(5)]

        s_w = al.sem("c_weights_in")
        s_vpass, s_gpass, s_ppass = al.sem("c_vector_passed"), al.sem("c_pool_passed"), al.sem("c_tensor_passed")
        s_cst = al.sem("c_constants_made")
        s_wh = al.sem("c_weights_high")
        s_wl = al.sem("c_weights_low")
        s_sum = al.sem("c_sums_in")
        s_rs = al.sem("c_reciprocals_made")
        s_rst = al.sem("c_reciprocals_stored")
        s_o = al.sem("c_attention_in")
        s_x = al.sem("c_x_in")
        s_on = al.sem("c_o_normalized")
        s_xw = al.sem("c_xw_made")
        s_oh = al.sem("c_oh_made")
        s_ol = al.sem("c_ol_made")
        s_at = al.sem("c_att_made")
        s_x1 = al.sem("c_x1_made")
        s_x1k = al.sem("c_x1_kept")
        s_stat = al.sem("c_stats_made")
        s_var = al.sem("c_var_made")
        s_vare = al.sem("c_vare_made")
        s_rstd = al.sem("c_rstd_made")
        s_xn = al.sem("c_xn_made")
        s_t = al.sem("c_transposed")
        s_xh = al.sem("c_xh_made")
        s_xl = al.sem("c_xl_made")
        s_lt = al.sem("c_logits_made")
        s_ltc = al.sem("c_logits_copied")
        s_gu = al.sem("c_gate_up_made")
        s_sg = al.sem("c_silu_made")
        s_h = al.sem("c_h_made")
        s_hh = al.sem("c_hh_made")
        s_hl = al.sem("c_hl_made")
        s_dn = al.sem("c_down_made")
        s_acc = al.sem("c_acc_made")
        s_xst = al.sem("c_xn_stored")
        s_ast = al.sem("c_acc_stored")
        s_lst = al.sem("c_logits_stored")

        with nc.Block() as block:
            @block.sync
            def _(sp):
                sp.dma_start(sums[:], scratch["sums"].rearrange("c h t -> (c h) t")).then_inc(s_sum, 16)
                sp.dma_start(wos[:], w["wo_w"].rearrange("(k p) n -> p k n", p=P)).then_inc(s_w, 16)
                sp.dma_start(wob[:], broadcast_rows(w["wo_b"], D)).then_inc(s_w, 16)
                with nc.allow_non_contiguous_dma(reason="router weights as columns"):
                    for k in range(KD):
                        sp.dma_start(gw[:, k], w["gate_w"][:, k * P:(k + 1) * P].rearrange("e p -> p e")).then_inc(s_w, 16)
                load_ffn(sp.dma_start, wt, w["sw_gate"], w["sw_up"], w["sw_down"], s_w)
                sp.wait_ge(s_rs, 1)
                sp.dma_start(scratch["rsum"].rearrange("c h t -> (c h) t"), rsum[:]).then_inc(s_rst, 16)
                sp.wait_ge(s_rst, 16)

                def load(c, first=False):
                    if not first:
                        sp.wait_ge(s_ol, c)
                    sp.dma_start(oin[:], scratch["oT"][bass.ds(c, 1)].rearrange("c (k p) t -> p (c k) t", p=P)).then_inc(s_o, 16)
                    if not first:
                        sp.wait_ge(s_x1, c * TPC)
                    for j in range(H // KD):
                        src = scratch["rsum"][bass.ds(c, 1), bass.ds(j, 1), :]
                        src = bass.AP(src.tensor, src.offset, [[0, DH], [H // KD * CH, KD], [1, CH]])
                        sp.dma_start(rin[j * DH:(j + 1) * DH], src).then_inc(s_o, 16)
                    sp.dma_start(xin[:], x[bass.ds(c * CH, CH), :].rearrange("(t p) n -> p t n", p=P)).then_inc(s_x, 16)

                def store_rows(c):
                    sp.wait_ge(s_xn, c * TPC + TPC)
                    sp.dma_start(scratch["xn"][bass.ds(c * CH, CH), :].rearrange("(t p) n -> p t n", p=P), xn[:]).then_inc(s_xst, 16)

                def store_acc(c):
                    sp.wait_ge(s_acc, c * TPC + TPC)
                    sp.dma_start(scratch["acc"][bass.ds(c * CH, CH), :].rearrange("(t p) n -> p t n", p=P), acc[:]).then_inc(s_ast, 16)

                def store_logits(c):
                    sp.wait_ge(s_ltc, c * 2 + 2)
                    sp.dma_start(scratch["logits"][:, bass.ds(c * TPC, TPC), :], lg[:]).then_inc(s_lst, 16)

                def step(c, last=False):
                    store_logits(c)
                    if not last:
                        load(c + 2)
                    store_rows(c + 1)
                    store_acc(c)

                load(0, first=True)
                load(1)
                store_rows(0)
                with sp.Fori(0, NCH - 2) as c:
                    step(c)
                step(NCH - 2, last=True)
                store_logits(NCH - 1)
                store_acc(NCH - 1)
                for sem in (s_xst, s_ast, s_lst):
                    sp.wait_ge(sem, NCH * 16)

            @block.gpsimd
            def _(g):
                make_identity(g, ident, s_cst, 0)
                g.memset(mhalf[:], -0.5).then_inc(s_cst, 1)

                def ahead(c, first=False):
                    g.wait_ge(s_o, c * 80 + 80)
                    g.tensor_tensor(on[:], oin[:], rin[:], ALU.mult).then_inc(s_on, 1)
                    g.wait_ge(s_x, c * 16 + 16)
                    g.wait_ge(s_on, c + 1)
                    for t in range(TPC):
                        ins = g.tensor_tensor(xw[:, t], xin[:, t], wob[:], ALU.add)
                    ins.then_inc(s_xw, 1)
                    wait_apart(g, s_var, c * TPC + TPC, s_gpass)
                    g.tensor_scalar(vare[:], mv[:, :, 1], EPS, None, ALU.add).then_inc(s_vare, 1)
                    g.wait_ge(s_vare, c + 1)
                    g.tensor_tensor(rstd[:], vare[:], mhalf[:], ALU.pow).then_inc(s_rstd, 1)

                g.wait_ge(s_cst, 3)
                g.wait_ge(s_w, 16 * 10)
                with g.Fori(0, NCH) as c:
                    ahead(c)

            @block.scalar
            def _(act):
                act.wait_ge(s_w, 16 * 10)
                act.activation(woh[:], wos[:], ACT.Copy).then_inc(s_wh, 1)
                act.activation(gwh[:], gw[:], ACT.Copy).then_inc(s_wh, 1)
                act.activation(wt.guh[:], wt.gu[:], ACT.Copy).then_inc(s_wh, 1)
                for raw, hi, lo in wt.down_parts():
                    act.activation(hi, raw, ACT.Copy).then_inc(s_wh, 1)

                def o_high(c, first=False):
                    act.wait_ge(s_on, c + 1)
                    if not first:
                        act.wait_ge(s_at, c * TPC)
                    act.activation(oh[:], on[:], ACT.Copy).then_inc(s_oh, 1)

                def hidden(c, f, first=False):
                    w = FS[f][1]
                    act.wait_ge(s_gu, (c * NF + f) * 2 + 2)
                    if not first:
                        act.wait_ge(s_h, (c - 1) * NF + f + 1)
                    act.activation(sg[0:w, f], fb[2 * f % 5][0:w, :], ACT.Silu).then_inc(s_sg, 1)
                    act.wait_ge(s_h, c * NF + f + 1)
                    if not first:
                        act.wait_ge(s_dn, c * TPC)
                    act.activation(hh[0:w, f], hf[0:w, f], ACT.Copy).then_inc(s_hh, 1)

                def x_high(c):
                    for k in range(KD):
                        act.wait_ge(s_t, c * KD + k + 1)
                        act.activation(xh[:, k], ab[k % 2][:], ACT.Copy).then_inc(s_xh, 1)

                def keep(c, first=False):
                    if not first:
                        act.wait_ge(s_acc, c * TPC)
                    act.wait_ge(s_x1, c * TPC + TPC)
                    act.activation(x1k[:], x1[:], ACT.Copy).then_inc(s_x1k, 1)

                o_high(0, first=True)
                x_high(0)
                keep(0, first=True)

                def step(c, first=False, last=False):
                    if not last:
                        o_high(c + 1)
                    for f in range(NF):
                        hidden(c, f, first)
                    if not last:
                        x_high(c + 1)
                        keep(c + 1)

                step(0, first=True)
                with act.Fori(1, NCH - 1) as c:
                    step(c)
                step(NCH - 1, last=True)

            @block.vector
            def _(v):
                v.wait_ge(s_sum, 16)
                v.reciprocal(rsum[:], sums[:]).then_inc(s_rs, 1)
                v.wait_ge(s_wh, 5)
                v.tensor_tensor(wol[:], wos[:], f32(woh[:]), ALU.subtract).then_inc(s_wl, 1)
                v.tensor_tensor(gwl[:], gw[:], f32(gwh[:]), ALU.subtract).then_inc(s_wl, 1)
                v.tensor_tensor(wt.gul[:], wt.gu[:], f32(wt.guh[:]), ALU.subtract).then_inc(s_wl, 1)
                for raw, hi, lo in wt.down_parts():
                    v.tensor_tensor(lo, raw, f32(hi), ALU.subtract).then_inc(s_wl, 1)

                def o_low(c, first=False):
                    v.wait_ge(s_oh, c + 1)
                    v.tensor_tensor(ol[:], on[:], f32(oh[:]), ALU.subtract).then_inc(s_ol, 1)

                def residual(c, first=False):
                    v.wait_ge(s_xw, c + 1)
                    if not first:
                        v.wait_ge(s_x1k, c)
                    for t in range(TPC):
                        v.wait_ge(s_at, c * TPC + t + 1)
                        v.tensor_tensor(x1[:, t], ab[t % 2][:], xw[:, t], ALU.add).then_inc(s_x1, 1)
                        v.wait_ge(s_x1, c * TPC + t + 1)
                        v.bn_stats(st[:, t], x1[:, t]).then_inc(s_stat, 1)
                    for t in range(TPC):
                        wait_apart(v, s_stat, c * TPC + t + 1, s_vpass)
                        v.bn_aggr(mv[:, t], st[:, t]).then_inc(s_var, 1)

                def norm(c, first=False):
                    v.wait_ge(s_rstd, c + 1)
                    v.wait_ge(s_var, c * TPC + TPC)
                    if not first:
                        v.wait_ge(s_xst, c * 16)
                        v.wait_ge(s_t, c * KD)
                    for t in range(TPC):
                        v.tensor_scalar(xn[:, t], x1[:, t], mv[:, t, 0:1], rstd[:, t:t + 1], ALU.subtract, ALU.mult).then_inc(s_xn, 1)

                def x_low(c, ks):
                    for k in ks:
                        v.wait_ge(s_xh, c * KD + k + 1)
                        v.tensor_tensor(xl[:, k], ab[k % 2][:], f32(xh[:, k]), ALU.subtract).then_inc(s_xl, 1)

                def expert_rows(c):
                    v.wait_ge(s_lt, c * 2 + 1)
                    v.tensor_copy(lgT[:], lb[0:E, :]).then_inc(s_ltc, 1)

                def token_rows(c, first=False):
                    v.wait_ge(s_lt, c * 2 + 2)
                    if not first:
                        v.wait_ge(s_lst, c * 16)
                    v.tensor_copy(lg[:], lb[:, 0:TPC * E].rearrange("p (t e) -> p t e", t=TPC)).then_inc(s_ltc, 1)

                def hidden(c, f, first=False):
                    w = FS[f][1]
                    v.wait_ge(s_sg, c * NF + f + 1)
                    if not first:
                        v.wait_ge(s_hl, (c - 1) * NF + f + 1)
                    v.tensor_tensor(hf[0:w, f], sg[0:w, f], fb[(2 * f + 1) % 5][0:w, :], ALU.mult).then_inc(s_h, 1)
                    v.wait_ge(s_hh, c * NF + f + 1)
                    v.tensor_tensor(hl[0:w, f], hf[0:w, f], f32(hh[0:w, f]), ALU.subtract).then_inc(s_hl, 1)

                def add_shared(c, ts, first=False):
                    v.wait_ge(s_x1k, c + 1)
                    if not first:
                        v.wait_ge(s_ast, c * 16)
                    for t in ts:
                        v.wait_ge(s_dn, c * TPC + t + 1)
                        v.tensor_tensor(acc[:, t], fb[(2 * NF + t) % 5][:], x1k[:, t], ALU.add).then_inc(s_acc, 1)

                o_low(0, first=True)
                residual(0, first=True)
                norm(0, first=True)
                x_low(0, range(KD))

                def step(c, first=False, last=False):
                    hidden(c, 0, first)
                    expert_rows(c)
                    if not last:
                        o_low(c + 1)
                    hidden(c, 1, first)
                    token_rows(c, first)
                    if not last:
                        residual(c + 1)
                        norm(c + 1)
                    hidden(c, NF - 1, first)
                    for half in (range(0, 2), range(2, 4)):
                        if not last:
                            x_low(c + 1, half)
                        add_shared(c, half, first)

                step(0, first=True)
                with v.Fori(1, NCH - 1) as c:
                    step(c)
                step(NCH - 1, last=True)

            @block.tensor
            def _(pe):
                NFB = 2 * NF + TPC

                def att(c, first=False):
                    pe.wait_ge(s_ol, c + 1)
                    for t in range(TPC):
                        if t >= 2:
                            pe.wait_ge(s_x1, c * TPC + t - 1)
                        elif not first:
                            pe.wait_ge(s_xl, c * KD - 1 + t)
                        for k in range(KD):
                            ins = mm3(nc, ab[t % 2][:], oh[:, k, t * P:(t + 1) * P], ol[:, k, t * P:(t + 1) * P],
                                      woh[:, k], wol[:, k], k == 0, k == KD - 1)
                        ins.then_inc(s_at, 1)

                def transposes(c, ks):
                    pe.wait_ge(s_xn, c * TPC + TPC)
                    for k in ks:
                        if k >= 2:
                            pe.wait_ge(s_xl, c * KD + k - 1)
                        for t in range(TPC):
                            ins = pe.transpose(ab[k % 2][:, t * P:(t + 1) * P], xn[:, t, k * P:(k + 1) * P], ident[:])
                        ins.then_inc(s_t, 1)

                def logits(c, first=False):
                    if not first:
                        pe.wait_ge(s_ltc, c * 2)
                    for k in range(KD):
                        ins = mm3(nc, lb[0:E, :], gwh[:, k], gwl[:, k], xh[:, k], xl[:, k], k == 0, k == KD - 1)
                    ins.then_inc(s_lt, 1)

                def turn_logits(c):
                    wait_apart(pe, s_ltc, c * 2 + 1, s_ppass)
                    for t in range(TPC):
                        ins = pe.transpose(lb[:, t * E:(t + 1) * E], lgT[:, t * P:(t + 1) * P], ident[0:E, 0:E])
                    ins.then_inc(s_lt, 1)

                def hidden(c, f, first=False):
                    for which in range(2):
                        n = 2 * f + which
                        if n >= 5:
                            pe.wait_ge(s_sg, c * NF + (n - 5) // 2 + 1)
                        elif n and not first:
                            pe.wait_ge(s_acc, (c - 1) * TPC + n)
                        elif not first:
                            pe.wait_ge(s_h, c * NF)
                        gate_up(nc, fb[n % 5][:], wt, which, f, xh, xl).then_inc(s_gu, 1)

                def down_rows(c, ts, slices):
                    pe.wait_ge(s_hl, c * NF + slices[-1] + 1)
                    for t in ts:
                        if t == TPC - 1:
                            pe.wait_ge(s_sg, c * NF + NF)
                        ins = down(nc, fb[(2 * NF + t) % 5][:], wt, hh, hl, t, slices)
                        if slices[-1] == NF - 1:
                            ins.then_inc(s_dn, 1)

                pe.wait_ge(s_cst, 3)
                pe.wait_ge(s_wl, 5)
                att(0, first=True)
                transposes(0, range(KD))
                pe.wait_ge(s_xl, KD)

                def step(c, first=False, last=False):
                    if not first:
                        pe.wait_ge(s_xl, c * KD + KD)
                    hidden(c, 0, first)
                    logits(c, first)
                    hidden(c, 1, first)
                    turn_logits(c)
                    if not last:
                        att(c + 1)
                    hidden(c, NF - 1, first)
                    down_rows(c, range(TPC), [0, 1])
                    for half in (range(0, 2), range(2, 4)):
                        if not last:
                            transposes(c + 1, half)
                        down_rows(c, half, [NF - 1])

                step(0, first=True)
                with pe.Fori(1, NCH - 1) as c:
                    step(c)
                step(NCH - 1, last=True)


SLOTS = 512
NB = (2 * T + E * (SLOTS - 1)) // SLOTS
TPB = SLOTS // P


def phase_route(nc, keep, scratch):
    with ExitStack() as ctx:
        al = Alloc(nc, ctx)
        ident = al.sb("d_ident", [P, P])
        ones = al.sb("d_ones", [P, P])
        before = al.sb("d_before", [P, P])
        rank = al.sb("d_rank", [P, NT, E])
        steps = al.sb("d_steps", [P, E, T // SLOTS])
        blk = al.sb("d_blk", [P, NB, E])
        tok = al.sb("d_tok", [P, NT])
        zero = al.sb("d_zero", [NB * TPB, P])
        lg = al.sb("d_lg", [P, NT, E])
        a, b2 = al.sb("d_a", [P, NT, E]), al.sb("d_b", [P, NT, E])
        oh = [al.sb(f"d_oh{n}", [P, NT, E]) for n in range(2)]
        m = [al.sb(f"d_m{n}", [P, NT]) for n in range(2)]
        r = al.sb("d_r", [P, NT])
        both = al.sb("d_both", [P, NT, E])
        tot, cum = al.sb("d_tot", [P, NT, E]), al.sb("d_cum", [P, NT, E])
        cmp1 = al.sb("d_cmp1", [P, E, T // SLOTS])
        cmp2 = al.sb("d_cmp2", [P, NB, E])
        nb, endb, startb = al.sb("d_nb", [P, E]), al.sb("d_endb", [P, E]), al.sb("d_startb", [P, E])
        ebf = al.sb("d_ebf", [P, NB])
        slotf = [al.sb(f"d_slotf{n}", [P, NT]) for n in range(2)]
        ex = al.sb("d_ex", [P, NT])
        den = al.sb("d_den", [P, NT])
        ids = al.sb("d_ids", [NB * TPB, P])
        pre, tob = al.bank("d_pre"), al.bank("d_totals")
        idb = al.bank("d_idb")

        s_in = al.sem("d_logits_in")
        s_cst = al.sem("d_constants_made")
        s_v = al.sem("d_vector_step")
        s_mm = al.sem("d_counts_made")
        s_ex = al.sem("d_exp_made")
        s_z = al.sem("d_ids_cleared")
        s_sc = al.sem("d_ids_scattered")
        s_id = al.sem("d_ids_in")
        s_it = al.sem("d_ids_turned")
        marks = {}

        with nc.Block() as block:
            @block.vector
            def _(v):
                done = [0]

                def step(ins, mark=None):
                    done[0] += 1
                    ins.then_inc(s_v, 1)
                    v.wait_ge(s_v, done[0])
                    if mark:
                        marks[mark] = done[0]

                def over(ap, n, axis):
                    return ap.unsqueeze(axis).to_broadcast([P, n, E] if axis == 1 else [P, ap.shape[1], n])

                v.wait_ge(s_cst, 10)
                v.wait_ge(s_in, 16)
                src = lg
                for n in range(2):
                    step(v.tensor_reduce(m[n][:], src[:], AX.X, ALU.max), "max2" if n else None)
                    step(v.tensor_tensor(a[:], src[:], over(m[n][:], E, 2), ALU.is_equal))
                    step(v.tensor_tensor(b2[:], a[:], rank[:], ALU.mult))
                    step(v.tensor_reduce(r[:], b2[:], AX.X, ALU.max))
                    step(v.tensor_tensor(oh[n][:], b2[:], over(r[:], E, 2), ALU.is_equal))
                    if n == 0:
                        step(v.scalar_tensor_tensor(out=both[:], in0=oh[0][:], scalar=-3e38, in1=lg[:], op0=ALU.mult, op1=ALU.add))
                        src = both
                step(v.tensor_tensor(both[:], oh[0][:], oh[1][:], ALU.add), "both")
                step(v.tensor_tensor(ex[:], m[1][:], m[0][:], ALU.subtract), "gap")
                v.wait_ge(s_mm, 1)
                step(v.tensor_copy(tot[:], tob[:, 0:NT * E].rearrange("p (t e) -> p t e", t=NT)))
                for e in range(E):
                    step(v.tensor_tensor_scan(cum[:, :, e], ones[:, 0:NT], tot[:, :, e], 0.0, ALU.mult, ALU.add))
                step(v.tensor_tensor(cmp1[:], steps[:], over(cum[:, NT - 1, :], T // SLOTS, 2), ALU.is_lt))
                step(v.tensor_reduce(nb[:], cmp1[:], AX.X, ALU.add))
                step(v.tensor_tensor_scan(endb[:], ones[:, 0:E], nb[:], 0.0, ALU.mult, ALU.add))
                step(v.tensor_tensor(startb[:], endb[:], nb[:], ALU.subtract))
                step(v.tensor_scalar(startb[:], startb[:], float(SLOTS), None, ALU.mult))
                step(v.tensor_tensor(cum[:], cum[:], tot[:], ALU.subtract))
                step(v.tensor_tensor(cum[:], cum[:], over(startb[:], NT, 1), ALU.add))
                step(v.tensor_tensor(cum[:], pre[:, 0:NT * E].rearrange("p (t e) -> p t e", t=NT), cum[:], ALU.add))
                for n in range(2):
                    step(v.tensor_tensor(a[:], cum[:], oh[n][:], ALU.mult))
                    step(v.tensor_reduce(slotf[n][:], a[:], AX.X, ALU.add))
                    step(v.tensor_copy(keep["slot"][n][:], slotf[n][:]), f"slot{n}")
                step(v.tensor_tensor(cmp2[:], blk[:], over(endb[:], NB, 1), ALU.is_ge))
                step(v.tensor_reduce(ebf[:], cmp2[:], AX.X, ALU.add))
                step(v.tensor_scalar(ebf[:], ebf[:], float(E - 1), None, ALU.min))
                step(v.tensor_copy(keep["expert"][:], ebf[:]))
                v.wait_ge(s_ex, 1)
                step(v.tensor_scalar(den[:], ex[:], 1.0, None, ALU.add))
                step(v.reciprocal(keep["weight"][0][:], den[:]))
                step(v.tensor_tensor(keep["weight"][1][:], ex[:], keep["weight"][0][:], ALU.mult))
                v.wait_ge(s_it, 1)
                v.tensor_copy(keep["token"][:], idb[:, 0:NB * TPB])

            @block.sync
            def _(sp):
                sp.dma_start(lg[:], scratch["logits"]).then_inc(s_in, 16)
                sp.wait_ge(s_cst, 10)
                sp.dma_start(scratch["tokens"].rearrange("(s p) a -> s (p a)", p=P), zero[:]).then_inc(s_z, 16)
                sp.wait_ge(s_sc, 16 * 2 * NT)
                sp.dma_start(ids[:], scratch["tokens"].rearrange("(s p) a -> s (p a)", p=P)).then_inc(s_id, 16)

            @block.gpsimd
            def _(g):
                with nc.allow_low_precision(reason="integers below 2^24"):
                    make_identity(g, ident, s_cst, 0)
                    g.memset(ones[:], 1.0).then_inc(s_cst, 1)
                    g.memset(before[:], 1.0).then_inc(s_cst, 1)
                    g.memset(zero[:], 0.0).then_inc(s_cst, 1)
                    g.wait_ge(s_cst, 5)
                    g.affine_select(out=before[:], in_=before[:], compare_op=ALU.is_gt, fill=0.0, base=0,
                                    pattern=[[1, P]], channel_multiplier=-1).then_inc(s_cst, 1)
                    kw = dict(allow_small_or_imprecise_dtypes=True)
                    g.iota(rank[:], [[0, NT], [-1, E]], base=E, channel_multiplier=0, **kw).then_inc(s_cst, 1)
                    g.iota(steps[:], [[0, E], [SLOTS, T // SLOTS]], base=0, channel_multiplier=0, **kw).then_inc(s_cst, 1)
                    g.iota(blk[:], [[1, NB], [0, E]], base=0, channel_multiplier=0, **kw).then_inc(s_cst, 1)
                    g.iota(tok[:], [[P, NT]], base=0, channel_multiplier=1, **kw).then_inc(s_cst, 1)
                g.wait_ge(s_cst, 10)
                g.wait_ge(s_z, 16)
                for n in range(2):
                    g.wait_ge(s_v, marks[f"slot{n}"])
                    for t in range(NT):
                        g.indirect_dma_start(out=scratch["tokens"], in_=tok[:, t:t + 1], in_offset=None,
                                             out_offset=bass.IndirectOffsetOnAxis(ap=keep["slot"][n][:, t:t + 1], axis=0)).then_inc(s_sc, 16)

            @block.scalar
            def _(act):
                act.wait_ge(s_v, marks["gap"])
                act.activation(ex[:], ex[:], ACT.Exp).then_inc(s_ex, 1)

            @block.tensor
            def _(pe):
                pe.wait_ge(s_cst, 10)
                pe.wait_ge(s_v, marks["both"])
                rows = both[:].rearrange("p t e -> p (t e)")
                pe.matmul(pre[:, 0:NT * E], before[:], rows, start=True, stop=True)
                pe.matmul(tob[:, 0:NT * E], ones[:], rows, start=True, stop=True).then_inc(s_mm, 1)
                pe.wait_ge(s_id, 16)
                pe.transpose(idb[:, 0:NB * TPB], ids[:], ident[0:NB * TPB, 0:NB * TPB]).then_inc(s_it, 1)


def phase_experts(nc, keep, w, scratch):
    with ExitStack() as ctx:
        al = Alloc(nc, ctx)
        ident = al.sb("e_ident", [P, P])
        wt = [FfnWeights(al, f"e_w{n}") for n in range(2)]
        xg = [al.sb(f"e_xg{n}", [P, TPB, D]) for n in range(2)]
        idx = [al.sb(f"e_idx{n}", [P, TPB], U32) for n in range(2)]
        xh = [al.sb(f"e_xh{n}", [P, KD, SLOTS], F32R) for n in range(2)]
        xl = [al.sb(f"e_xl{n}", [P, KD, SLOTS], F32R) for n in range(2)]
        sg, hf = al.sb("e_sg", [P, NF, SLOTS]), al.sb("e_hf", [P, NF, SLOTS])
        hh, hl = al.sb("e_hh", [P, NF, SLOTS], F32R), al.sb("e_hl", [P, NF, SLOTS], F32R)
        y = al.sb("e_y", [P, TPB, D])
        tbk = [al.bank(f"e_tb{n}") for n in range(2)]
        fb = [al.bank(f"e_fb{n}") for n in range(2 * NF)]

        WP = 4

        def parts(n):
            return [(wt[n].gu[:, j], wt[n].guh[:, j], wt[n].gul[:, j]) for j in range(2)] + wt[n].down_parts()

        s_cst = al.sem("e_constants_made")
        s_gpass = al.sem("e_pool_passed")
        s_w = [al.sem(f"e_weights_in{n}") for n in range(2)]
        s_x = [al.sem(f"e_rows_in{n}") for n in range(2)]
        s_wh, s_wl = al.sem("e_weights_high"), al.sem("e_weights_low")
        s_idx = al.sem("e_tokens_copied")
        s_t = al.sem("e_transposed")
        s_xh, s_xl = al.sem("e_xh_made"), al.sem("e_xl_made")
        s_gu, s_sg, s_h = al.sem("e_gate_up_made"), al.sem("e_silu_made"), al.sem("e_h_made")
        s_hh, s_hl = al.sem("e_hh_made"), al.sem("e_hl_made")
        s_dn, s_y, s_yst = al.sem("e_down_made"), al.sem("e_y_made"), al.sem("e_y_stored")

        def in_pairs(eng, step):
            step(0, 0, True, False)
            step(1, 1, False, False)
            with eng.Fori(1, (NB - 1) // 2) as i:
                step(i * 2, 0, False, False)
                step(i * 2 + 1, 1, False, False)
            step(NB - 1, 0, False, True)

        assert NB % 2 == 1

        def turns(b, n):
            return b // 2 + 1 if isinstance(b, int) else (b - n) // 2 + 1

        with nc.Block() as block:
            @block.sync
            def _(sp):
                def fetch(b, n, first=False):
                    if not first:
                        sp.wait_ge(s_wl, (b - 1) * WP)
                    e = sp.value_load(keep["expert"][0:1, bass.ds(b, 1)], min_val=0, max_val=E - 1)
                    load_ffn(sp.dma_start, wt[n], w["w_gate"][bass.ds(e, 1)].rearrange("e d f -> (e d) f"),
                             w["w_up"][bass.ds(e, 1)].rearrange("e d f -> (e d) f"),
                             w["w_down"][bass.ds(e, 1)].rearrange("e f d -> (e f) d"), s_w[n])

                def store(b):
                    sp.wait_ge(s_y, b * TPB + TPB)
                    sp.dma_start(scratch["y"][bass.ds(b * SLOTS, SLOTS), :].rearrange("(t p) n -> p t n", p=P), y[:]).then_inc(s_yst, 16)

                fetch(0, 0, True)
                fetch(1, 1, True)
                fetch(2, 0)
                store(0)
                with sp.Fori(1, (NB - 1) // 2) as i:
                    fetch(i * 2 + 1, 1)
                    store(i * 2 - 1)
                    fetch(i * 2 + 2, 0)
                    store(i * 2)
                store(NB - 2)
                store(NB - 1)
                sp.wait_ge(s_yst, NB * 16)

            @block.gpsimd
            def _(g):
                make_identity(g, ident, s_cst, 0)

                def gather(b, n, first=False, last=False):
                    if not (isinstance(b, int) and b < 2):
                        g.wait_ge(s_t, (b - 1) * KD)
                    g.tensor_copy(idx[n][:], keep["token"][:, bass.ds(b * TPB, TPB)]).then_inc(s_idx, 1)
                    wait_apart(g, s_idx, b + 1, s_gpass)
                    for t in range(TPB):
                        g.indirect_dma_start(out=xg[n][:, t, :], in_=scratch["xn"], out_offset=None,
                                             in_offset=bass.IndirectOffsetOnAxis(ap=idx[n][:, t:t + 1], axis=0)).then_inc(s_x[n], 16)

                in_pairs(g, gather)

            @block.scalar
            def _(act):
                def split(b, n, some, first=False):
                    act.wait_ge(s_w[n], turns(b, n) * 64)
                    if not first:
                        act.wait_ge(s_dn, (b - 1) * TPB)
                    for raw, hi, lo in parts(n)[some]:
                        act.activation(hi, raw, ACT.Copy).then_inc(s_wh, 1)

                def x_high(b, n, ks):
                    for k in ks:
                        act.wait_ge(s_t, b * KD + k + 1)
                        act.activation(xh[n][:, k], tbk[k % 2][:], ACT.Copy).then_inc(s_xh, 1)

                def hidden(b, f, first):
                    width = FS[f][1]
                    act.wait_ge(s_gu, (b * NF + f) * 2 + 2)
                    if not first:
                        act.wait_ge(s_h, (b - 1) * NF + f + 1)
                    act.activation(sg[0:width, f], fb[2 * f][0:width, :], ACT.Silu).then_inc(s_sg, 1)
                    act.wait_ge(s_h, b * NF + f + 1)
                    if not first:
                        act.wait_ge(s_dn, b * TPB)
                    act.activation(hh[0:width, f], hf[0:width, f], ACT.Copy).then_inc(s_hh, 1)

                def step(b, n, first, last):
                    for f in range(NF):
                        hidden(b, f, first)
                        if not last:
                            if f:
                                x_high(b + 1, 1 - n, range(2 * f - 2, 2 * f))
                            split(b + 1, 1 - n, slice(f, f + 1 if f < 2 else WP), first)

                split(0, 0, slice(0, WP), True)
                x_high(0, 0, range(KD))
                in_pairs(act, step)

            @block.vector
            def _(v):
                def split(b, n, some):
                    for j, (raw, hi, lo) in list(enumerate(parts(n)))[some]:
                        v.wait_ge(s_wh, b * WP + j + 1)
                        v.tensor_tensor(lo, raw, f32(hi), ALU.subtract).then_inc(s_wl, 1)

                def x_low(b, n, ks):
                    for k in ks:
                        v.wait_ge(s_xh, b * KD + k + 1)
                        v.tensor_tensor(xl[n][:, k], tbk[k % 2][:], f32(xh[n][:, k]), ALU.subtract).then_inc(s_xl, 1)

                def hidden(b, f):
                    width = FS[f][1]
                    v.wait_ge(s_sg, b * NF + f + 1)
                    v.tensor_tensor(hf[0:width, f], sg[0:width, f], fb[2 * f + 1][0:width, :], ALU.mult).then_inc(s_h, 1)
                    v.wait_ge(s_hh, b * NF + f + 1)
                    v.tensor_tensor(hl[0:width, f], hf[0:width, f], f32(hh[0:width, f]), ALU.subtract).then_inc(s_hl, 1)

                def step(b, n, first, last):
                    for f in range(NF):
                        hidden(b, f)
                        if not last:
                            if f:
                                x_low(b + 1, 1 - n, range(2 * f - 2, 2 * f))
                            split(b + 1, 1 - n, slice(f, f + 1 if f < 2 else WP))
                    if not first:
                        v.wait_ge(s_yst, b * 16)
                    for t in range(TPB):
                        v.wait_ge(s_dn, b * TPB + t + 1)
                        v.tensor_copy(y[:, t], fb[t][:]).then_inc(s_y, 1)

                split(0, 0, slice(0, WP))
                x_low(0, 0, range(KD))
                in_pairs(v, step)

            @block.tensor
            def _(pe):
                def transposes(b, n, ks, first=False):
                    pe.wait_ge(s_x[n], turns(b, n) * TPB * 16)
                    for k in ks:
                        if k >= 2 or not first:
                            pe.wait_ge(s_xl, b * KD - 1 + k)
                        for t in range(TPB):
                            ins = pe.transpose(tbk[k % 2][:, t * P:(t + 1) * P], xg[n][:, t, k * P:(k + 1) * P], ident[:])
                        ins.then_inc(s_t, 1)

                def step(b, n, first, last):
                    pe.wait_ge(s_wl, b * WP + WP)
                    pe.wait_ge(s_xl, b * KD + KD)
                    for f in range(NF):
                        for which in range(2):
                            j = 2 * f + which
                            if j < TPB and not first:
                                pe.wait_ge(s_y, (b - 1) * TPB + j + 1)
                            gate_up(nc, fb[j][:], wt[n], which, f, xh[n], xl[n]).then_inc(s_gu, 1)
                        if f and not last:
                            transposes(b + 1, 1 - n, range(2 * f - 2, 2 * f))
                    pe.wait_ge(s_hl, b * NF + NF - 1)
                    for t in range(TPB):
                        down(nc, fb[t][:], wt[n], hh, hl, t, range(NF - 1))
                    pe.wait_ge(s_hl, b * NF + NF)
                    for t in range(TPB):
                        down(nc, fb[t][:], wt[n], hh, hl, t, [NF - 1]).then_inc(s_dn, 1)

                pe.wait_ge(s_cst, 2)
                transposes(0, 0, range(KD), True)
                in_pairs(pe, step)


def phase_combine(nc, keep, scratch, out):
    RING = 4
    with ExitStack() as ctx:
        al = Alloc(nc, ctx)
        y = [[al.sb(f"f_y{k}_{n}", [P, D]) for n in range(RING)] for k in range(2)]
        acc = [al.sb(f"f_acc{n}", [P, D]) for n in range(RING)]
        mid = al.sb("f_mid", [P, D])
        res = [al.sb(f"f_res{n}", [P, D]) for n in range(RING)]
        s_y = [al.sem(f"f_rows_in{n}") for n in range(RING)]
        s_a = [al.sem(f"f_acc_in{n}") for n in range(RING)]
        s_o = [al.sem(f"f_out_stored{n}") for n in range(RING)]
        s_m, s_r = al.sem("f_first_added"), al.sem("f_second_added")

        with nc.Block() as block:
            @block.gpsimd
            def _(g):
                for t in range(NT):
                    n = t % RING
                    if t >= RING:
                        g.wait_ge(s_r, t - RING + 1)
                    for k in range(2):
                        g.indirect_dma_start(out=y[k][n][:], in_=scratch["y"], out_offset=None,
                                             in_offset=bass.IndirectOffsetOnAxis(ap=keep["slot"][k][:, t:t + 1], axis=0)).then_inc(s_y[n], 16)

            @block.sync
            def _(sp):
                for t in range(NT):
                    n = t % RING
                    if t >= RING:
                        sp.wait_ge(s_r, t - RING + 1)
                    sp.dma_start(acc[n][:], scratch["acc"][t * P:(t + 1) * P, :]).then_inc(s_a[n], 16)

            @block.scalar
            def _(act):
                for t in range(NT):
                    act.wait_ge(s_r, t + 1)
                    act.dma_start(out[t * P:(t + 1) * P, :], res[t % RING][:]).then_inc(s_o[t % RING], 16)
                for n in range(RING):
                    act.wait_ge(s_o[n], 16 * NT // RING)

            @block.vector
            def _(v):
                for t in range(NT):
                    n = t % RING
                    v.wait_ge(s_y[n], (t // RING + 1) * 32)
                    v.wait_ge(s_a[n], (t // RING + 1) * 16)
                    if t:
                        v.wait_ge(s_r, t)
                    v.scalar_tensor_tensor(out=mid[:], in0=y[0][n][:], scalar=keep["weight"][0][:, t:t + 1], in1=acc[n][:],
                                           op0=ALU.mult, op1=ALU.add).then_inc(s_m, 1)
                    v.wait_ge(s_m, t + 1)
                    if t >= RING:
                        v.wait_ge(s_o[n], t // RING * 16)
                    v.scalar_tensor_tensor(out=res[n][:], in0=y[1][n][:], scalar=keep["weight"][1][:, t:t + 1], in1=mid[:],
                                           op0=ALU.mult, op1=ALU.add).then_inc(s_r, 1)


INS = ['L0_attn_x', 'L0_attn_wq_w', 'L0_attn_wq_b', 'L0_attn_wk_w', 'L0_attn_wk_b', 'L0_attn_wkl_w', 'L0_attn_wkl_b',
       'L0_attn_wv_w', 'L0_attn_wv_b', 'L0_attn_wvl_w', 'L0_attn_wvl_b', 'L0_attn_upk_w', 'L0_attn_upk_b',
       'L0_attn_upv_w', 'L0_attn_upv_b', 'L0_attn_wo_w', 'L0_attn_wo_b', 'L0_ffn_gate_w', 'L0_ffn_w_gate',
       'L0_ffn_w_up', 'L0_ffn_w_down', 'L0_ffn_sw_gate', 'L0_ffn_sw_up', 'L0_ffn_sw_down']


def program(nc, ins, out):
    w = {n.split("_", 2)[2]: ap for n, ap in ins.items()}
    x = ins['L0_attn_x'].rearrange("b s d -> (b s) d")

    def dram(name, shape, dt=F32):
        return nc.dram_tensor(name, shape, dt, kind="Internal").ap()

    scratch = {
        "qh": dram("scr_qh", (NCH, D, CH)), "ql": dram("scr_ql", (NCH, D, CH)),
        "kh": dram("scr_kh", (NCH, D, CH)), "kl": dram("scr_kl", (NCH, D, CH)),
        "v": dram("scr_v", (NCH, CH, D)),
        "oT": dram("scr_oT", (NCH, D, CH)), "sums": dram("scr_sums", (NCH, H, CH)),
        "rsum": dram("scr_rsum", (NCH, H, CH)), "xn": dram("scr_xn", (T, D)), "acc": dram("scr_acc", (T, D)),
        "logits": dram("scr_logits", (P, NT, E)), "tokens": dram("scr_tokens", (NB * SLOTS, 1)),
        "y": dram("scr_y", (NB * SLOTS, D)),
    }
    phase_project(nc, x, w, scratch)
    phase_attention(nc, scratch)
    phase_shared(nc, x, w, scratch)
    with ExitStack() as ctx:
        al = Alloc(nc, ctx)
        keep = {
            "slot": [al.sb(f"slot{n}", [P, NT], U32) for n in range(2)],
            "weight": [al.sb(f"weight{n}", [P, NT]) for n in range(2)],
            "expert": al.sb("expert", [P, NB], I32),
            "token": al.sb("token", [P, NB * TPB], U32),
        }
        phase_route(nc, keep, scratch)
        phase_experts(nc, keep, w, scratch)
        phase_combine(nc, keep, scratch, out.rearrange("b s d -> (b s) d"))


_OUTS = [((BATCH, SEQ, D), 'float32')]


def kernel(**inputs):
    import numpy as _np
    import concourse.bacc as _bacc
    from concourse import mybir as _mybir
    from concourse.bass_utils import run_bass_kernel_spmd as _run

    nc = _bacc.Bacc("TRN2", target_bir_lowering=False, num_devices=1)
    arrays, ins = {}, {}
    for name in INS:
        a = _np.ascontiguousarray(inputs[name])
        arrays[f"in_{name}_dram"] = a
        ins[name] = nc.dram_tensor(f"in_{name}_dram", a.shape, _mybir.dt.from_np(a.dtype), kind="ExternalInput").ap()
    shape, dtype = _OUTS[0]
    out = nc.dram_tensor("out_0_dram", shape, _mybir.dt.from_np(_np.dtype(dtype)), kind="ExternalOutput").ap()
    program(nc, ins, out)
    r = _run(nc, [arrays], core_ids=[0])
    return r.results[0]["out_0_dram"]
```

```python
from contextlib import ExitStack

import concourse.bass as bass
from concourse import mybir

F32 = mybir.dt.float32
F32R = mybir.dt.float32r
I32 = mybir.dt.int32
U32 = mybir.dt.uint32
ALU = mybir.AluOpType
ACT = mybir.ActivationFunctionType
AX = mybir.AxisListType

P = 128
BATCH, SEQ, D = 2, 2048, 512
T = BATCH * SEQ
H, DH, DL = 16, 32, 128
KD = D // P
CH = 512
NCH = T // CH
CPB = SEQ // CH
TPC = CH // P
EPS = 1e-5
E = 8
F = 352
FS = [(0, P), (P, P), (2 * P, F - 2 * P)]
NF = len(FS)
NT = T // P


class Alloc:

    def __init__(self, nc, ctx):
        self.nc, self.ctx = nc, ctx

    def sb(self, name, shape, dt=F32):
        return self.ctx.enter_context(self.nc.sbuf_tensor(name, shape, dt))

    def bank(self, name, cols=512, dt=F32):
        return self.ctx.enter_context(self.nc.psum_tensor(name, [P, cols], dt))

    def sem(self, name):
        return self.ctx.enter_context(self.nc.semaphore(name))


def f32(ap):
    return ap.bitcast(F32)


def wait_apart(eng, sem, value, passed):
    eng.wait_ge(sem, value)
    eng.sem_inc(passed, 1)


def mm3(nc, out, wh, wl, xh, xl, first, last):
    nc.tensor.matmul(out, wh, xh, start=first, stop=False)
    nc.tensor.matmul(out, wl, xh, start=False, stop=False)
    return nc.tensor.matmul(out, wh, xl, start=False, stop=last)


def broadcast_rows(ap1d, n):
    return bass.AP(ap1d.tensor, ap1d.offset, [[0, P], [1, n]])


def make_identity(g, ident, s_made, count):
    g.memset(ident[:], 0.0).then_inc(s_made, 1)
    g.wait_ge(s_made, count + 1)
    g.affine_select(out=ident[:], in_=ident[:], compare_op=ALU.not_equal, fill=1.0, base=0,
                    pattern=[[-1, P]], channel_multiplier=1).then_inc(s_made, 1)


def phase_project(nc, x, w, scratch):
    with ExitStack() as ctx:
        al = Alloc(nc, ctx)
        ident = al.sb("a_ident", [P, P])
        wstage = al.sb("a_wstage", [P, 3, KD, D])
        lat = al.sb("a_lat", [P, 2, KD, DL])
        up = al.sb("a_up", [P, 2, D])
        wT = al.sb("a_wT", [P, 2, KD, D])
        bcol = al.sb("a_bcol", [P, 5, KD])
        vb = al.sb("a_vb", [P, D])
        wqh, wql = al.sb("a_wqh", [P, KD, D], F32R), al.sb("a_wql", [P, KD, D], F32R)
        fh, fl = al.sb("a_fh", [P, 2, KD, DL], F32R), al.sb("a_fl", [P, 2, KD, DL], F32R)
        uh, ul = al.sb("a_uh", [P, 2, D], F32R), al.sb("a_ul", [P, 2, D], F32R)
        xin = al.sb("a_xin", [P, TPC, D])
        xn = al.sb("a_xn", [P, TPC, D])
        xh, xl = al.sb("a_xh", [P, KD, CH], F32R), al.sb("a_xl", [P, KD, CH], F32R)
        st = al.sb("a_stats", [P, TPC, 6])
        mv = al.sb("a_mv", [P, TPC, 2])
        vare = al.sb("a_vare", [P, TPC])
        mhalf = al.sb("a_mhalf", [P, TPC])
        rstd = al.sb("a_rstd", [P, TPC])
        lh, ll = al.sb("a_lh", [P, 2, CH], F32R), al.sb("a_ll", [P, 2, CH], F32R)
        qh, ql = al.sb("a_qh", [P, KD, CH], F32R), al.sb("a_ql", [P, KD, CH], F32R)
        kh, kl = al.sb("a_kh", [P, KD, CH], F32R), al.sb("a_kl", [P, KD, CH], F32R)
        vo = al.sb("a_vo", [P, TPC, D])
        tb = [al.bank(f"a_tb{n}") for n in range(KD)]
        ob = [al.bank(f"a_ob{n}") for n in range(4)]

        s_kv = al.sem("a_wk_wv_in")
        s_w = al.sem("a_weights_in")
        s_high = al.sem("a_weights_high")
        s_vpass, s_gpass = al.sem("a_vector_passed"), al.sem("a_pool_passed")
        s_id = al.sem("a_ident_made")
        s_wt = al.sem("a_weight_transposed")
        s_wc = al.sem("a_weight_copied")
        s_fold = al.sem("a_folded")
        s_split = al.sem("a_weights_split")
        s_x = al.sem("a_x_in")
        s_xfree = al.sem("a_x_read")
        s_stat = al.sem("a_stats_made")
        s_var = al.sem("a_var_made")
        s_vare = al.sem("a_vare_made")
        s_rstd = al.sem("a_rstd_made")
        s_xn = al.sem("a_xn_made")
        s_t = al.sem("a_x_transposed")
        s_xh = al.sem("a_xh_made")
        s_xl = al.sem("a_xl_made")
        s_mm = al.sem("a_product_made")
        s_hi = al.sem("a_hi_made")
        s_out = al.sem("a_bank_read")
        s_st = al.sem("a_stored")
        s_free = al.sem("a_stage_free")

        NP = 2 + KD + KD + TPC
        Q0, K0, V0 = 2, 2 + KD, 2 + 2 * KD

        with nc.Block() as block:
            @block.sync
            def _(sp):
                with nc.allow_non_contiguous_dma(reason="bias columns"):
                    for n, name in ((1, "wk_w"), (2, "wv_w"), (0, "wq_w")):
                        sp.dma_start(wstage[:, n], w[name].rearrange("(k p) n -> p k n", p=P)).then_inc(s_kv if n else s_w, 16)
                    for n, name in enumerate(("wkl_w", "wvl_w")):
                        sp.dma_start(lat[:, n], w[name].rearrange("(k p) n -> p k n", p=P)).then_inc(s_w, 16)
                    for n, name in enumerate(("upk_w", "upv_w")):
                        sp.dma_start(up[:, n].rearrange("p (h d) -> p h d", h=H),
                                     w[name].rearrange("h l d -> l h d")).then_inc(s_w, 16)
                    for n, name in enumerate(("wq_b", "wk_b", "wv_b")):
                        sp.dma_start(bcol[:, n], w[name].rearrange("(k p) -> p k", p=P)).then_inc(s_w, 16)
                    sp.dma_start(bcol[:, 3], w["upk_b"].rearrange("h d -> (h d)").rearrange("(k p) -> p k", p=P)).then_inc(s_w, 16)
                    for n, name in enumerate(("wkl_b", "wvl_b")):
                        sp.dma_start(bcol[:, 4, n:n + 1], w[name].rearrange("(p a) -> p a", a=1)).then_inc(s_w, 16)
                    sp.dma_start(vb[:], broadcast_rows(w["upv_b"], D)).then_inc(s_w, 16)

                def store(c):
                    rows = "(k p) t -> p k t"
                    sp.wait_ge(s_out, c * NP + K0)
                    sp.dma_start(scratch["qh"][c].rearrange(rows, p=P), f32(qh[:])).then_inc(s_st, 16)
                    sp.dma_start(scratch["ql"][c].rearrange(rows, p=P), f32(ql[:])).then_inc(s_st, 16)
                    sp.wait_ge(s_out, c * NP + V0)
                    sp.dma_start(scratch["kh"][c].rearrange(rows, p=P), f32(kh[:])).then_inc(s_st, 16)
                    sp.dma_start(scratch["kl"][c].rearrange(rows, p=P), f32(kl[:])).then_inc(s_st, 16)
                    sp.wait_ge(s_out, c * NP + NP)
                    sp.dma_start(scratch["v"][c].rearrange("(t p) n -> p t n", p=P), vo[:]).then_inc(s_st, 16)
                    sp.wait_ge(s_st, c * 80 + 80)
                    sp.nop().then_inc(s_free, 1)

                with sp.Fori(0, NCH) as c:
                    store(c)

            @block.gpsimd
            def _(g):
                make_identity(g, ident, s_id, 0)
                g.memset(mhalf[:], -0.5).then_inc(s_vare, 1)

                def chunk(c, first=False):
                    if not first:
                        g.wait_ge(s_xfree, c)
                    g.dma_start(xin[:], x[bass.ds(c * CH, CH), :].rearrange("(t p) n -> p t n", p=P)).then_inc(s_x, 16)
                    wait_apart(g, s_var, c * TPC + TPC, s_gpass)
                    g.tensor_scalar(vare[:], mv[:, :, 1], EPS, None, ALU.add).then_inc(s_vare, 1)
                    g.wait_ge(s_vare, c + 2)
                    g.tensor_tensor(rstd[:], vare[:], mhalf[:], ALU.pow).then_inc(s_rstd, 1)

                chunk(0, first=True)
                with g.Fori(1, NCH) as c:
                    chunk(c)

            @block.scalar
            def _(act):
                for n in range(2):
                    for k in range(KD):
                        act.wait_ge(s_wt, n * KD + k + 1)
                        act.activation(wT[:, n, k], tb[k][:], ACT.Copy).then_inc(s_wc, 1)
                for n in range(2):
                    act.wait_ge(s_fold, n + 1)
                    act.activation(fh[:, n], ob[n][:].rearrange("p (k l) -> p k l", k=KD), ACT.Copy).then_inc(s_high, 1)
                act.wait_ge(s_w, 16 * 12)
                act.activation(wqh[:], wstage[:, 0], ACT.Copy).then_inc(s_high, 1)
                act.activation(uh[:], up[:], ACT.Copy).then_inc(s_high, 1)

                def high_x(c, first=False):
                    if not first:
                        act.wait_ge(s_mm, (c - 1) * NP + K0)
                    for k in range(KD):
                        act.wait_ge(s_t, c * KD + k + 1)
                        act.activation(xh[:, k], tb[k][:], ACT.Copy).then_inc(s_xh, 1)

                def high(c, js, first=False):
                    for j in js:
                        if j == Q0 and not first:
                            act.wait_ge(s_free, c)
                        act.wait_ge(s_mm, c * NP + j + 1)
                        dst, bias = (
                            (lh[:, j], bcol[:, 4, 2 + j:3 + j]) if j < Q0 else
                            (qh[:, j - Q0], bcol[:, 0, j - Q0:j - Q0 + 1]) if j < K0 else
                            (kh[:, j - K0], bcol[:, 3, j - K0:j - K0 + 1]))
                        act.activation(dst, ob[j % 4][:], ACT.Identity, bias=bias).then_inc(s_hi, 1)

                act.wait_ge(s_split, 5)
                high_x(0, first=True)
                high(0, range(K0), first=True)
                high_x(1)
                high(0, range(K0, V0))
                with act.Fori(1, NCH - 1) as c:
                    high(c, range(K0))
                    high_x(c + 1)
                    high(c, range(K0, V0))
                high(NCH - 1, range(V0))

            @block.vector
            def _(v):
                def norm(c, first=False):
                    v.wait_ge(s_x, c * 16 + 16)
                    for t in range(TPC):
                        v.bn_stats(st[:, t], xin[:, t]).then_inc(s_stat, 1)
                    for t in range(TPC):
                        wait_apart(v, s_stat, c * TPC + t + 1, s_vpass)
                        v.bn_aggr(mv[:, t], st[:, t]).then_inc(s_var, 1)
                    v.wait_ge(s_rstd, c + 1)
                    if not first:
                        v.wait_ge(s_t, c * KD)
                    for t in range(TPC):
                        ins = v.tensor_scalar(xn[:, t], xin[:, t], mv[:, t, 0:1], rstd[:, t:t + 1], ALU.subtract, ALU.mult)
                        ins.then_inc(s_xn, 1)
                    v.wait_ge(s_xn, c * TPC + TPC)
                    v.nop().then_inc(s_xfree, 1)

                def low_x(c):
                    for k in range(KD):
                        v.wait_ge(s_xh, c * KD + k + 1)
                        v.tensor_tensor(xl[:, k], tb[k][:], f32(xh[:, k]), ALU.subtract).then_inc(s_xl, 1)

                def low(c, js):
                    for j in js:
                        if j < V0:
                            v.wait_ge(s_hi, c * V0 + j + 1)
                            dst, hi, bias = (
                                (ll[:, j], lh[:, j], bcol[:, 4, 2 + j:3 + j]) if j < Q0 else
                                (ql[:, j - Q0], qh[:, j - Q0], bcol[:, 0, j - Q0:j - Q0 + 1]) if j < K0 else
                                (kl[:, j - K0], kh[:, j - K0], bcol[:, 3, j - K0:j - K0 + 1]))
                            ins = v.scalar_tensor_tensor(out=dst, in0=ob[j % 4][:], scalar=bias, in1=f32(hi), op0=ALU.add, op1=ALU.subtract)
                        else:
                            v.wait_ge(s_mm, c * NP + j + 1)
                            ins = v.tensor_tensor(vo[:, j - V0], ob[j % 4][:], vb[:], ALU.add)
                        ins.then_inc(s_out, 1)

                norm(0, first=True)
                for n in range(2):
                    v.wait_ge(s_high, 2)
                    v.tensor_tensor(fl[:, n], ob[n][:].rearrange("p (k l) -> p k l", k=KD), f32(fh[:, n]), ALU.subtract).then_inc(s_split, 1)
                v.wait_ge(s_fold, 3)
                v.tensor_tensor(bcol[:, 4, 2:4], ob[2][:, 0:2], bcol[:, 4, 0:2], ALU.add).then_inc(s_split, 1)
                v.wait_ge(s_high, 4)
                v.tensor_tensor(wql[:], wstage[:, 0], f32(wqh[:]), ALU.subtract).then_inc(s_split, 1)
                v.tensor_tensor(ul[:], up[:], f32(uh[:]), ALU.subtract).then_inc(s_split, 1)
                v.wait_ge(s_split, 5)
                low_x(0)
                with v.Fori(0, NCH - 1) as c:
                    low(c, range(Q0))
                    norm(c + 1)
                    low(c, range(Q0, K0))
                    low_x(c + 1)
                    low(c, range(K0, NP))
                low(NCH - 1, range(NP))

            @block.tensor
            def _(pe):
                pe.wait_ge(s_id, 2)
                pe.wait_ge(s_kv, 32)
                for n in range(2):
                    for k in range(KD):
                        if n:
                            pe.wait_ge(s_wc, k + 1)
                        for m in range(KD):
                            ins = pe.transpose(tb[k][:, m * P:(m + 1) * P], wstage[:, 1 + n, m, k * P:(k + 1) * P], ident[:])
                        ins.then_inc(s_wt, 1)
                pe.wait_ge(s_wc, 2 * KD)
                pe.wait_ge(s_w, 16 * 12)
                for n in range(2):
                    for m in range(KD):
                        for k in range(KD):
                            ins = pe.matmul(ob[n][:, m * DL:(m + 1) * DL], wT[:, n, k, m * P:(m + 1) * P], lat[:, n, k],
                                            start=(k == 0), stop=(k == KD - 1))
                    ins.then_inc(s_fold, 1)
                for n in range(2):
                    for k in range(KD):
                        ins = pe.matmul(ob[2][:, n:n + 1], lat[:, n, k], bcol[:, 1 + n, k:k + 1],
                                        start=(k == 0), stop=(k == KD - 1))
                ins.then_inc(s_fold, 1)

                def transposes(c, first=False):
                    pe.wait_ge(s_xn, c * TPC + TPC)
                    for k in range(KD):
                        if not first:
                            pe.wait_ge(s_xl, (c - 1) * KD + k + 1)
                        for t in range(TPC):
                            ins = pe.transpose(tb[k][:, t * P:(t + 1) * P], xn[:, t, k * P:(k + 1) * P], ident[:])
                        ins.then_inc(s_t, 1)

                def products(c, js, first=False):
                    for j in js:
                        if not (first and j < 4):
                            pe.wait_ge(s_out, c * NP + (j - 3 if j >= 4 else -((NP - 1 - j) % 4)))
                        bank = ob[j % 4][:]
                        if j < K0:
                            if j == 0:
                                pe.wait_ge(s_xl, c * KD + KD)
                            for k in range(KD):
                                wh, wl = ((fh[:, j, k], fl[:, j, k]) if j < Q0 else
                                          (wqh[:, k, (j - Q0) * P:(j - Q0 + 1) * P], wql[:, k, (j - Q0) * P:(j - Q0 + 1) * P]))
                                ins = mm3(nc, bank, wh, wl, xh[:, k], xl[:, k], k == 0, k == KD - 1)
                        elif j < V0:
                            m = j - K0
                            ins = mm3(nc, bank, uh[:, 0, m * P:(m + 1) * P], ul[:, 0, m * P:(m + 1) * P], lh[:, 0], ll[:, 0], True, True)
                        else:
                            t = j - V0
                            ins = mm3(nc, bank, lh[:, 1, t * P:(t + 1) * P], ll[:, 1, t * P:(t + 1) * P], uh[:, 1], ul[:, 1], True, True)
                        ins.then_inc(s_mm, 1)

                pe.wait_ge(s_split, 5)
                transposes(0, first=True)
                products(0, range(K0), first=True)
                transposes(1)
                products(0, range(K0, NP))
                with pe.Fori(1, NCH - 1) as c:
                    products(c, range(K0))
                    transposes(c + 1)
                    products(c, range(K0, NP))
                products(NCH - 1, range(NP))


GPB = H // 4
NG = BATCH * GPB
PAIRS = 2
NQ = SEQ // CH
SCALE = 1.0 / DH ** 0.5


SHARE = (0, 1, 1, 2)
ADDED = 0.9


def by_pool(q, kt):
    return kt < TPC * q - SHARE[q]


PARTS = ((3, 3), (0, 3))


def attention_plan():
    units = [(p, q) for p in range(PAIRS) for q in range(NQ)]
    steps, first_step = [], []
    for u, (p, q) in enumerate(units):
        first_step.append(len(steps))
        steps += [(u, p, q, kt) for kt in range(TPC * (q + 1))]
    stream, pending, end = [], None, []
    for u, (p, q) in enumerate(units):
        items = [("max", u, t, h, c) for t in range(TPC) for h in range(2) for c in range(q + 1)]
        lag = min(4, len(items))
        stream += items[:lag]
        if pending is not None:
            stream.append(("turn", pending))
            end.append(len(stream))
        stream += items[lag:]
        pending = u
    stream.append(("turn", pending))
    end.append(len(stream))
    ahead = 3

    def cost(item):
        if item[0] == "turn":
            return 450
        _, u, t, h, c = item
        return 80 + min(CH, (TPC * units[u][1] + t + 1) * P - c * CH)

    def room(n):
        _, p, q, kt = steps[n - 1]
        d = kt - TPC * q
        width = 0 if by_pool(q, kt - 1) or d - 1 < -SHARE[q] else CH - max(d, 0) * P
        return 1400 - ADDED * 2 * width

    ni = len(stream)
    costs = [cost(i) for i in stream]
    rooms = [room(n) for n in range(len(steps))]
    for start in range(end[0] + 1, ni):
        upto, pos, spent, due = [], start, 0, 0
        for n in range(len(steps)):
            due += rooms[n] * sum(costs) / sum(rooms)
            while pos < start + ni and spent + costs[pos % ni] / 2 < due:
                spent += costs[pos % ni]
                pos += 1
            upto.append(pos)
        upto[-1] = start + ni
        if all(end[u] < upto[first_step[u] - ahead - 1] for u in range(1, len(units))):
            break
    return units, steps, first_step, stream, start, upto, end


def over_groups(eng, group):
    group(0, True, False)
    with eng.Fori(1, NG - 1) as it:
        group(it, False, False)
    group(NG - 1, False, True)


class Ahead:

    def __init__(self, al):
        self.wos, self.wob = al.sb("wo", [P, KD, D]), al.sb("wo_b", [P, D])
        self.gw = al.sb("gate_w", [P, KD, E])
        self.raw = (al.sb("sw_gu", [P, 2, KD, F]), al.sb("sw_d", [P, NF, D]))
        self.oin = al.sb("oin", [P, KD, CH])
        self.rin = al.sb("rin", [P, KD, CH])
        self.xin = al.sb("xin", [P, TPC, D])


def load_attention(dma, scratch, c, ahead):
    return dma(ahead.oin[:], scratch["oT"][bass.ds(c, 1)].rearrange("c (k p) t -> p (c k) t", p=P))


def load_rows(dma, x, c, ahead):
    return dma(ahead.xin[:], x[bass.ds(c * CH, CH), :].rearrange("(t p) n -> p t n", p=P))


def load_reciprocals(dma, scratch, c, ahead):
    loads = []
    for j in range(H // KD):
        src = scratch["rsum"][bass.ds(c, 1), bass.ds(j, 1), :]
        src = bass.AP(src.tensor, src.offset, [[0, DH], [H // KD * CH, KD], [1, CH]])
        loads.append(dma(ahead.rin[j * DH:(j + 1) * DH], src))
    return loads


def batch_rows(scratch, name, b):
    return scratch[name][b * CPB:(b + 1) * CPB].rearrange("c h t -> (c h) t")


def phase_attention(nc, x, w, scratch, ahead):
    units, steps, first_step, stream, start, upto, end = attention_plan()
    NS, NI, NU = len(steps), len(stream), len(units)
    NPB, NST, NMX, NOB, NSB = 8, 2, 2, 2, 2
    assert NS % NPB == 0 and NI % NMX == 0 and NU % NOB == 0 and NS % NST == 0
    pool_ops, vec_ops = [], []
    for n, (u, p, q, kt) in enumerate(steps):
        begin = TPC * q - SHARE[q]
        if 0 < kt < begin:
            pool_ops.append(("tile", n))
        if kt > begin:
            vec_ops += [("copy", n)] * (kt == TPC * q + 1 == begin + 1) + [("tile", n)]
        if q > 0 and kt == TPC * q + TPC - 1:
            pool_ops.append(("rest", n))
    NA, ND = len(pool_ops), len(vec_ops)
    fin = [u for u, (p, q) in enumerate(units) if q > 0]
    assert len(fin) % NSB == 0

    def pool_count(n):
        return pool_ops.index(("tile", n + (steps[n][3] == 0))) + 1

    def vec_count(n):
        q, kt = steps[n][2:]
        return vec_ops.index(("tile", n + (kt == TPC * q - SHARE[q]))) + 1

    def unit_count(u):
        return pool_ops.index(("rest", (first_step + [NS])[u + 1] - 1)) + 1

    RAW, FOLD, FINAL, STORE = 2, 4, 5, 6

    def units_at(n, offset):
        for u in range(NU):
            at = (first_step + [NS])[u + 1] + offset
            if at == n:
                return [(u, False)]
            if at - NS == n:
                return [(u, True)]
        return []

    KR = 3 * DH
    MROW = KR
    MCOL = (MROW, 64)

    with ExitStack() as ctx:
        al = Alloc(nc, ctx)
        ident = al.sb("b_ident", [P, P])
        ones = al.sb("b_ones", [P, DH])
        qb = [al.sb(f"b_q{p}", [MROW + 1, 2, SEQ], F32R) for p in range(PAIRS)]
        kb = [al.sb(f"b_k{p}", [MROW + 1, 2, SEQ], F32R) for p in range(PAIRS)]
        vbuf = [al.sb(f"b_v{p}", [P, SEQ // P, 2 * DH]) for p in range(PAIRS)]
        pt = [al.sb(f"b_pt{n}", [P, 2, CH]) for n in range(NPB)]
        below = [al.sb(f"b_below{n}", [P, 2, CH]) for n in range(NSB)]
        diag = [al.sb(f"b_diag{n}", [P, 2, CH]) for n in range(NOB)]
        raw = [al.sb(f"b_raw{n}", [P, CH]) for n in range(NOB)]
        fold = al.sb("b_fold", [P, 2 * DH])
        zerob = al.sb("b_zero", [P, DH], mybir.dt.bfloat16)
        mpart = [al.sb(f"b_mpart{n}", [P, 2, TPC, NQ]) for n in range(2)]
        mt = [al.sb(f"b_mt{n}", [P, TPC, MROW + 1]) for n in range(2)]
        ost = [al.sb(f"b_ost{n}", [P, CH]) for n in range(NOB)]
        causal = al.sb("b_causal", [P, P], mybir.dt.bfloat16)
        identb = al.sb("b_identb", [P, P], mybir.dt.bfloat16)
        stb = [al.bank(f"b_st{n}", 2 * CH) for n in range(NST)]
        mxb = [al.bank(f"b_mx{n}") for n in range(NMX)]
        ob = [al.bank(f"b_ob{n}") for n in range(NOB)]

        sums, rsum = al.sb("b_sums", [CPB * H, CH]), al.sb("b_rsum", [CPB * H, CH])

        s_cst = al.sem("b_constants_made")
        s_ahead = al.sem("b_weights_in")
        s_batch = al.sem("b_batch_stored")
        s_sum = al.sem("b_sums_in")
        s_rec = al.sem("b_reciprocals_made")
        s_rst = al.sem("b_reciprocals_stored")
        s_first = al.sem("b_chunk_in")
        s_rows = al.sem("b_rows_made")
        s_ld = [al.sem(f"b_pair{p}_in") for p in range(PAIRS)]
        s_item = al.sem("b_item_made")
        s_iread = al.sem("b_item_read")
        s_mcol = al.sem("b_max_columns")
        s_red = al.sem("b_partial_max")
        s_st = al.sem("b_scores_made")
        s_exp = al.sem("b_exp_made")
        s_pv = al.sem("b_step_used")
        s_add = al.sem("b_pool_added")
        s_dia = al.sem("b_vector_added")
        s_raw = al.sem("b_halves_copied")
        s_fold = al.sem("b_folded")
        s_oev = al.sem("b_out_read")
        s_ost = [al.sem(f"b_out_stored{n}") for n in range(NOB)]

        with nc.Block() as block:
            @block.gpsimd
            def _(g):
                make_identity(g, ident, s_cst, 0)
                g.memset(causal[:], 0.0).then_inc(s_cst, 1)
                g.wait_ge(s_cst, 3)
                g.affine_select(out=causal[:], in_=causal[:], compare_op=ALU.is_ge, fill=-1e30, base=0,
                                pattern=[[-1, P]], channel_multiplier=1).then_inc(s_cst, 1)
                g.memset(identb[:], 0.0).then_inc(s_cst, 1)
                g.wait_ge(s_cst, 5)
                g.affine_select(out=identb[:], in_=identb[:], compare_op=ALU.not_equal, fill=1.0, base=0,
                                pattern=[[-1, P]], channel_multiplier=1).then_inc(s_cst, 1)
                g.memset(ones[:], 1.0).then_inc(s_cst, 1)
                g.memset(zerob[:], 0.0).then_inc(s_cst, 1)

                def add(it, i, first):
                    what, n = pool_ops[i]
                    u, kt = steps[n][0], steps[n][3]
                    f = fin.index(u)
                    out = below[f % NSB][:]
                    so_far = out
                    if kt == 1:
                        so_far = pt[(n - 1) % NPB][:]
                        if f >= NSB:
                            g.wait_ge(s_fold, it * NU + fin[f - NSB] + 1)
                        elif not first:
                            g.wait_ge(s_fold, it * NU + fin[f - NSB] - NU + 1)
                    else:
                        g.wait_ge(s_add, it * NA + i)
                    if what == "tile":
                        g.wait_ge(s_exp, it * NS + n + 1)
                        more = pt[n % NPB][:]
                    else:
                        g.wait_ge(s_dia, it * ND + vec_count(n))
                        more = diag[u % NOB][:]
                    g.tensor_tensor(out, so_far, more, ALU.add).then_inc(s_add, 1)

                def group(it, first, last):
                    for i in range(NA):
                        add(it, i, first)

                over_groups(g, group)

            NROW = 5
            NCST = 8
            LD = 13 * 16
            STO = NU // NOB * 48

            @block.sync
            def _(sp):
                def load(it, p, first=False):
                    if not first:
                        sp.wait_ge(s_pv, (it - 1) * NS + (p + 1) * NS // PAIRS)
                    b, g = (it // GPB, it % GPB) if not first else (0, 0)
                    if not first:
                        b, g = sp.snap(b), sp.snap(g)
                    for h in range(2):
                        row = g * P + p * 2 * DH + h * DH
                        for buf, parts in ((qb[p], ("qh", "ql", "qh")), (kb[p], ("kh", "kh", "kl"))):
                            for n, name in enumerate(parts):
                                dst = f32(buf[n * DH:(n + 1) * DH, h]).rearrange("d (c t) -> d c t", c=CPB)
                                src = scratch[name][bass.ds(b * CPB, CPB), bass.ds(row, DH), :].rearrange("c d t -> d c t")
                                sp.dma_start(dst, src).then_inc(s_ld[p], 16)
                    src = scratch["v"][bass.ds(b * CPB, CPB), :, bass.ds(g * P + p * 2 * DH, 2 * DH)]
                    sp.dma_start(vbuf[p][:], src.rearrange("c (t k) d -> k (c t) d", k=P)).then_inc(s_ld[p], 16)

                for p in range(PAIRS):
                    load(0, p, first=True)
                with sp.Fori(1, NG) as it:
                    for p in range(PAIRS):
                        load(it, p)
                sp.dma_start(ahead.wos[:], w["wo_w"].rearrange("(k p) n -> p k n", p=P)).then_inc(s_ahead, 16)
                sp.dma_start(ahead.wob[:], broadcast_rows(w["wo_b"], D)).then_inc(s_ahead, 16)
                with nc.allow_non_contiguous_dma(reason="router weights as columns"):
                    for k in range(KD):
                        sp.dma_start(ahead.gw[:, k], w["gate_w"][:, k * P:(k + 1) * P].rearrange("e p -> p e")).then_inc(s_ahead, 16)
                load_ffn(sp.dma_start, FfnRaw(ahead.raw), w["sw_gate"], w["sw_up"], w["sw_down"], s_ahead)
                sp.wait_ge(s_batch, 1)
                sp.dma_start(sums[:], batch_rows(scratch, "sums", 0)).then_inc(s_sum, 16)
                load_attention(sp.dma_start, scratch, 0, ahead).then_inc(s_first, 16)
                load_rows(sp.dma_start, x, 0, ahead).then_inc(s_first, 16)
                sp.wait_ge(s_rec, 1)
                sp.dma_start(batch_rows(scratch, "rsum", 0), rsum[:]).then_inc(s_rst, 16)
                sp.wait_ge(s_rst, 16)
                for ins in load_reciprocals(sp.dma_start, scratch, 0, ahead):
                    ins.then_inc(s_first, 16)
                sp.wait_ge(s_first, 16 * (2 + H // KD))
                sp.wait_ge(s_ahead, 16 * (2 + KD + 4))
                for sem in s_ost:
                    sp.wait_ge(sem, NG * STO)


            @block.vector
            def _(v):
                def item(it, i, what):
                    bank = mxb[i % NMX]
                    v.wait_ge(s_item, it * NI + i + 1)
                    if what[0] == "max":
                        _, u, t, h, c = what
                        n = (TPC * units[u][1] + t + 1) * P
                        w = min(CH, n - c * CH)
                        w = 2 * P if w == P and n > P else w
                        v.tensor_reduce(mpart[u % 2][:, h, t, c:c + 1], bank[:, 0:w], AX.X, ALU.max).then_inc(s_iread, 1)
                        if (t, h, c) == (TPC - 1, 1, units[u][1]):
                            done = sum(x[0] == "max" for x in stream[:i + 1]) + sum(x[0] == "turn" for x in stream[:i + 1])
                            v.wait_ge(s_iread, it * NI + done)
                            for hh in range(2):
                                v.tensor_reduce(mt[u % 2][:, :, MCOL[hh]], mpart[u % 2][:, hh, :, 0:units[u][1] + 1],
                                                AX.X, ALU.max, negate=True).then_inc(s_mcol, 1)
                    else:
                        u = what[1]
                        p, q = units[u]
                        for h in range(2):
                            ins = v.tensor_copy(qb[p][MROW:MROW + 1, h, q * CH:(q + 1) * CH], bank[MCOL[h]:MCOL[h] + 1, :])
                        ins.then_inc(s_iread, 1)

                for p in range(PAIRS):
                    v.memset(f32(kb[p][MROW:MROW + 1]), 1.0).then_inc(s_rows, 1)
                for n in range(2):
                    v.memset(mt[n][:], 0.0).then_inc(s_rows, 1)
                v.wait_ge(s_cst, NCST)
                v.tensor_tensor(fold[:], ident[:, 0:2 * DH], ident[:, 2 * DH:4 * DH], ALU.add).then_inc(s_rows, 1)
                v.wait_ge(s_rows, NROW)

                def add(it, n, first):
                    u, p, q, kt = steps[n]
                    begin = TPC * q - SHARE[q]
                    if kt <= begin:
                        return
                    out, lo = diag[u % NOB], max(kt - TPC * q, 0) * P
                    if kt == begin + 1 and (u >= NOB or not first):
                        v.wait_ge(s_fold, it * NU + u - NOB + 1)
                    v.wait_ge(s_exp, it * NS + n + 1)
                    if kt == begin + 1:
                        so_far = pt[(n - 1) % NPB]
                        if lo:
                            v.tensor_copy(out[:, :, 0:lo], so_far[:, :, 0:lo]).then_inc(s_dia, 1)
                    else:
                        so_far = out
                        v.wait_ge(s_dia, it * ND + vec_count(n) - 1)
                    v.tensor_tensor(out[:, :, lo:], so_far[:, :, lo:], pt[n % NPB][:, :, lo:], ALU.add).then_inc(s_dia, 1)

                def group(it, first, last):
                    done = start
                    for n in range(NS):
                        for i in range(done, upto[n]):
                            if i < NI:
                                item(it, i, stream[i])
                            elif not last:
                                item(it + 1, i - NI, stream[i - NI])
                        done = upto[n]
                        if n:
                            add(it, n - 1, first)
                        elif not first:
                            add(it - 1, NS - 1, False)
                        if last and n == first_step[3]:
                            v.wait_ge(s_sum, 16)
                            v.reciprocal(rsum[:], sums[:]).then_inc(s_rec, 1)
                    if last:
                        add(it, NS - 1, False)

                for i in range(start):
                    item(0, i, stream[i])
                over_groups(v, group)

            @block.scalar
            def _(act):
                def exps(it, n, first):
                    u, p, q, kt = steps[n]
                    lo = max(kt - TPC * q, 0) * P
                    act.wait_ge(s_st, it * NS + n + 1)
                    before = n - NPB
                    if before >= 0 or not first:
                        act.wait_ge(s_pv, it * NS + before + 1)
                        back = 1 if before < 0 else 0
                        if by_pool(*steps[before][2:]):
                            act.wait_ge(s_add, it * NA + pool_count(before % NS) - back * NA)
                        else:
                            act.wait_ge(s_dia, it * ND + vec_count(before % NS) - back * ND)
                    act.activation(pt[n % NPB][:, :, lo:], stb[n % NST][:].rearrange("k (h q) -> k h q", h=2)[:, :, lo:],
                                   ACT.Exp, scale=SCALE).then_inc(s_exp, 1)

                def copy_halves(it, u):
                    act.wait_ge(s_pv, it * NS + (first_step + [NS])[u + 1])
                    act.activation(raw[u % NOB][:], ob[u % NOB][:], ACT.Copy).then_inc(s_raw, 1)

                def evacuate(it, u, first):
                    act.wait_ge(s_fold, it * NU + u + 1)
                    if u >= NOB or not first:
                        act.wait_ge(s_ost[u % NOB], it * STO + u // NOB * 48)
                    act.activation(ost[u % NOB][:], ob[u % NOB][:], ACT.Copy).then_inc(s_oev, 1)

                def store(it, b, g, u):
                    p, q = units[u]
                    act.wait_ge(s_oev, it * NU + u + 1)
                    st, chunk = ost[u % NOB], b * CPB + q
                    act.dma_start(scratch["oT"][bass.ds(chunk, 1), bass.ds(g * P + p * 2 * DH, 2 * DH), :].rearrange("c d t -> (c d) t"),
                                  st[0:2 * DH, :]).then_inc(s_ost[u % NOB], 16)
                    for h in range(2):
                        act.dma_start(scratch["sums"][bass.ds(chunk, 1), bass.ds(g * 4 + p * 2 + h, 1), :].rearrange("c d t -> (c d) t"),
                                      st[2 * DH + h * DH:2 * DH + h * DH + 1, :]).then_inc(s_ost[u % NOB], 16)

                def place(it):
                    return (it // GPB, it % GPB) if isinstance(it, int) else (act.snap(it // GPB), act.snap(it % GPB))

                def group(it, first, last):
                    b, g = place(it)
                    if not first:
                        before = it - 1
                        bb, gg = place(before)
                    for n in range(NS):
                        exps(it, n, first)
                        for u, prev in units_at(n, RAW):
                            if not (prev and first):
                                copy_halves(before if prev else it, u)
                        for u, prev in units_at(n, FINAL):
                            if not (prev and first):
                                evacuate(before if prev else it, u, first and not prev)
                                if last and not prev and u == NOB - 1:
                                    act.sem_inc(s_batch, 1)
                        for u, prev in units_at(n, STORE):
                            if not prev:
                                store(it, b, g, u)
                            elif not first:
                                store(before, bb, gg, u)
                    if last:
                        copy_halves(it, NU - 1)
                        evacuate(it, NU - 1, False)
                        store(it, b, g, NU - 1)

                over_groups(act, group)
                for sem in s_ost:
                    act.wait_ge(sem, NG * STO)

            @block.tensor
            def _(pe):
                def item(it, i, first):
                    what = stream[i]
                    bank = mxb[i % NMX]
                    if i >= NMX or not first:
                        pe.wait_ge(s_iread, it * NI + i - NMX + 1)
                    if what[0] == "max":
                        _, u, t, h, c = what
                        p, q = units[u]
                        tile = TPC * q + t
                        n = (tile + 1) * P
                        w = min(CH, n - c * CH)
                        lo = c * CH
                        if w == P and n > P:
                            lo, w = lo - P, 2 * P
                        if (t, h, c) == (0, 0, 0):
                            pe.wait_ge(s_ld[p], it * LD + LD)
                        diag = lo + w == n
                        ins = pe.matmul(bank[:, 0:w], qb[p][0:KR, h, tile * P:(tile + 1) * P], kb[p][0:KR, h, lo:lo + w],
                                        start=True, stop=not diag)
                        if diag:
                            ins = pe.matmul(bank[:, w - P:w], identb[:], causal[:], start=False, stop=True)
                        ins.then_inc(s_item, 1)
                    else:
                        u = what[1]
                        pe.wait_ge(s_mcol, it * 2 * NU + 2 * u + 2)
                        for t in range(TPC):
                            ins = pe.transpose(bank[0:MROW + 1, t * P:(t + 1) * P], mt[u % 2][:, t, :], ident[:])
                        ins.then_inc(s_item, 1)

                def scores(it, n, first, between):
                    u, p, q, kt = steps[n]
                    d = kt - TPC * q
                    lo = min(max(d, 0) * P, 2 * P)
                    if n >= NST or not first:
                        pe.wait_ge(s_exp, it * NS + n - NST + 1)
                    if kt == 0:
                        pe.wait_ge(s_iread, it * NI + end[u])
                    for h in range(2):
                        ins = pe.matmul(stb[n % NST][:, h * CH + lo:(h + 1) * CH], kb[p][:, h, kt * P:(kt + 1) * P],
                                        qb[p][:, h, q * CH + lo:(q + 1) * CH], start=True, stop=d < 0)
                        if d >= 0:
                            ins = pe.matmul(stb[n % NST][:, h * CH + d * P:h * CH + (d + 1) * P], causal[:], identb[:],
                                            start=False, stop=True)
                        if h == 0:
                            between()
                    ins.then_inc(s_st, 1)

                def values(it, n, first):
                    u, p, q, kt = steps[n]
                    out = ob[u % NOB]
                    pe.wait_ge(s_exp, it * NS + n + 2)
                    if kt == 0 and (u >= NOB or not first):
                        pe.wait_ge(s_oev, it * NU + u - NOB + 1)
                    if kt == 0 and q == 0:
                        for j in range(2):
                            pe.matmul(out[(2 + j) * DH:(3 + j) * DH, 0:P], zerob[:], identb[:], start=True, stop=False)
                    for m in range(2):
                        d = kt + m - TPC * q
                        lo = max(d, 0) * P
                        for j in range(2):
                            ins = pe.matmul(out[(2 * m + j) * DH:(2 * m + j + 1) * DH, lo:],
                                            vbuf[p][:, kt + m, j * DH:(j + 1) * DH], pt[(n + m) % NPB][:, j, lo:],
                                            start=(kt == 0 and lo == 0), stop=(d == TPC - 2 + m))
                    ins.then_inc(s_pv, 2)

                def finish(it, u):
                    q = units[u][1]
                    pe.wait_ge(s_raw, it * NU + u + 1)
                    if q:
                        pe.wait_ge(s_add, it * NA + unit_count(u))
                        total = below[fin.index(u) % NSB]
                    else:
                        pe.wait_ge(s_dia, it * ND + vec_count((first_step + [NS])[u + 1] - 1))
                        total = diag[u % NOB]
                    out = ob[u % NOB]
                    pe.matmul(out[0:2 * DH, :], fold[:], raw[u % NOB][:], start=True, stop=True)
                    for j in range(2):
                        ins = pe.matmul(out[(2 + j) * DH:(3 + j) * DH, :], ones[:], total[:, j], start=True, stop=True)
                    ins.then_inc(s_fold, 1)

                pe.wait_ge(s_cst, NCST)
                pe.wait_ge(s_rows, NROW)
                for i in range(start):
                    item(0, i, True)

                def group(it, first, last):
                    done = start

                    def items(upto):
                        nonlocal done
                        for i in range(done, upto):
                            if i < NI:
                                item(it, i, first)
                            elif not last:
                                item(it + 1, i - NI, False)
                        done = max(done, upto)

                    for n in range(NS):
                        here = done
                        share = [here + -(-(upto[n] - here) * f // 6) for f in PARTS[n % 2]]
                        scores(it, n, first, lambda: items(share[0]))
                        items(share[1])
                        if n % 2 and n > 2:
                            values(it, n - 3, first)
                        elif n % 2 and not first:
                            values(it - 1, NS - 2, False)
                        for u, prev in units_at(n, FOLD):
                            if not prev:
                                finish(it, u)
                            elif not first:
                                finish(it - 1, u)
                        items(upto[n])
                    if last:
                        values(it, NS - 2, False)
                        finish(it, NU - 1)

                over_groups(pe, group)


class FfnRaw:

    def __init__(self, raw):
        self.gu, self.d = raw


class FfnWeights:

    def __init__(self, al, name, raw=None):
        if raw is None:
            raw = (al.sb(f"{name}_gu", [P, 2, KD, F]), al.sb(f"{name}_d", [P, NF, D]))
        self.gu, self.d = raw
        self.guh, self.gul = al.sb(f"{name}_guh", [P, 2, KD, F], F32R), al.sb(f"{name}_gul", [P, 2, KD, F], F32R)
        self.dh, self.dl = al.sb(f"{name}_dh", [P, NF, D], F32R), al.sb(f"{name}_dl", [P, NF, D], F32R)

    def down_parts(self):
        w = FS[-1][1]
        return [(self.d[:, 0:NF - 1], self.dh[:, 0:NF - 1], self.dl[:, 0:NF - 1]),
                (self.d[0:w, NF - 1], self.dh[0:w, NF - 1], self.dl[0:w, NF - 1])]


def load_ffn(dma, wt, gate, up, down, sem):
    dma(wt.gu[:, 0], gate.rearrange("(k p) f -> p k f", p=P)).then_inc(sem, 16)
    dma(wt.gu[:, 1], up.rearrange("(k p) f -> p k f", p=P)).then_inc(sem, 16)
    dma(wt.d[:, 0:NF - 1], down[0:(NF - 1) * P].rearrange("(k p) n -> p k n", p=P)).then_inc(sem, 16)
    dma(wt.d[0:FS[-1][1], NF - 1], down[(NF - 1) * P:F]).then_inc(sem, 16)


def gate_up(nc, bank, wt, which, f, xh, xl):
    lo, w = FS[f]
    for k in range(KD):
        ins = mm3(nc, bank[0:w, :], wt.guh[:, which, k, lo:lo + w], wt.gul[:, which, k, lo:lo + w],
                  xh[:, k], xl[:, k], k == 0, k == KD - 1)
    return ins


def down(nc, bank, wt, hh, hl, t, slices=range(NF)):
    for f in slices:
        w = FS[f][1]
        ins = mm3(nc, bank, hh[0:w, f, t * P:(t + 1) * P], hl[0:w, f, t * P:(t + 1) * P],
                  wt.dh[0:w, f], wt.dl[0:w, f], f == 0, f == NF - 1)
    return ins


def phase_shared(nc, x, scratch, ahead):
    with ExitStack() as ctx:
        al = Alloc(nc, ctx)
        ident = al.sb("c_ident", [P, P])
        mhalf = al.sb("c_mhalf", [P, TPC])
        wos, wob, gw = ahead.wos, ahead.wob, ahead.gw
        woh, wol = al.sb("c_woh", [P, KD, D], F32R), al.sb("c_wol", [P, KD, D], F32R)
        gwh, gwl = al.sb("c_gwh", [P, KD, E], F32R), al.sb("c_gwl", [P, KD, E], F32R)
        wt = FfnWeights(al, "c_sw", ahead.raw)
        sums, rsum = al.sb("c_sums", [CPB * H, CH]), al.sb("c_rsum", [CPB * H, CH])
        oin, rin, xin = ahead.oin, ahead.rin, ahead.xin
        on = oin
        oh, ol = al.sb("c_oh", [P, KD, CH], F32R), al.sb("c_ol", [P, KD, CH], F32R)
        xw = rin[:].rearrange("p k n -> p (k n)").rearrange("p (t n) -> p t n", t=TPC)
        x1 = al.sb("c_x1", [P, TPC, D])
        x1k = al.sb("c_x1k", [P, TPC, D])
        xn = al.sb("c_xn", [P, TPC, D])
        st, mv = al.sb("c_stats", [P, TPC, 6]), al.sb("c_mv", [P, TPC, 2])
        vare, rstd = al.sb("c_vare", [P, TPC]), al.sb("c_rstd", [P, TPC])
        xh, xl = al.sb("c_xh", [P, KD, CH], F32R), al.sb("c_xl", [P, KD, CH], F32R)
        sg = al.sb("c_sg", [P, NF, CH])
        hf = al.sb("c_hf", [P, NF, CH])
        hh, hl = al.sb("c_hh", [P, NF, CH], F32R), al.sb("c_hl", [P, NF, CH], F32R)
        acc = al.sb("c_acc", [P, TPC, D])
        lgT = al.sb("c_lgT", [E, CH])
        lg = al.sb("c_lg", [P, TPC, E])
        ab = [al.bank(f"c_ab{n}") for n in range(2)]
        lb = al.bank("c_lb")
        fb = [al.bank(f"c_fb{n}") for n in range(5)]

        s_vpass, s_gpass, s_ppass = al.sem("c_vector_passed"), al.sem("c_pool_passed"), al.sem("c_tensor_passed")
        s_cst = al.sem("c_constants_made")
        s_wh = al.sem("c_weights_high")
        s_wl = al.sem("c_weights_low")
        s_sum = al.sem("c_sums_in")
        s_rs = al.sem("c_reciprocals_made")
        s_rst = al.sem("c_reciprocals_stored")
        s_o = al.sem("c_attention_in")
        s_x = al.sem("c_x_in")
        s_on = al.sem("c_o_normalized")
        s_xw = al.sem("c_xw_made")
        s_oh = al.sem("c_oh_made")
        s_ol = al.sem("c_ol_made")
        s_at = al.sem("c_att_made")
        s_x1 = al.sem("c_x1_made")
        s_x1k = al.sem("c_x1_kept")
        s_stat = al.sem("c_stats_made")
        s_var = al.sem("c_var_made")
        s_vare = al.sem("c_vare_made")
        s_rstd = al.sem("c_rstd_made")
        s_xn = al.sem("c_xn_made")
        s_t = al.sem("c_transposed")
        s_xh = al.sem("c_xh_made")
        s_xl = al.sem("c_xl_made")
        s_lt = al.sem("c_logits_made")
        s_ltc = al.sem("c_logits_copied")
        s_gu = al.sem("c_gate_up_made")
        s_sg = al.sem("c_silu_made")
        s_h = al.sem("c_h_made")
        s_hh = al.sem("c_hh_made")
        s_hl = al.sem("c_hl_made")
        s_dn = al.sem("c_down_made")
        s_acc = al.sem("c_acc_made")
        s_xst = al.sem("c_xn_stored")
        s_ast = al.sem("c_acc_stored")
        s_lst = al.sem("c_logits_stored")

        with nc.Block() as block:
            @block.sync
            def _(sp):
                sp.dma_start(sums[:], batch_rows(scratch, "sums", 1)).then_inc(s_sum, 16)

                def load(c):
                    sp.wait_ge(s_ol, c)
                    load_attention(sp.dma_start, scratch, c, ahead).then_inc(s_o, 16)
                    sp.wait_ge(s_x1, c * TPC)
                    for ins in load_reciprocals(sp.dma_start, scratch, c, ahead):
                        ins.then_inc(s_o, 16)
                    load_rows(sp.dma_start, x, c, ahead).then_inc(s_x, 16)

                def store_rows(c):
                    sp.wait_ge(s_xn, c * TPC + TPC)
                    sp.dma_start(scratch["xn"][bass.ds(c * CH, CH), :].rearrange("(t p) n -> p t n", p=P), xn[:]).then_inc(s_xst, 16)

                def store_acc(c):
                    sp.wait_ge(s_acc, c * TPC + TPC)
                    sp.dma_start(scratch["acc"][bass.ds(c * CH, CH), :].rearrange("(t p) n -> p t n", p=P), acc[:]).then_inc(s_ast, 16)

                def store_logits(c):
                    sp.wait_ge(s_ltc, c * 2 + 2)
                    sp.dma_start(scratch["logits"][:, bass.ds(c * TPC, TPC), :], lg[:]).then_inc(s_lst, 16)

                def step(c, last=False):
                    store_logits(c)
                    if not last:
                        load(c + 2)
                    store_rows(c + 1)
                    store_acc(c)

                load(1)
                sp.wait_ge(s_rs, 1)
                sp.dma_start(batch_rows(scratch, "rsum", 1), rsum[:]).then_inc(s_rst, 16)
                sp.wait_ge(s_rst, 16)
                store_rows(0)
                with sp.Fori(0, NCH - 2) as c:
                    step(c)
                step(NCH - 2, last=True)
                store_logits(NCH - 1)
                store_acc(NCH - 1)
                for sem in (s_xst, s_ast, s_lst):
                    sp.wait_ge(sem, NCH * 16)

            @block.gpsimd
            def _(g):
                make_identity(g, ident, s_cst, 0)
                g.memset(mhalf[:], -0.5).then_inc(s_cst, 1)

                def before_norm(c, first=False):
                    if not first:
                        g.wait_ge(s_o, c * 80)
                    g.tensor_tensor(on[:], oin[:], rin[:], ALU.mult).then_inc(s_on, 1)
                    if not first:
                        g.wait_ge(s_x, c * 16)
                    g.wait_ge(s_on, c + 1)
                    for t in range(TPC):
                        ins = g.tensor_tensor(xw[:, t], xin[:, t], wob[:], ALU.add)
                    ins.then_inc(s_xw, 1)
                    wait_apart(g, s_var, c * TPC + TPC, s_gpass)
                    g.tensor_scalar(vare[:], mv[:, :, 1], EPS, None, ALU.add).then_inc(s_vare, 1)
                    g.wait_ge(s_vare, c + 1)
                    g.tensor_tensor(rstd[:], vare[:], mhalf[:], ALU.pow).then_inc(s_rstd, 1)

                g.wait_ge(s_cst, 3)
                before_norm(0, first=True)
                with g.Fori(1, NCH) as c:
                    before_norm(c)

            @block.scalar
            def _(act):
                act.activation(woh[:], wos[:], ACT.Copy).then_inc(s_wh, 1)
                def o_high(c, first=False):
                    act.wait_ge(s_on, c + 1)
                    if not first:
                        act.wait_ge(s_at, c * TPC)
                    act.activation(oh[:], on[:], ACT.Copy).then_inc(s_oh, 1)

                def hidden(c, f, first=False):
                    w = FS[f][1]
                    act.wait_ge(s_gu, (c * NF + f) * 2 + 2)
                    if not first:
                        act.wait_ge(s_h, (c - 1) * NF + f + 1)
                    act.activation(sg[0:w, f], fb[2 * f % 5][0:w, :], ACT.Silu).then_inc(s_sg, 1)
                    act.wait_ge(s_h, c * NF + f + 1)
                    if not first:
                        act.wait_ge(s_dn, c * TPC)
                    act.activation(hh[0:w, f], hf[0:w, f], ACT.Copy).then_inc(s_hh, 1)

                def x_high(c):
                    for k in range(KD):
                        act.wait_ge(s_t, c * KD + k + 1)
                        act.activation(xh[:, k], ab[k % 2][:], ACT.Copy).then_inc(s_xh, 1)

                def keep(c, first=False):
                    if not first:
                        act.wait_ge(s_acc, c * TPC)
                    act.wait_ge(s_x1, c * TPC + TPC)
                    act.activation(x1k[:], x1[:], ACT.Copy).then_inc(s_x1k, 1)

                o_high(0, first=True)
                act.activation(gwh[:], gw[:], ACT.Copy).then_inc(s_wh, 1)
                act.activation(wt.guh[:], wt.gu[:], ACT.Copy).then_inc(s_wh, 1)
                for raw, hi, lo in wt.down_parts():
                    act.activation(hi, raw, ACT.Copy).then_inc(s_wh, 1)
                x_high(0)
                keep(0, first=True)

                def step(c, first=False, last=False):
                    if not last:
                        o_high(c + 1)
                    for f in range(NF):
                        hidden(c, f, first)
                    if not last:
                        x_high(c + 1)
                        keep(c + 1)

                step(0, first=True)
                with act.Fori(1, NCH - 1) as c:
                    step(c)
                step(NCH - 1, last=True)

            @block.vector
            def _(v):

                def o_low(c, first=False):
                    v.wait_ge(s_oh, c + 1)
                    v.tensor_tensor(ol[:], on[:], f32(oh[:]), ALU.subtract).then_inc(s_ol, 1)

                def residual(c, first=False):
                    v.wait_ge(s_xw, c + 1)
                    if not first:
                        v.wait_ge(s_x1k, c)
                    for t in range(TPC):
                        v.wait_ge(s_at, c * TPC + t + 1)
                        v.tensor_tensor(x1[:, t], ab[t % 2][:], xw[:, t], ALU.add).then_inc(s_x1, 1)
                        v.wait_ge(s_x1, c * TPC + t + 1)
                        v.bn_stats(st[:, t], x1[:, t]).then_inc(s_stat, 1)
                    for t in range(TPC):
                        wait_apart(v, s_stat, c * TPC + t + 1, s_vpass)
                        v.bn_aggr(mv[:, t], st[:, t]).then_inc(s_var, 1)

                def norm(c, first=False):
                    v.wait_ge(s_rstd, c + 1)
                    v.wait_ge(s_var, c * TPC + TPC)
                    if not first:
                        v.wait_ge(s_xst, c * 16)
                        v.wait_ge(s_t, c * KD)
                    for t in range(TPC):
                        v.tensor_scalar(xn[:, t], x1[:, t], mv[:, t, 0:1], rstd[:, t:t + 1], ALU.subtract, ALU.mult).then_inc(s_xn, 1)

                def x_low(c, ks):
                    for k in ks:
                        v.wait_ge(s_xh, c * KD + k + 1)
                        v.tensor_tensor(xl[:, k], ab[k % 2][:], f32(xh[:, k]), ALU.subtract).then_inc(s_xl, 1)

                def expert_rows(c):
                    v.wait_ge(s_lt, c * 2 + 1)
                    v.tensor_copy(lgT[:], lb[0:E, :]).then_inc(s_ltc, 1)

                def token_rows(c, first=False):
                    v.wait_ge(s_lt, c * 2 + 2)
                    if not first:
                        v.wait_ge(s_lst, c * 16)
                    v.tensor_copy(lg[:], lb[:, 0:TPC * E].rearrange("p (t e) -> p t e", t=TPC)).then_inc(s_ltc, 1)

                def hidden(c, f, first=False):
                    w = FS[f][1]
                    v.wait_ge(s_sg, c * NF + f + 1)
                    if not first:
                        v.wait_ge(s_hl, (c - 1) * NF + f + 1)
                    v.tensor_tensor(hf[0:w, f], sg[0:w, f], fb[(2 * f + 1) % 5][0:w, :], ALU.mult).then_inc(s_h, 1)
                    v.wait_ge(s_hh, c * NF + f + 1)
                    v.tensor_tensor(hl[0:w, f], hf[0:w, f], f32(hh[0:w, f]), ALU.subtract).then_inc(s_hl, 1)

                def add_shared(c, ts, first=False):
                    v.wait_ge(s_x1k, c + 1)
                    if not first:
                        v.wait_ge(s_ast, c * 16)
                    for t in ts:
                        v.wait_ge(s_dn, c * TPC + t + 1)
                        v.tensor_tensor(acc[:, t], fb[(2 * NF + t) % 5][:], x1k[:, t], ALU.add).then_inc(s_acc, 1)

                v.wait_ge(s_wh, 1)
                v.tensor_tensor(wol[:], wos[:], f32(woh[:]), ALU.subtract).then_inc(s_wl, 1)
                o_low(0, first=True)
                v.wait_ge(s_wh, 5)
                v.tensor_tensor(gwl[:], gw[:], f32(gwh[:]), ALU.subtract).then_inc(s_wl, 1)
                v.tensor_tensor(wt.gul[:], wt.gu[:], f32(wt.guh[:]), ALU.subtract).then_inc(s_wl, 1)
                for raw, hi, lo in wt.down_parts():
                    v.tensor_tensor(lo, raw, f32(hi), ALU.subtract).then_inc(s_wl, 1)
                residual(0, first=True)
                norm(0, first=True)
                x_low(0, range(KD))
                v.wait_ge(s_sum, 16)
                v.reciprocal(rsum[:], sums[:]).then_inc(s_rs, 1)

                def step(c, first=False, last=False):
                    hidden(c, 0, first)
                    expert_rows(c)
                    if not last:
                        o_low(c + 1)
                    hidden(c, 1, first)
                    token_rows(c, first)
                    if not last:
                        residual(c + 1)
                        norm(c + 1)
                    hidden(c, NF - 1, first)
                    for half in (range(0, 2), range(2, 4)):
                        if not last:
                            x_low(c + 1, half)
                        add_shared(c, half, first)

                step(0, first=True)
                with v.Fori(1, NCH - 1) as c:
                    step(c)
                step(NCH - 1, last=True)

            @block.tensor
            def _(pe):
                NFB = 2 * NF + TPC

                def att(c, first=False):
                    pe.wait_ge(s_ol, c + 1)
                    for t in range(TPC):
                        if t >= 2:
                            pe.wait_ge(s_x1, c * TPC + t - 1)
                        elif not first:
                            pe.wait_ge(s_xl, c * KD - 1 + t)
                        for k in range(KD):
                            ins = mm3(nc, ab[t % 2][:], oh[:, k, t * P:(t + 1) * P], ol[:, k, t * P:(t + 1) * P],
                                      woh[:, k], wol[:, k], k == 0, k == KD - 1)
                        ins.then_inc(s_at, 1)

                def transposes(c, ks):
                    pe.wait_ge(s_xn, c * TPC + TPC)
                    for k in ks:
                        if k >= 2:
                            pe.wait_ge(s_xl, c * KD + k - 1)
                        for t in range(TPC):
                            ins = pe.transpose(ab[k % 2][:, t * P:(t + 1) * P], xn[:, t, k * P:(k + 1) * P], ident[:])
                        ins.then_inc(s_t, 1)

                def logits(c, first=False):
                    if not first:
                        pe.wait_ge(s_ltc, c * 2)
                    for k in range(KD):
                        ins = mm3(nc, lb[0:E, :], gwh[:, k], gwl[:, k], xh[:, k], xl[:, k], k == 0, k == KD - 1)
                    ins.then_inc(s_lt, 1)

                def turn_logits(c):
                    wait_apart(pe, s_ltc, c * 2 + 1, s_ppass)
                    for t in range(TPC):
                        ins = pe.transpose(lb[:, t * E:(t + 1) * E], lgT[:, t * P:(t + 1) * P], ident[0:E, 0:E])
                    ins.then_inc(s_lt, 1)

                def hidden(c, f, first=False):
                    for which in range(2):
                        n = 2 * f + which
                        if n >= 5:
                            pe.wait_ge(s_sg, c * NF + (n - 5) // 2 + 1)
                        elif n and not first:
                            pe.wait_ge(s_acc, (c - 1) * TPC + n)
                        elif not first:
                            pe.wait_ge(s_h, c * NF)
                        gate_up(nc, fb[n % 5][:], wt, which, f, xh, xl).then_inc(s_gu, 1)

                def down_rows(c, ts, slices):
                    pe.wait_ge(s_hl, c * NF + slices[-1] + 1)
                    for t in ts:
                        if t == TPC - 1:
                            pe.wait_ge(s_sg, c * NF + NF)
                        ins = down(nc, fb[(2 * NF + t) % 5][:], wt, hh, hl, t, slices)
                        if slices[-1] == NF - 1:
                            ins.then_inc(s_dn, 1)

                pe.wait_ge(s_cst, 3)
                pe.wait_ge(s_wl, 1)
                att(0, first=True)
                transposes(0, range(KD))
                pe.wait_ge(s_wl, 5)
                pe.wait_ge(s_xl, KD)

                def step(c, first=False, last=False):
                    if not first:
                        pe.wait_ge(s_xl, c * KD + KD)
                    hidden(c, 0, first)
                    logits(c, first)
                    hidden(c, 1, first)
                    turn_logits(c)
                    if not last:
                        att(c + 1)
                    hidden(c, NF - 1, first)
                    down_rows(c, range(TPC), [0, 1])
                    for half in (range(0, 2), range(2, 4)):
                        if not last:
                            transposes(c + 1, half)
                        down_rows(c, half, [NF - 1])

                step(0, first=True)
                with pe.Fori(1, NCH - 1) as c:
                    step(c)
                step(NCH - 1, last=True)


SLOTS = 512
NB = (2 * T + E * (SLOTS - 1)) // SLOTS
TPB = SLOTS // P


def phase_route(nc, keep, w, scratch):
    with ExitStack() as ctx:
        al = Alloc(nc, ctx)
        NC = NB * TPB
        lane = al.sb("d_lane", [P, P])
        column = al.sb("d_column", [P, NC])
        ones = al.sb("d_ones", [P, P])
        before = al.sb("d_before", [P, P])
        rank = al.sb("d_rank", [P, NT, E])
        steps = al.sb("d_steps", [P, E, T // SLOTS])
        blk = al.sb("d_blk", [P, NB, E])
        tok = al.sb("d_tok", [P, NT])
        lg = al.sb("d_lg", [P, NT, E])
        a, b2 = al.sb("d_a", [P, NT, E]), al.sb("d_b", [P, NT, E])
        oh = [al.sb(f"d_oh{n}", [P, NT, E]) for n in range(2)]
        m = [al.sb(f"d_m{n}", [P, NT]) for n in range(2)]
        r = al.sb("d_r", [P, NT])
        both = al.sb("d_both", [P, NT, E])
        tot, cum = al.sb("d_tot", [P, NT, E]), al.sb("d_cum", [P, NT, E])
        cmp1 = al.sb("d_cmp1", [P, E, T // SLOTS])
        cmp2 = al.sb("d_cmp2", [P, NB, E])
        nb, endb, startb = al.sb("d_nb", [P, E]), al.sb("d_endb", [P, E]), al.sb("d_startb", [P, E])
        ebf = al.sb("d_ebf", [P, NB])
        slotf = [al.sb(f"d_slotf{n}", [P, NT]) for n in range(2)]
        ex = al.sb("d_ex", [P, NT])
        den = al.sb("d_den", [P, NT])
        part = al.sb("d_part", [P, NT], U32)
        low, high = ([al.sb(f"d_{x}{n}", [P, NT]) for n in range(2)] for x in ("low", "high"))
        at_lane = [al.sb(f"d_at_lane{n}", [P, NT, P]) for n in range(2)]
        at_col = [al.sb(f"d_at_column{n}", [P, NT, NC]) for n in range(2)]
        pre, tob = al.bank("d_pre"), al.bank("d_totals")
        idb = al.bank("d_idb")

        s_in = al.sem("d_logits_in")
        s_w = al.sem("d_weights_in")
        s_cst = al.sem("d_constants_made")
        s_v = al.sem("d_vector_step")
        s_mm = al.sem("d_counts_made")
        s_ex = al.sem("d_exp_made")
        s_first = al.sem("d_first_numbers_made")
        s_it = al.sem("d_tokens_placed")
        marks = {}

        NCST = 9

        with nc.Block() as block:
            @block.vector
            def _(v):
                done = [0]

                def step(ins, mark=None):
                    done[0] += 1
                    ins.then_inc(s_v, 1)
                    v.wait_ge(s_v, done[0])
                    if mark:
                        marks[mark] = done[0]

                def over(ap, n, axis):
                    return ap.unsqueeze(axis).to_broadcast([P, n, E] if axis == 1 else [P, ap.shape[1], n])

                v.wait_ge(s_cst, NCST)
                v.wait_ge(s_in, 16)
                src = lg
                for n in range(2):
                    step(v.tensor_reduce(m[n][:], src[:], AX.X, ALU.max), "max2" if n else None)
                    step(v.tensor_tensor(a[:], src[:], over(m[n][:], E, 2), ALU.is_equal))
                    step(v.tensor_tensor(b2[:], a[:], rank[:], ALU.mult))
                    step(v.tensor_reduce(r[:], b2[:], AX.X, ALU.max))
                    step(v.tensor_tensor(oh[n][:], b2[:], over(r[:], E, 2), ALU.is_equal))
                    if n == 0:
                        step(v.scalar_tensor_tensor(out=both[:], in0=oh[0][:], scalar=-3e38, in1=lg[:], op0=ALU.mult, op1=ALU.add))
                        src = both
                step(v.tensor_tensor(both[:], oh[0][:], oh[1][:], ALU.add), "both")
                step(v.tensor_tensor(ex[:], m[1][:], m[0][:], ALU.subtract), "gap")
                v.wait_ge(s_mm, 1)
                step(v.tensor_copy(tot[:], tob[:, 0:NT * E].rearrange("p (t e) -> p t e", t=NT)))
                for e in range(E):
                    step(v.tensor_tensor_scan(cum[:, :, e], ones[:, 0:NT], tot[:, :, e], 0.0, ALU.mult, ALU.add))
                step(v.tensor_tensor(cmp1[:], steps[:], over(cum[:, NT - 1, :], T // SLOTS, 2), ALU.is_lt))
                step(v.tensor_reduce(nb[:], cmp1[:], AX.X, ALU.add))
                step(v.tensor_tensor_scan(endb[:], ones[:, 0:E], nb[:], 0.0, ALU.mult, ALU.add))
                step(v.tensor_tensor(startb[:], endb[:], nb[:], ALU.subtract))
                step(v.tensor_scalar(startb[:], startb[:], float(SLOTS), None, ALU.mult))
                step(v.tensor_tensor(cmp2[:], blk[:], over(endb[:], NB, 1), ALU.is_ge))
                step(v.tensor_reduce(ebf[:], cmp2[:], AX.X, ALU.add))
                step(v.tensor_scalar(ebf[:], ebf[:], float(E - 1), None, ALU.min))
                step(v.tensor_copy(keep["expert"][:], ebf[:]), "expert")
                step(v.tensor_tensor(cum[:], cum[:], tot[:], ALU.subtract))
                step(v.tensor_tensor(cum[:], cum[:], over(startb[:], NT, 1), ALU.add))
                step(v.tensor_tensor(cum[:], pre[:, 0:NT * E].rearrange("p (t e) -> p t e", t=NT), cum[:], ALU.add))
                for n in range(2):
                    step(v.tensor_tensor(a[:], cum[:], oh[n][:], ALU.mult))
                    step(v.tensor_reduce(slotf[n][:], a[:], AX.X, ALU.add))
                    step(v.tensor_copy(keep["slot"][n][:], slotf[n][:]), f"slot{n}")
                for n in range(2):
                    for parts, op, by in ((low, ALU.bitwise_and, P - 1), (high, ALU.logical_shift_right, P.bit_length() - 1)):
                        step(v.tensor_scalar(part[:], keep["slot"][n][:], by, None, op))
                        step(v.tensor_copy(parts[n][:], part[:]))
                for n in range(2):
                    wide = [P, NT, NC]
                    step(v.tensor_tensor(at_col[n][:], column[:].unsqueeze(1).to_broadcast(wide),
                                         high[n][:].unsqueeze(2).to_broadcast(wide), ALU.is_equal), f"column{n}")
                    if n:
                        step(v.tensor_tensor(at_col[n][:], at_col[n][:], tok[:].unsqueeze(2).to_broadcast(wide), ALU.mult))
                    step(v.tensor_tensor(at_lane[n][:], lane[:].unsqueeze(1).to_broadcast([P, NT, P]),
                                         low[n][:].unsqueeze(2).to_broadcast([P, NT, P]), ALU.is_equal), f"placed{n}")
                v.wait_ge(s_ex, 1)
                step(v.tensor_scalar(den[:], ex[:], 1.0, None, ALU.add))
                step(v.reciprocal(keep["weight"][0][:], den[:]))
                step(v.tensor_tensor(keep["weight"][1][:], ex[:], keep["weight"][0][:], ALU.mult))
                v.wait_ge(s_it, 1)
                v.tensor_copy(keep["token"][:], idb[:, 0:NB * TPB])

            @block.sync
            def _(sp):
                sp.dma_start(lg[:], scratch["logits"]).then_inc(s_in, 16)
                sp.wait_ge(s_v, marks["expert"])
                for b in range(2):
                    fetch_expert(nc, sp, keep, w, b, FfnRaw(keep["raw"][b]), s_w)
                sp.wait_ge(s_w, 2 * 64)

            @block.gpsimd
            def _(g):
                with nc.allow_low_precision(reason="integers below 2^24"):
                    g.memset(ones[:], 1.0).then_inc(s_cst, 1)
                    g.memset(before[:], 1.0).then_inc(s_cst, 1)
                    g.wait_ge(s_cst, 2)
                    g.affine_select(out=before[:], in_=before[:], compare_op=ALU.is_gt, fill=0.0, base=0,
                                    pattern=[[1, P]], channel_multiplier=-1).then_inc(s_cst, 1)
                    kw = dict(allow_small_or_imprecise_dtypes=True)
                    g.iota(rank[:], [[0, NT], [-1, E]], base=E, channel_multiplier=0, **kw).then_inc(s_cst, 1)
                    g.iota(steps[:], [[0, E], [SLOTS, T // SLOTS]], base=0, channel_multiplier=0, **kw).then_inc(s_cst, 1)
                    g.iota(blk[:], [[1, NB], [0, E]], base=0, channel_multiplier=0, **kw).then_inc(s_cst, 1)
                    g.iota(tok[:], [[P, NT]], base=0, channel_multiplier=1, **kw).then_inc(s_cst, 1)
                    g.iota(lane[:], [[1, P]], base=0, channel_multiplier=0, **kw).then_inc(s_cst, 1)
                    g.iota(column[:], [[1, NC]], base=0, channel_multiplier=0, **kw).then_inc(s_cst, 1)
                g.wait_ge(s_cst, NCST)
                g.wait_ge(s_v, marks["column0"])
                g.tensor_tensor(at_col[0][:], at_col[0][:], tok[:].unsqueeze(2).to_broadcast([P, NT, NC]), ALU.mult).then_inc(s_first, 1)

            @block.scalar
            def _(act):
                act.wait_ge(s_v, marks["gap"])
                act.activation(ex[:], ex[:], ACT.Exp).then_inc(s_ex, 1)

            @block.tensor
            def _(pe):
                pe.wait_ge(s_cst, NCST)
                pe.wait_ge(s_v, marks["both"])
                rows = both[:].rearrange("p t e -> p (t e)")
                pe.matmul(pre[:, 0:NT * E], before[:], rows, start=True, stop=True)
                pe.matmul(tob[:, 0:NT * E], ones[:], rows, start=True, stop=True).then_inc(s_mm, 1)
                for n in range(2):
                    pe.wait_ge(s_v, marks[f"placed{n}"])
                    if n == 0:
                        pe.wait_ge(s_first, 1)
                    for t in range(NT):
                        ins = pe.matmul(idb[:, 0:NC], at_lane[n][:, t], at_col[n][:, t],
                                        start=(n == 0 and t == 0), stop=(n == 1 and t == NT - 1))
                ins.then_inc(s_it, 1)


def fetch_expert(nc, sp, keep, w, b, raw, sem):
    e = sp.value_load(keep["expert"][0:1, bass.ds(b, 1)], min_val=0, max_val=E - 1)
    load_ffn(sp.dma_start, raw, w["w_gate"][bass.ds(e, 1)].rearrange("e d f -> (e d) f"),
             w["w_up"][bass.ds(e, 1)].rearrange("e d f -> (e d) f"),
             w["w_down"][bass.ds(e, 1)].rearrange("e f d -> (e f) d"), sem)


def phase_experts(nc, keep, w, scratch):
    with ExitStack() as ctx:
        al = Alloc(nc, ctx)
        ident = al.sb("e_ident", [P, P])
        wt = [FfnWeights(al, f"e_w{n}", keep["raw"][n]) for n in range(2)]
        xg = [al.sb(f"e_xg{n}", [P, TPB, D]) for n in range(2)]
        idx = [al.sb(f"e_idx{n}", [P, TPB], U32) for n in range(2)]
        xh = [al.sb(f"e_xh{n}", [P, KD, SLOTS], F32R) for n in range(2)]
        xl = [al.sb(f"e_xl{n}", [P, KD, SLOTS], F32R) for n in range(2)]
        sg, hf = al.sb("e_sg", [P, NF, SLOTS]), al.sb("e_hf", [P, NF, SLOTS])
        hh, hl = al.sb("e_hh", [P, NF, SLOTS], F32R), al.sb("e_hl", [P, NF, SLOTS], F32R)
        y = al.sb("e_y", [P, TPB, D])
        tbk = [al.bank(f"e_tb{n}") for n in range(2)]
        fb = [al.bank(f"e_fb{n}") for n in range(2 * NF)]

        WP = 4

        def parts(n):
            return [(wt[n].gu[:, j], wt[n].guh[:, j], wt[n].gul[:, j]) for j in range(2)] + wt[n].down_parts()

        s_cst = al.sem("e_constants_made")
        s_gpass = al.sem("e_pool_passed")
        s_w = [al.sem(f"e_weights_in{n}") for n in range(2)]
        s_x = [al.sem(f"e_rows_in{n}") for n in range(2)]
        s_wh, s_wl = al.sem("e_weights_high"), al.sem("e_weights_low")
        s_idx = al.sem("e_tokens_copied")
        s_t = al.sem("e_transposed")
        s_xh, s_xl = al.sem("e_xh_made"), al.sem("e_xl_made")
        s_gu, s_sg, s_h = al.sem("e_gate_up_made"), al.sem("e_silu_made"), al.sem("e_h_made")
        s_hh, s_hl = al.sem("e_hh_made"), al.sem("e_hl_made")
        s_dn, s_y, s_yst = al.sem("e_down_made"), al.sem("e_y_made"), al.sem("e_y_stored")

        def in_pairs(eng, step):
            step(0, 0, True, False)
            step(1, 1, False, False)
            with eng.Fori(1, (NB - 1) // 2) as i:
                step(i * 2, 0, False, False)
                step(i * 2 + 1, 1, False, False)
            step(NB - 1, 0, False, True)

        assert NB % 2 == 1

        def turns(b, n):
            return b // 2 + 1 if isinstance(b, int) else (b - n) // 2 + 1

        with nc.Block() as block:
            @block.sync
            def _(sp):
                def fetch(b, n):
                    sp.wait_ge(s_wl, (b - 1) * WP)
                    fetch_expert(nc, sp, keep, w, b, wt[n], s_w[n])

                def store(b):
                    sp.wait_ge(s_y, b * TPB + TPB)
                    sp.dma_start(scratch["y"][bass.ds(b * SLOTS, SLOTS), :].rearrange("(t p) n -> p t n", p=P), y[:]).then_inc(s_yst, 16)

                fetch(2, 0)
                store(0)
                with sp.Fori(1, (NB - 1) // 2) as i:
                    fetch(i * 2 + 1, 1)
                    store(i * 2 - 1)
                    fetch(i * 2 + 2, 0)
                    store(i * 2)
                store(NB - 2)
                store(NB - 1)
                sp.wait_ge(s_yst, NB * 16)

            @block.gpsimd
            def _(g):
                make_identity(g, ident, s_cst, 0)

                def gather(b, n, first=False, last=False):
                    if not (isinstance(b, int) and b < 2):
                        g.wait_ge(s_t, (b - 1) * KD)
                    g.tensor_copy(idx[n][:], keep["token"][:, bass.ds(b * TPB, TPB)]).then_inc(s_idx, 1)
                    wait_apart(g, s_idx, b + 1, s_gpass)
                    for t in range(TPB):
                        g.indirect_dma_start(out=xg[n][:, t, :], in_=scratch["xn"], out_offset=None,
                                             in_offset=bass.IndirectOffsetOnAxis(ap=idx[n][:, t:t + 1], axis=0)).then_inc(s_x[n], 16)

                in_pairs(g, gather)

            @block.scalar
            def _(act):
                def split(b, n, some, first=False):
                    if not (isinstance(b, int) and b < 2):
                        act.wait_ge(s_w[n], (turns(b, n) - 1) * 64)
                    if not first:
                        act.wait_ge(s_dn, (b - 1) * TPB)
                    for raw, hi, lo in parts(n)[some]:
                        act.activation(hi, raw, ACT.Copy).then_inc(s_wh, 1)

                def x_high(b, n, ks):
                    for k in ks:
                        act.wait_ge(s_t, b * KD + k + 1)
                        act.activation(xh[n][:, k], tbk[k % 2][:], ACT.Copy).then_inc(s_xh, 1)

                def hidden(b, f, first):
                    width = FS[f][1]
                    act.wait_ge(s_gu, (b * NF + f) * 2 + 2)
                    if not first:
                        act.wait_ge(s_h, (b - 1) * NF + f + 1)
                    act.activation(sg[0:width, f], fb[2 * f][0:width, :], ACT.Silu).then_inc(s_sg, 1)
                    act.wait_ge(s_h, b * NF + f + 1)
                    if not first:
                        act.wait_ge(s_dn, b * TPB)
                    act.activation(hh[0:width, f], hf[0:width, f], ACT.Copy).then_inc(s_hh, 1)

                def step(b, n, first, last):
                    for f in range(NF):
                        hidden(b, f, first)
                        if not last:
                            if f:
                                x_high(b + 1, 1 - n, range(2 * f - 2, 2 * f))
                            split(b + 1, 1 - n, slice(f, f + 1 if f < 2 else WP), first)

                split(0, 0, slice(0, WP), True)
                x_high(0, 0, range(KD))
                in_pairs(act, step)

            @block.vector
            def _(v):
                def split(b, n, some):
                    for j, (raw, hi, lo) in list(enumerate(parts(n)))[some]:
                        v.wait_ge(s_wh, b * WP + j + 1)
                        v.tensor_tensor(lo, raw, f32(hi), ALU.subtract).then_inc(s_wl, 1)

                def x_low(b, n, ks):
                    for k in ks:
                        v.wait_ge(s_xh, b * KD + k + 1)
                        v.tensor_tensor(xl[n][:, k], tbk[k % 2][:], f32(xh[n][:, k]), ALU.subtract).then_inc(s_xl, 1)

                def hidden(b, f):
                    width = FS[f][1]
                    v.wait_ge(s_sg, b * NF + f + 1)
                    v.tensor_tensor(hf[0:width, f], sg[0:width, f], fb[2 * f + 1][0:width, :], ALU.mult).then_inc(s_h, 1)
                    v.wait_ge(s_hh, b * NF + f + 1)
                    v.tensor_tensor(hl[0:width, f], hf[0:width, f], f32(hh[0:width, f]), ALU.subtract).then_inc(s_hl, 1)

                def step(b, n, first, last):
                    for f in range(NF):
                        hidden(b, f)
                        if not last:
                            if f:
                                x_low(b + 1, 1 - n, range(2 * f - 2, 2 * f))
                            split(b + 1, 1 - n, slice(f, f + 1 if f < 2 else WP))
                    if not first:
                        v.wait_ge(s_yst, b * 16)
                    for t in range(TPB):
                        v.wait_ge(s_dn, b * TPB + t + 1)
                        v.tensor_copy(y[:, t], fb[t][:]).then_inc(s_y, 1)

                split(0, 0, slice(0, WP))
                x_low(0, 0, range(KD))
                in_pairs(v, step)

            @block.tensor
            def _(pe):
                def transposes(b, n, ks, first=False):
                    pe.wait_ge(s_x[n], turns(b, n) * TPB * 16)
                    for k in ks:
                        if k >= 2 or not first:
                            pe.wait_ge(s_xl, b * KD - 1 + k)
                        for t in range(TPB):
                            ins = pe.transpose(tbk[k % 2][:, t * P:(t + 1) * P], xg[n][:, t, k * P:(k + 1) * P], ident[:])
                        ins.then_inc(s_t, 1)

                def step(b, n, first, last):
                    pe.wait_ge(s_wl, b * WP + WP)
                    pe.wait_ge(s_xl, b * KD + KD)
                    for f in range(NF):
                        for which in range(2):
                            j = 2 * f + which
                            if j < TPB and not first:
                                pe.wait_ge(s_y, (b - 1) * TPB + j + 1)
                            gate_up(nc, fb[j][:], wt[n], which, f, xh[n], xl[n]).then_inc(s_gu, 1)
                        if f and not last:
                            transposes(b + 1, 1 - n, range(2 * f - 2, 2 * f))
                    pe.wait_ge(s_hl, b * NF + NF - 1)
                    for t in range(TPB):
                        down(nc, fb[t][:], wt[n], hh, hl, t, range(NF - 1))
                    pe.wait_ge(s_hl, b * NF + NF)
                    for t in range(TPB):
                        down(nc, fb[t][:], wt[n], hh, hl, t, [NF - 1]).then_inc(s_dn, 1)

                pe.wait_ge(s_cst, 2)
                transposes(0, 0, range(KD), True)
                in_pairs(pe, step)


def phase_combine(nc, keep, scratch, out):
    RING = 4
    with ExitStack() as ctx:
        al = Alloc(nc, ctx)
        y = [[al.sb(f"f_y{k}_{n}", [P, D]) for n in range(RING)] for k in range(2)]
        acc = [al.sb(f"f_acc{n}", [P, D]) for n in range(RING)]
        mid = al.sb("f_mid", [P, D])
        res = [al.sb(f"f_res{n}", [P, D]) for n in range(RING)]
        s_y = [al.sem(f"f_rows_in{n}") for n in range(RING)]
        s_a = [al.sem(f"f_acc_in{n}") for n in range(RING)]
        s_o = [al.sem(f"f_out_stored{n}") for n in range(RING)]
        s_m, s_r = al.sem("f_first_added"), al.sem("f_second_added")

        with nc.Block() as block:
            @block.gpsimd
            def _(g):
                for t in range(NT):
                    n = t % RING
                    if t >= RING:
                        g.wait_ge(s_r, t - RING + 1)
                    for k in range(2):
                        g.indirect_dma_start(out=y[k][n][:], in_=scratch["y"], out_offset=None,
                                             in_offset=bass.IndirectOffsetOnAxis(ap=keep["slot"][k][:, t:t + 1], axis=0)).then_inc(s_y[n], 16)

            @block.sync
            def _(sp):
                for t in range(NT):
                    n = t % RING
                    if t >= RING:
                        sp.wait_ge(s_r, t - RING + 1)
                    sp.dma_start(acc[n][:], scratch["acc"][t * P:(t + 1) * P, :]).then_inc(s_a[n], 16)

            @block.scalar
            def _(act):
                for t in range(NT):
                    act.wait_ge(s_r, t + 1)
                    act.dma_start(out[t * P:(t + 1) * P, :], res[t % RING][:]).then_inc(s_o[t % RING], 16)
                for n in range(RING):
                    act.wait_ge(s_o[n], 16 * NT // RING)

            @block.vector
            def _(v):
                for t in range(NT):
                    n = t % RING
                    v.wait_ge(s_y[n], (t // RING + 1) * 32)
                    v.wait_ge(s_a[n], (t // RING + 1) * 16)
                    if t:
                        v.wait_ge(s_r, t)
                    v.scalar_tensor_tensor(out=mid[:], in0=y[0][n][:], scalar=keep["weight"][0][:, t:t + 1], in1=acc[n][:],
                                           op0=ALU.mult, op1=ALU.add).then_inc(s_m, 1)
                    v.wait_ge(s_m, t + 1)
                    if t >= RING:
                        v.wait_ge(s_o[n], t // RING * 16)
                    v.scalar_tensor_tensor(out=res[n][:], in0=y[1][n][:], scalar=keep["weight"][1][:, t:t + 1], in1=mid[:],
                                           op0=ALU.mult, op1=ALU.add).then_inc(s_r, 1)


INS = ['L0_attn_x', 'L0_attn_wq_w', 'L0_attn_wq_b', 'L0_attn_wk_w', 'L0_attn_wk_b', 'L0_attn_wkl_w', 'L0_attn_wkl_b',
       'L0_attn_wv_w', 'L0_attn_wv_b', 'L0_attn_wvl_w', 'L0_attn_wvl_b', 'L0_attn_upk_w', 'L0_attn_upk_b',
       'L0_attn_upv_w', 'L0_attn_upv_b', 'L0_attn_wo_w', 'L0_attn_wo_b', 'L0_ffn_gate_w', 'L0_ffn_w_gate',
       'L0_ffn_w_up', 'L0_ffn_w_down', 'L0_ffn_sw_gate', 'L0_ffn_sw_up', 'L0_ffn_sw_down']


def program(nc, ins, out):
    w = {n.split("_", 2)[2]: ap for n, ap in ins.items()}
    x = ins['L0_attn_x'].rearrange("b s d -> (b s) d")

    def dram(name, shape, dt=F32):
        return nc.dram_tensor(name, shape, dt, kind="Internal").ap()

    scratch = {
        "qh": dram("scr_qh", (NCH, D, CH)), "ql": dram("scr_ql", (NCH, D, CH)),
        "kh": dram("scr_kh", (NCH, D, CH)), "kl": dram("scr_kl", (NCH, D, CH)),
        "v": dram("scr_v", (NCH, CH, D)),
        "oT": dram("scr_oT", (NCH, D, CH)), "sums": dram("scr_sums", (NCH, H, CH)),
        "rsum": dram("scr_rsum", (NCH, H, CH)), "xn": dram("scr_xn", (T, D)), "acc": dram("scr_acc", (T, D)),
        "logits": dram("scr_logits", (P, NT, E)),
        "y": dram("scr_y", (NB * SLOTS, D)),
    }
    phase_project(nc, x, w, scratch)
    with ExitStack() as ctx:
        ahead = Ahead(Alloc(nc, ctx))
        phase_attention(nc, x, w, scratch, ahead)
        phase_shared(nc, x, scratch, ahead)
    with ExitStack() as ctx:
        al = Alloc(nc, ctx)
        keep = {
            "slot": [al.sb(f"slot{n}", [P, NT], U32) for n in range(2)],
            "weight": [al.sb(f"weight{n}", [P, NT]) for n in range(2)],
            "expert": al.sb("expert", [P, NB], I32),
            "token": al.sb("token", [P, NB * TPB], U32),
            "raw": [(al.sb(f"e_gu{n}", [P, 2, KD, F]), al.sb(f"e_d{n}", [P, NF, D])) for n in range(2)],
        }
        phase_route(nc, keep, w, scratch)
        phase_experts(nc, keep, w, scratch)
        phase_combine(nc, keep, scratch, out.rearrange("b s d -> (b s) d"))


_OUTS = [((BATCH, SEQ, D), 'float32')]


def kernel(**inputs):
    import numpy as _np
    import concourse.bacc as _bacc
    from concourse import mybir as _mybir
    from concourse.bass_utils import run_bass_kernel_spmd as _run

    nc = _bacc.Bacc("TRN2", target_bir_lowering=False, num_devices=1)
    arrays, ins = {}, {}
    for name in INS:
        a = _np.ascontiguousarray(inputs[name])
        arrays[f"in_{name}_dram"] = a
        ins[name] = nc.dram_tensor(f"in_{name}_dram", a.shape, _mybir.dt.from_np(a.dtype), kind="ExternalInput").ap()
    shape, dtype = _OUTS[0]
    out = nc.dram_tensor("out_0_dram", shape, _mybir.dt.from_np(_np.dtype(dtype)), kind="ExternalOutput").ap()
    program(nc, ins, out)
    r = _run(nc, [arrays], core_ids=[0])
    return r.results[0]["out_0_dram"]
```
